# Optimizing a Trainium2 kernel written in Bass

```python
import numpy as np
import jax
import jax.numpy as jnp

def _softmax(x, axis=-1):
    return jax.nn.softmax(x, axis=axis)

def _gelu(x):
    return jax.nn.gelu(x, approximate=True)

def _silu(x):
    return jax.nn.silu(x)

def _sigmoid(x):
    return jax.nn.sigmoid(x)

def _layernorm(x, axis=-1, eps=1e-05):
    m = jnp.mean(x, axis=axis, keepdims=True)
    v = jnp.var(x, axis=axis, keepdims=True)
    return (x - m) / jnp.sqrt(v + eps)

def _scatter_add(tgt, idx, src, axis=0):
    return tgt.at[idx].add(src)

def _segment_sum(src, seg, n):
    return jax.ops.segment_sum(src, seg, n)
kernel_name = 'mk_xattn_ffn_d1_seqx_r4_c5d6ed'

def setup_inputs(seed: int=0):
    np.random.seed(seed)
    _w = jnp.asarray

    def _rec_inputs():
        import jax
        import jax.numpy as jnp
        _rk = jax.random.key(seed)
        x = -0.0002928 + 1 * jax.random.normal(jax.random.fold_in(_rk, 1), (4, 512, 256), jnp.float32)
        _lenS = 512 - jax.random.randint(jax.random.fold_in(_rk, 7), (4,), 0, max(1, 512 // 4) + 1, jnp.int32)
        _lenS2 = 512 - jax.random.randint(jax.random.fold_in(_rk, 8), (4,), 0, max(1, 512 // 4) + 1, jnp.int32)
        _ctx_1024P = jax.random.normal(jax.random.fold_in(_rk, 11), (4, 16, 256), jnp.float32)
        _ctx_1024c = jax.random.dirichlet(jax.random.fold_in(_rk, 511), 0.3 * jnp.ones((16,), jnp.float32), (4, 512))
        _ctx_1024t = jnp.einsum('bsk,bkd->bsd', _ctx_1024c, _ctx_1024P)
        _ctx_1024t = _ctx_1024t * jax.lax.rsqrt(jnp.mean(jnp.square(_ctx_1024t)) + 1e-12) * 0.953939
        ctx_1024 = -1.39393e-06 + 0.999914 * (_ctx_1024t + 0.3 * jax.random.normal(jax.random.fold_in(_rk, 611), (4, 512, 256), jnp.float32))
        return (x, ctx_1024)
    x, ctx_1024 = _rec_inputs()

    def _L0_xattn_setup():
        import jax, jax.numpy as jnp
        import numpy as np
        EMBED_DIM = 256
        NUM_HEADS = 16
        HEAD_DIM = EMBED_DIM // NUM_HEADS
        key = jax.random.key(seed)
        ks = jax.random.split(key, 11)
        B, S, D = (2, 512, EMBED_DIM)
        scale = 1.0 / np.sqrt(D)
        inp = {'query': jax.random.normal(ks[0], (B, S, D), dtype=jnp.float32), 'key': jax.random.normal(ks[1], (B, S, D), dtype=jnp.float32), 'value': jax.random.normal(ks[2], (B, S, D), dtype=jnp.float32), 'wq': jax.random.normal(ks[3], (D, D), dtype=jnp.float32) * scale, 'bq': jnp.zeros((D,), dtype=jnp.float32), 'wk': jax.random.normal(ks[4], (D, D), dtype=jnp.float32) * scale, 'bk': jnp.zeros((D,), dtype=jnp.float32), 'wv': jax.random.normal(ks[5], (D, D), dtype=jnp.float32) * scale, 'bv': jnp.zeros((D,), dtype=jnp.float32), 'wo': jax.random.normal(ks[6], (D, D), dtype=jnp.float32) * scale, 'bo': jnp.zeros((D,), dtype=jnp.float32)}
        return inp
    _L0_xattn_all = _L0_xattn_setup()
    _L0_xattn_in = {k: v for k, v in _L0_xattn_all.items() if k in ('wq', 'bq', 'wk', 'bk', 'wv', 'bv', 'wo', 'bo')}
    del _L0_xattn_all

    def _L0_ffn_setup():
        import jax, jax.numpy as jnp
        import numpy as np
        B, S, D = (2, 256, 256)
        H, HD = (16, 64)
        E_R = 31
        K_ACT = 3
        INTER = 256
        EPS = 1e-05
        BASE = 10000.0

        def _rmsnorm(x, gamma):
            rms = jnp.sqrt(jnp.mean(x * x, axis=-1, keepdims=True) + EPS)
            return x / rms * gamma

        def _rope(x, theta):
            seq = x.shape[2]
            angles = jnp.arange(seq, dtype=theta.dtype)[:, None] * theta
            cos = jnp.cos(angles)[None, None]
            sin = jnp.sin(angles)[None, None]
            x1, x2 = (x[..., 0::2], x[..., 1::2])
            return jnp.concatenate([x1 * cos - x2 * sin, x1 * sin + x2 * cos], axis=-1)

        def _forward(x, theta, gamma1, gamma2, q_w, q_b, k_w, k_b, v_w, v_b, o_w, o_b, router_w, router_b, sh_w1, sh_b1, sh_w2, sh_b2, re_w1, re_b1, re_w2, re_b2):
            b, s, d = x.shape
            xn = _rmsnorm(x, gamma1)
            q = (xn @ q_w + q_b).reshape(b, s, H, HD).transpose(0, 2, 1, 3)
            k = (xn @ k_w + k_b).reshape(b, s, H, HD).transpose(0, 2, 1, 3)
            v = (xn @ v_w + v_b).reshape(b, s, H, HD).transpose(0, 2, 1, 3)
            q = _rope(q, theta)
            k = _rope(k, theta)
            scale = 1.0 / np.sqrt(HD)
            scores = jnp.einsum('bhqd,bhkd->bhqk', q, k) * scale
            causal = jnp.tril(jnp.ones((s, s), dtype=bool))
            scores = jnp.where(causal, scores, -jnp.inf)
            attn = jax.nn.softmax(scores, axis=-1)
            ctx = jnp.einsum('bhqk,bhkd->bhqd', attn, v)
            ctx = ctx.transpose(0, 2, 1, 3).reshape(b, s, H * HD)
            attn_out = ctx @ o_w + o_b + xn
            an = _rmsnorm(attn_out, gamma2)
            shared = jax.nn.gelu(an @ sh_w1 + sh_b1, approximate=False) @ sh_w2 + sh_b2
            logits = an @ router_w + router_b
            aff = jax.nn.softmax(logits, axis=-1)
            topv, topi = jax.lax.top_k(aff, K_ACT)
            gates = jnp.sum(jax.nn.one_hot(topi, E_R, dtype=aff.dtype) * topv[..., None], axis=-2)
            h = jax.nn.gelu(jnp.einsum('bsd,edh->besh', an, re_w1) + re_b1[None, :, None, :], approximate=False)
            routed = jnp.einsum('bse,besh,ehd->bsd', gates, h, re_w2) + jnp.einsum('bse,ed->bsd', gates, re_b2)
            return shared + routed + an + attn_out
        key = jax.random.key(seed)
        ks = jax.random.split(key, 24)
        s = 0.02
        theta = BASE ** (-jnp.arange(HD // 2, dtype=jnp.float32) * 2.0 / HD)
        inp = {'x': jax.random.normal(ks[0], (B, S, D), jnp.float32), 'positions': jnp.arange(S, dtype=jnp.int32), 'theta': theta, 'gamma1': jnp.ones((D,), jnp.float32), 'gamma2': jnp.ones((D,), jnp.float32), 'q_w': jax.random.normal(ks[1], (D, H * HD), jnp.float32) * s, 'q_b': jnp.zeros((H * HD,), jnp.float32), 'k_w': jax.random.normal(ks[2], (D, H * HD), jnp.float32) * s, 'k_b': jnp.zeros((H * HD,), jnp.float32), 'v_w': jax.random.normal(ks[3], (D, H * HD), jnp.float32) * s, 'v_b': jnp.zeros((H * HD,), jnp.float32), 'o_w': jax.random.normal(ks[4], (H * HD, D), jnp.float32) * s, 'o_b': jnp.zeros((D,), jnp.float32), 'router_w': jax.random.normal(ks[5], (D, E_R), jnp.float32) * s, 'router_b': jnp.zeros((E_R,), jnp.float32), 'sh_w1': jax.random.normal(ks[6], (D, INTER), jnp.float32) * s, 'sh_b1': jnp.zeros((INTER,), jnp.float32), 'sh_w2': jax.random.normal(ks[7], (INTER, D), jnp.float32) * s, 'sh_b2': jnp.zeros((D,), jnp.float32), 're_w1': jax.random.normal(ks[8], (E_R, D, INTER), jnp.float32) * s, 're_b1': jnp.zeros((E_R, INTER), jnp.float32), 're_w2': jax.random.normal(ks[9], (E_R, INTER, D), jnp.float32) * s, 're_b2': jnp.zeros((E_R, D), jnp.float32)}
        return inp
    _L0_ffn_all = _L0_ffn_setup()
    _L0_ffn_in = {k: v for k, v in _L0_ffn_all.items() if k in ('positions', 'theta', 'gamma1', 'gamma2', 'q_w', 'q_b', 'k_w', 'k_b', 'v_w', 'v_b', 'o_w', 'o_b', 'router_w', 'router_b', 'sh_w1', 'sh_b1', 'sh_w2', 'sh_b2', 're_w1', 're_b1', 're_w2', 're_b2')}
    del _L0_ffn_all
    return {'x': x, 'ctx_1024': ctx_1024, 'L0_xattn_wq': _L0_xattn_in['wq'], 'L0_xattn_bq': _L0_xattn_in['bq'], 'L0_xattn_wk': _L0_xattn_in['wk'], 'L0_xattn_bk': _L0_xattn_in['bk'], 'L0_xattn_wv': _L0_xattn_in['wv'], 'L0_xattn_bv': _L0_xattn_in['bv'], 'L0_xattn_wo': _L0_xattn_in['wo'], 'L0_xattn_bo': _L0_xattn_in['bo'], 'L0_ffn_positions': _L0_ffn_in['positions'], 'L0_ffn_theta': _L0_ffn_in['theta'], 'L0_ffn_gamma1': _L0_ffn_in['gamma1'], 'L0_ffn_gamma2': _L0_ffn_in['gamma2'], 'L0_ffn_q_w': _L0_ffn_in['q_w'], 'L0_ffn_q_b': _L0_ffn_in['q_b'], 'L0_ffn_k_w': _L0_ffn_in['k_w'], 'L0_ffn_k_b': _L0_ffn_in['k_b'], 'L0_ffn_v_w': _L0_ffn_in['v_w'], 'L0_ffn_v_b': _L0_ffn_in['v_b'], 'L0_ffn_o_w': _L0_ffn_in['o_w'], 'L0_ffn_o_b': _L0_ffn_in['o_b'], 'L0_ffn_router_w': _L0_ffn_in['router_w'], 'L0_ffn_router_b': _L0_ffn_in['router_b'], 'L0_ffn_sh_w1': _L0_ffn_in['sh_w1'], 'L0_ffn_sh_b1': _L0_ffn_in['sh_b1'], 'L0_ffn_sh_w2': _L0_ffn_in['sh_w2'], 'L0_ffn_sh_b2': _L0_ffn_in['sh_b2'], 'L0_ffn_re_w1': _L0_ffn_in['re_w1'], 'L0_ffn_re_b1': _L0_ffn_in['re_b1'], 'L0_ffn_re_w2': _L0_ffn_in['re_w2'], 'L0_ffn_re_b2': _L0_ffn_in['re_b2']}

def reference(x, ctx_1024, L0_xattn_wq, L0_xattn_bq, L0_xattn_wk, L0_xattn_bk, L0_xattn_wv, L0_xattn_bv, L0_xattn_wo, L0_xattn_bo, L0_ffn_positions, L0_ffn_theta, L0_ffn_gamma1, L0_ffn_gamma2, L0_ffn_q_w, L0_ffn_q_b, L0_ffn_k_w, L0_ffn_k_b, L0_ffn_v_w, L0_ffn_v_b, L0_ffn_o_w, L0_ffn_o_b, L0_ffn_router_w, L0_ffn_router_b, L0_ffn_sh_w1, L0_ffn_sh_b1, L0_ffn_sh_w2, L0_ffn_sh_b2, L0_ffn_re_w1, L0_ffn_re_b1, L0_ffn_re_w2, L0_ffn_re_b2):
    import jax
    import jax.numpy as jnp

    def _L0_xattn_ref(query, key, value, wq, bq, wk, bk, wv, bv, wo, bo):
        import jax, jax.numpy as jnp
        import numpy as np
        EMBED_DIM = 256
        NUM_HEADS = 16
        HEAD_DIM = EMBED_DIM // NUM_HEADS
        B, S, D = query.shape
        H, Dh = (NUM_HEADS, HEAD_DIM)
        q = query @ wq + bq
        k = key @ wk + bk
        v = value @ wv + bv
        q = q.reshape(B, S, H, Dh).transpose(0, 2, 1, 3)
        k = k.reshape(B, S, H, Dh).transpose(0, 2, 1, 3)
        v = v.reshape(B, S, H, Dh).transpose(0, 2, 1, 3)
        scores = jnp.einsum('bhqd,bhkd->bhqk', q, k) / jnp.sqrt(jnp.float32(Dh))
        causal = jnp.tril(jnp.ones((S, S), dtype=bool))
        scores = jnp.where(causal, scores, -jnp.inf)
        attn = jax.nn.softmax(scores, axis=-1)
        out = jnp.einsum('bhqk,bhkd->bhqd', attn, v)
        out = out.transpose(0, 2, 1, 3).reshape(B, S, D)
        return out @ wo + bo

    def _L0_ffn_ref(x, positions, theta, gamma1, gamma2, q_w, q_b, k_w, k_b, v_w, v_b, o_w, o_b, router_w, router_b, sh_w1, sh_b1, sh_w2, sh_b2, re_w1, re_b1, re_w2, re_b2):
        import jax, jax.numpy as jnp
        import numpy as np
        B, S, D = (2, 256, 256)
        H, HD = (16, 64)
        E_R = 31
        K_ACT = 3
        INTER = 256
        EPS = 1e-05
        BASE = 10000.0

        def _rmsnorm(x, gamma):
            rms = jnp.sqrt(jnp.mean(x * x, axis=-1, keepdims=True) + EPS)
            return x / rms * gamma

        def _rope(x, theta):
            seq = x.shape[2]
            angles = jnp.arange(seq, dtype=theta.dtype)[:, None] * theta
            cos = jnp.cos(angles)[None, None]
            sin = jnp.sin(angles)[None, None]
            x1, x2 = (x[..., 0::2], x[..., 1::2])
            return jnp.concatenate([x1 * cos - x2 * sin, x1 * sin + x2 * cos], axis=-1)

        def _forward(x, theta, gamma1, gamma2, q_w, q_b, k_w, k_b, v_w, v_b, o_w, o_b, router_w, router_b, sh_w1, sh_b1, sh_w2, sh_b2, re_w1, re_b1, re_w2, re_b2):
            b, s, d = x.shape
            xn = _rmsnorm(x, gamma1)
            q = (xn @ q_w + q_b).reshape(b, s, H, HD).transpose(0, 2, 1, 3)
            k = (xn @ k_w + k_b).reshape(b, s, H, HD).transpose(0, 2, 1, 3)
            v = (xn @ v_w + v_b).reshape(b, s, H, HD).transpose(0, 2, 1, 3)
            q = _rope(q, theta)
            k = _rope(k, theta)
            scale = 1.0 / np.sqrt(HD)
            scores = jnp.einsum('bhqd,bhkd->bhqk', q, k) * scale
            causal = jnp.tril(jnp.ones((s, s), dtype=bool))
            scores = jnp.where(causal, scores, -jnp.inf)
            attn = jax.nn.softmax(scores, axis=-1)
            ctx = jnp.einsum('bhqk,bhkd->bhqd', attn, v)
            ctx = ctx.transpose(0, 2, 1, 3).reshape(b, s, H * HD)
            attn_out = ctx @ o_w + o_b + xn
            an = _rmsnorm(attn_out, gamma2)
            shared = jax.nn.gelu(an @ sh_w1 + sh_b1, approximate=False) @ sh_w2 + sh_b2
            logits = an @ router_w + router_b
            aff = jax.nn.softmax(logits, axis=-1)
            topv, topi = jax.lax.top_k(aff, K_ACT)
            gates = jnp.sum(jax.nn.one_hot(topi, E_R, dtype=aff.dtype) * topv[..., None], axis=-2)
            h = jax.nn.gelu(jnp.einsum('bsd,edh->besh', an, re_w1) + re_b1[None, :, None, :], approximate=False)
            routed = jnp.einsum('bse,besh,ehd->bsd', gates, h, re_w2) + jnp.einsum('bse,ed->bsd', gates, re_b2)
            return shared + routed + an + attn_out
        del positions
        return _forward(x, theta, gamma1, gamma2, q_w, q_b, k_w, k_b, v_w, v_b, o_w, o_b, router_w, router_b, sh_w1, sh_b1, sh_w2, sh_b2, re_w1, re_b1, re_w2, re_b2)
    x = x + _L0_xattn_ref(_layernorm(x, axis=-1), ctx_1024, ctx_1024, L0_xattn_wq, L0_xattn_bq, L0_xattn_wk, L0_xattn_bk, L0_xattn_wv, L0_xattn_bv, L0_xattn_wo, L0_xattn_bo)
    x = x + _L0_ffn_ref(_layernorm(x, axis=-1), L0_ffn_positions, L0_ffn_theta, L0_ffn_gamma1, L0_ffn_gamma2, L0_ffn_q_w, L0_ffn_q_b, L0_ffn_k_w, L0_ffn_k_b, L0_ffn_v_w, L0_ffn_v_b, L0_ffn_o_w, L0_ffn_o_b, L0_ffn_router_w, L0_ffn_router_b, L0_ffn_sh_w1, L0_ffn_sh_b1, L0_ffn_sh_w2, L0_ffn_sh_b2, L0_ffn_re_w1, L0_ffn_re_b1, L0_ffn_re_w2, L0_ffn_re_b2)
    return x

_drawn_inputs = setup_inputs


def setup_inputs(seed=0):
    import zlib

    import numpy as np

    out = dict(_drawn_inputs(seed))
    spreads = {'L0_xattn_bq': (0.0, 0.341),
     'L0_xattn_bk': (0.0, 2.0),
     'L0_xattn_bv': (0.0, 0.1),
     'L0_xattn_bo': (0.0, 0.1),
     'L0_ffn_gamma1': (1.0, 0.2),
     'L0_ffn_gamma2': (1.0, 0.2),
     'L0_ffn_q_b': (0.0, 0.8),
     'L0_ffn_k_b': (0.0, 0.8),
     'L0_ffn_v_b': (0.0, 0.1),
     'L0_ffn_o_b': (0.0, 0.1),
     'L0_ffn_router_b': (0.0, 0.8),
     'L0_ffn_sh_b1': (0.0, 0.8),
     'L0_ffn_sh_b2': (0.0, 0.351),
     'L0_ffn_re_b1': (0.0, 0.8),
     'L0_ffn_re_b2': (0.0, 0.8)}
    factors = {'L0_ffn_theta': 8.0,
     'L0_ffn_q_w': 8.0,
     'L0_ffn_k_w': 8.0,
     'L0_ffn_router_w': 8.0,
     'L0_ffn_sh_w1': 3.243,
     'L0_ffn_sh_w2': 3.052,
     'L0_ffn_re_w1': 8.0,
     'L0_ffn_re_w2': 8.0}
    for name, (base, spread) in spreads.items():
        noise = np.random.default_rng([zlib.crc32(name.encode()), seed]).standard_normal(out[name].shape)
        drawn = base * np.exp(spread * noise) if base else spread * noise
        out[name] = jnp.asarray(drawn.astype(out[name].dtype))
    for name, factor in factors.items():
        out[name] = (out[name] * factor).astype(out[name].dtype)
    return out
```

```python
from contextlib import ExitStack

import numpy as np

import concourse.bass as bass
from concourse import mybir
from concourse.alu_op_type import AluOpType as ALU

F32 = mybir.dt.float32
F32R = mybir.dt.float32r
BF16 = mybir.dt.bfloat16
I32 = mybir.dt.int32
U32 = mybir.dt.uint32
ACT = mybir.ActivationFunctionType
AX = mybir.AxisListType

P = 128
B, S, D = 4, 512, 256
TOK = B * S
TILES = TOK // P
SB = S // P
DC = D // P
H = 16
D1 = D // H
D2 = 64
W2 = H * D2
QUADS = B * H // 4
E = 31
TOPK = 3
FF = 256
NT = (TOK * TOPK + E * (P - 1)) // P
EPS = 1e-5
MASKED = -1e30
TWO_PI = 2 * np.pi
TWO_PI_1 = 6.28125
TWO_PI_2 = float(np.round((TWO_PI - TWO_PI_1) * 2 ** 20) / 2 ** 20)
TWO_PI_3 = TWO_PI - TWO_PI_1 - TWO_PI_2
PI_BELOW = 3.1415925
ROUNDER = 1.5 * 2 ** 23
SP1 = 3 * D1
KCOL = [0, 512, 1024, 896]
KLEN = [S - P * kb for kb in range(SB)]
PCOLS = sum(KLEN)


class Alloc:

    def __init__(self, nc, tag):
        self.nc, self.tag, self.stack, self.sems = nc, tag, ExitStack(), []
        self.stack.callback(self.clear)

    def clear(self):
        if self.sems:
            self.nc.clear_and_free_semaphores(self.sems)
            self.nc.all_engine_barrier()

    def sb(self, name, shape, dt=F32):
        return self.stack.enter_context(self.nc.sbuf_tensor(f"{self.tag}_{name}", shape, dt))

    def ps(self, name, cols=512):
        return self.stack.enter_context(self.nc.psum_tensor(f"{self.tag}_{name}", [P, cols], F32))

    def sem(self, name):
        self.sems.append(self.nc.alloc_semaphore(f"{self.tag}_{name}"))
        return self.sems[-1]


def make_identities(nc, c):
    a = Alloc(nc, "const")
    c.ident = c.sb("ident", [P, P])
    c.ident_r = c.sb("ident_r", [P, P], F32R)
    c.ident_b = c.sb("ident_b", [P, P], BF16)
    c.mask_kq = c.sb("mask_kq", [P, P], BF16)
    c.mask_qk = c.sb("mask_qk", [P, S])
    with a.stack:
        filled, shaped, turned = a.sem("filled"), a.sem("shaped"), a.sem("turned")
        block = a.stack.enter_context(nc.Block())

        @block.gpsimd
        def _(pool):
            pool.memset(c.ident[:, :], 0.0).then_inc(filled, 1)
            pool.memset(c.ident_b[:, :], 0.0).then_inc(filled, 1)
            pool.memset(c.mask_kq[:, :], 0.0).then_inc(filled, 1)
            pool.memset(c.mask_qk[:, :], 0.0).then_inc(filled, 1)
            pool.wait_ge(filled, 4)
            for m in (c.ident, c.ident_b):
                pool.affine_select(out=m[:, :], in_=m[:, :], compare_op=ALU.not_equal, fill=1.0, base=0,
                                   pattern=[[-1, P]], channel_multiplier=1).then_inc(shaped, 1)
            pool.affine_select(out=c.mask_kq[:, :], in_=c.mask_kq[:, :], compare_op=ALU.is_ge, fill=MASKED,
                               base=0, pattern=[[1, P]], channel_multiplier=-1).then_inc(shaped, 1)
            pool.affine_select(out=c.mask_qk[:, S - P:S], in_=c.mask_qk[:, S - P:S], compare_op=ALU.is_ge,
                               fill=MASKED, base=0, pattern=[[-1, P]], channel_multiplier=1).then_inc(shaped, 1)

        @block.vector
        def _(dve):
            dve.wait_ge(shaped, 1)
            dve.tensor_scalar(c.ident_r[:, :], c.ident[:, :], -1.0, None, ALU.mult).then_inc(turned, 1)
            dve.wait_ge(turned, 1)
            dve.wait_ge(shaped, 4)


def make_tables(nc, c, rope, t):
    a = Alloc(nc, "table")
    c.cos, c.sin, c.cos_q, c.sin_q = (rope.sb(n, [P, S]) for n in ("cos", "sin", "cos_q", "sin_q"))
    with a.stack:
        counted, turned = a.sem("counted"), a.sem("turned")
        theta_in, reduced, sine, scaled_done = (a.sem(n) for n in ("theta_in", "reduced", "sine", "scaled_done"))
        theta, angle, whole, turn = a.sb("theta", [P, 1]), a.sb("angle", [P, S]), a.sb("whole", [P, S]), a.sb("turn", [P, 2, S])
        count = a.sb("count", [P, S], I32)
        block = a.stack.enter_context(nc.Block())

        @block.gpsimd
        def _(pool):
            pool.iota(count[:, :], pattern=[[1, S]], base=0, channel_multiplier=0).then_inc(counted, 1)

        @block.sync
        def _(sp):
            for h in range(4):
                sp.dma_start(theta[32 * h:32 * h + 32, :], t["L0_ffn_theta"]).then_inc(theta_in, 16)

        @block.scalar
        def _(act):
            for n, (table, scaled) in enumerate(((c.sin, c.sin_q), (c.cos, c.cos_q))):
                act.wait_ge(reduced, n + 1)
                act.activation(table[:, :], turn[:, n, :], ACT.Sin).then_inc(sine, 1)
                act.wait_ge(sine, n + 1)
                act.activation(scaled[:, :], table[:, :], ACT.Copy, scale=D2 ** -0.5).then_inc(scaled_done, 1)

        @block.vector
        def _(dve):
            dve.wait_ge(counted, 1)
            dve.tensor_copy(angle[:, :], count[:, :]).then_inc(turned, 1)
            dve.wait_ge(theta_in, 64)
            dve.wait_ge(turned, 1)
            dve.tensor_scalar(angle[:, :], angle[:, :], theta[:, 0:1], None, ALU.mult).then_inc(turned, 1)
            dve.wait_ge(turned, 2)
            n = 2
            for i, quarter in enumerate((0.0, 0.25)):
                tr = turn[:, i, :]
                steps = [lambda: dve.tensor_scalar(whole[:, :], angle[:, :], 1.0 / TWO_PI, quarter, ALU.mult, ALU.add),
                         lambda: dve.tensor_scalar(whole[:, :], whole[:, :], ROUNDER, None, ALU.add),
                         lambda: dve.tensor_scalar(whole[:, :], whole[:, :], -ROUNDER, None, ALU.add),
                         lambda: dve.scalar_tensor_tensor(out=tr, in0=whole[:, :], scalar=-TWO_PI_1, in1=angle[:, :],
                                                          op0=ALU.mult, op1=ALU.add),
                         lambda: dve.scalar_tensor_tensor(out=tr, in0=whole[:, :], scalar=-TWO_PI_2, in1=tr,
                                                          op0=ALU.mult, op1=ALU.add),
                         lambda: dve.scalar_tensor_tensor(out=tr, in0=whole[:, :], scalar=-TWO_PI_3, in1=tr,
                                                          op0=ALU.mult, op1=ALU.add),
                         lambda: dve.tensor_scalar(tr, tr, TWO_PI * quarter, PI_BELOW, ALU.add, ALU.min)]
                for s in steps:
                    s().then_inc(turned, 1)
                    n += 1
                    dve.wait_ge(turned, n)
                dve.tensor_scalar(tr, tr, -PI_BELOW, None, ALU.max).then_inc(reduced, 1)
            dve.wait_ge(scaled_done, 2)


def project1(nc, c, t):
    a = Alloc(nc, "p1")
    with a.stack:
        x, ctx_in, xl = (a.sb(n, [P, TILES, D]) for n in ("x", "ctx", "xl"))
        xT, cT = (a.sb(n, [P, DC, TOK]) for n in ("xT", "cT"))
        wq, wk, wv = (a.sb(n, [P, DC, D]) for n in ("wq", "wk", "wv"))
        bq, bq4, bk = (a.sb(n, [P, DC]) for n in ("bq", "bq4", "bk"))
        bv = a.sb("bv", [P, D])
        stats, mv, rstd = a.sb("stats", [P, TILES, 6]), a.sb("mv", [P, TILES, 2]), a.sb("rstd", [P, 3, TILES])
        full = a.sb("full", [P, 4, S])
        high, low = a.sb("high", [P, 4, S], F32R), a.sb("low", [P, 4, S], F32R)
        vout = a.sb("vout", [P, 4, 2, D])
        tb = [a.ps(f"tb{i}") for i in range(4)]
        qb = [a.ps(f"qb{i}") for i in range(2)]
        vb = [a.ps(f"vb{i}") for i in range(2)]
        x_in = [a.sem(f"x_in{b}") for b in range(B)]
        c_in = [a.sem(f"c_in{b}") for b in range(B)]
        w_in, stat_done, norm_step, xl_ready = a.sem("w_in"), a.sem("stat_done"), a.sem("norm_step"), a.sem("xl_ready")
        sq_done, c_turned, x_turned, c_copied, x_copied = (a.sem(n) for n in (
            "sq_done", "c_turned", "x_turned", "c_copied", "x_copied"))
        qk_mul, qk_full, split, v_mul, v_full = (a.sem(n) for n in ("qk_mul", "qk_full", "split", "v_mul", "v_full"))
        high_done = a.sem("high_done")
        bq_scaled = a.sem("bq_scaled")
        stack_out = [a.sem(f"stack_out{i}") for i in range(4)]
        v_out = [a.sem(f"v_out{i}") for i in range(4)]
        block = a.stack.enter_context(nc.Block())
        SCALE = D1 ** -0.5

        @block.sync
        def _(sp):
            xv = t["x"].rearrange("b (s p) d -> b p s d", p=P)
            cv = t["ctx_1024"].rearrange("b (s p) d -> b p s d", p=P)
            for b in range(B):
                sp.dma_start(ctx_in[:, SB * b:SB * b + SB, :], cv[b]).then_inc(c_in[b], 16)
                sp.dma_start(x[:, SB * b:SB * b + SB, :], xv[b]).then_inc(x_in[b], 16)
            for u in range(4 * B):
                b, is_q, m = u // 4, u % 4 >= 2, u % 2
                sp.wait_ge(split, u + 1)
                dst = (t["qs1"] if is_q else t["ks1"])[b * H + 8 * m:b * H + 8 * m + 8]
                parts = [(high, 0), (low, D1), (high, 2 * D1)] if is_q else [(high, 0), (high, D1), (low, 2 * D1)]
                for src, row in parts:
                    sp.dma_start(dst[:, row:row + D1, :], src[:, u % 4, :].bitcast(F32)).then_inc(stack_out[u % 4], 16)
                if not is_q:
                    n = 2 * b + m
                    sp.wait_ge(v_full, 2 * (n + 1))
                    for j in range(2):
                        tile = 2 * n + j
                        sp.dma_start(t["vs1"][SB * b:SB * b + SB, P * (tile % SB):P * (tile % SB) + P, :]
                                     .rearrange("g p d -> p g d"),
                                     vout[:, n % 4, j, :].rearrange("p (g d) -> p g d", g=4)).then_inc(v_out[n % 4], 16)
            for i in range(4):
                sp.wait_ge(stack_out[i], 16 * 3 * B)
                sp.wait_ge(v_out[i], 16 * 2 * 2 * B // 4)

        @block.scalar
        def _(act):
            for dst, name in ((wk, "L0_xattn_wk"), (wv, "L0_xattn_wv"), (wq, "L0_xattn_wq")):
                act.dma_start(dst[:, :, :], t[name].rearrange("(k p) n -> p k n", p=P)).then_inc(w_in, 16)
            for dst, name in ((bq, "L0_xattn_bq"), (bk, "L0_xattn_bk")):
                act.dma_start(dst[:, :], t[name]).then_inc(w_in, 16)
            act.dma_start(bv[:, :], t["L0_xattn_bv"].to_broadcast([P, D])).then_inc(w_in, 16)
            act.wait_ge(w_in, 16 * 6)
            act.activation(bq4[:, :], bq[:, :], ACT.Copy, scale=SCALE).then_inc(bq_scaled, 1)

            def turned_ctx(b):
                for k in range(DC):
                    n = DC * b + k
                    act.wait_ge(c_turned, n + 1)
                    act.activation(cT[:, k, S * b:S * b + S], tb[n % 2][:, :], ACT.Copy).then_inc(c_copied, 1)

            def unit(u):
                is_q, m = u % 4 >= 2, u % 2
                act.wait_ge(qk_mul, u + 1)
                if u >= 4:
                    act.wait_ge(split, u - 3)
                if u == 2:
                    act.wait_ge(bq_scaled, 1)
                act.activation(full[:, u % 4, :], qb[u % 2][:, :], ACT.Identity,
                               bias=(bq4 if is_q else bk)[:, m:m + 1], scale=SCALE if is_q else 1.0).then_inc(qk_full, 1)

            turned_ctx(0)
            for b in range(B):
                act.wait_ge(norm_step, 2 * b + 1)
                act.activation(rstd[:, 1, SB * b:SB * b + SB], rstd[:, 0, SB * b:SB * b + SB], ACT.Sqrt).then_inc(sq_done, 1)
            for b in range(B):
                unit(4 * b)
                unit(4 * b + 1)
                if b + 1 < B:
                    turned_ctx(b + 1)
                unit(4 * b + 2)
                unit(4 * b + 3)

        @block.tensor
        def _(pe):
            def turn(src, banks, b, copied, turned):
                for k in range(DC):
                    n = DC * b + k
                    if n >= 2:
                        pe.wait_ge(copied, n - 1)
                    for s in range(SB):
                        mm = pe.transpose(banks[n % 2][:, P * s:P * s + P], src[:, SB * b + s, P * k:P * k + P],
                                          c.ident[:, :])
                    mm.then_inc(turned, 1)

            def unit(u, w, src):
                b, m = u // 4, u % 2
                if u >= 2:
                    pe.wait_ge(qk_full, u - 1)
                for k in range(DC):
                    mm = pe.matmul(qb[u % 2][:, :], w[:, k, P * m:P * m + P], src[:, k, S * b:S * b + S],
                                   start=(k == 0), stop=(k == DC - 1))
                mm.then_inc(qk_mul, 1)

            def values(n):
                if n >= 2:
                    pe.wait_ge(v_full, 2 * (n - 1))
                for j in range(2):
                    tile = 2 * n + j
                    for k in range(DC):
                        mm = pe.matmul(vb[n % 2][:, D * j:D * j + D], cT[:, k, P * tile:P * tile + P], wv[:, k, :],
                                       start=(k == 0), stop=(k == DC - 1))
                mm.then_inc(v_mul, 1)

            pe.wait_ge(c_in[0], 16)
            turn(ctx_in, tb[0:2], 0, c_copied, c_turned)
            for b in range(B):
                pe.wait_ge(c_copied, DC * (b + 1))
                if b == 0:
                    pe.wait_ge(w_in, 16 * 6)
                unit(4 * b, wk, cT)
                unit(4 * b + 1, wk, cT)
                values(2 * b)
                values(2 * b + 1)
                if b + 1 < B:
                    pe.wait_ge(c_in[b + 1], 16)
                    turn(ctx_in, tb[0:2], b + 1, c_copied, c_turned)
                pe.wait_ge(xl_ready, SB * (b + 1))
                turn(xl, tb[2:4], b, x_copied, x_turned)
                pe.wait_ge(x_copied, DC * (b + 1))
                unit(4 * b + 2, wq, xT)
                unit(4 * b + 3, wq, xT)

        @block.vector
        def _(dve):
            for b in range(B):
                dve.wait_ge(x_in[b], 16)
                for i in range(SB * b, SB * b + SB):
                    dve.bn_stats(stats[:, i, :], x[:, i, :]).then_inc(stat_done, 1)
                    dve.wait_ge(stat_done, 2 * i + 1)
                    dve.bn_aggr(mv[:, i, :], stats[:, i, :]).then_inc(stat_done, 1)
                tiles = slice(SB * b, SB * b + SB)
                dve.wait_ge(stat_done, 2 * SB * (b + 1))
                dve.tensor_scalar(rstd[:, 0, tiles], mv[:, tiles, 1], EPS, None, ALU.add).then_inc(norm_step, 1)
                dve.wait_ge(sq_done, b + 1)
                dve.reciprocal(rstd[:, 2, tiles], rstd[:, 1, tiles]).then_inc(norm_step, 1)
                dve.wait_ge(norm_step, 2 * b + 2)
                for i in range(SB * b, SB * b + SB):
                    dve.tensor_scalar(xl[:, i, :], x[:, i, :], mv[:, i, 0:1], rstd[:, 2, i:i + 1],
                                      ALU.subtract, ALU.mult).then_inc(xl_ready, 1)

            def parts(u):
                dve.wait_ge(qk_full, u + 1)
                if u >= 4:
                    dve.wait_ge(stack_out[u % 4], 16 * 3 * (u // 4))
                dve.tensor_copy(high[:, u % 4, :], full[:, u % 4, :]).then_inc(high_done, 1)
                dve.wait_ge(high_done, u + 1)
                dve.tensor_sub(low[:, u % 4, :], full[:, u % 4, :], high[:, u % 4, :].bitcast(F32)).then_inc(split, 1)

            for b in range(B):
                for n in (2 * b, 2 * b + 1):
                    dve.wait_ge(v_mul, n + 1)
                    if n == 0:
                        dve.wait_ge(w_in, 16 * 6)
                    if n >= 4:
                        dve.wait_ge(v_out[n % 4], 32 * (n // 4))
                    for j in range(2):
                        dve.tensor_add(vout[:, n % 4, j, :], vb[n % 2][:, D * j:D * j + D], bv[:, :]).then_inc(v_full, 1)
                parts(4 * b)
                parts(4 * b + 1)
                for k in range(DC):
                    n = DC * b + k
                    dve.wait_ge(x_turned, n + 1)
                    dve.tensor_copy(xT[:, k, S * b:S * b + S], tb[2 + n % 2][:, :]).then_inc(x_copied, 1)
                parts(4 * b + 2)
                parts(4 * b + 3)



def attention(nc, c, t, two):
    a = Alloc(nc, "a2" if two else "a1")
    stacks_q, stacks_k, values_d, out_d, sums_d = (
        t["qs2" if two else "qs1"], t["ks2" if two else "ks1"], t["vs2" if two else "vs1"], t["o2" if two else "o1"],
        t["s2" if two else "s1"])
    HEADS = B * H
    PASSES = HEADS // 8
    PEELED = 2
    NLOAD = 5 if two else 2
    NV = 1 if two else SB
    KR = 64
    KS = D2 if two else SP1
    OUTS = 2 if two else 1
    NSTORE = 3 if two else 5
    with a.stack:
        qa = a.sb("qa", [P, 4, S], F32R) if two else None
        ka = a.sb("ka", [P, 4, S], F32R) if two else None
        qm = a.sb("qm", [KR + 1, 4, S], F32R)
        km = a.sb("km", [KR + 1, 4, S], F32R)
        vals = a.sb("vals", [P, 2, SB, 4, D2 if two else 32])
        probs = a.sb("probs", [P, 8, PCOLS])
        junk = a.sb("junk", [P, SB, S], BF16)
        mx = a.sb("mx", [P, 2, SB])
        mxr = a.sb("mxr", [P, 2, SB], F32R)
        ones = a.sb("ones", [P, 32]) if two else None
        osb = a.sb("osb", [P, 2, S])
        ssb = a.sb("ssb", [P, 2, S]) if two else None
        sc = [a.ps("sc0"), a.ps("sc1")]
        sc.append(sc[0] if two else a.ps("sc2"))
        mrow = a.ps("mrow")
        st = a.ps("st", 1536)
        ob = a.ps("ob")
        sums = a.ps("sums") if two else None

        loaded = [a.sem(f"loaded{i}") for i in range(4)]
        v_loaded = [a.sem(f"v_loaded{i}") for i in range(2)]
        stored = [a.sem(f"stored{i}") for i in range(2)]
        set_up, scored, reduced, maxed, turned, row_set, st_done, exp_done = (a.sem(n) for n in (
            "set_up", "scored", "reduced", "maxed", "turned", "row_set", "st_done", "exp_done"))
        pv_done, o_copied = a.sem("pv_done"), a.sem("o_copied")
        block = a.stack.enter_context(nc.Block())
        NSET = 3 if two else 4

        def ge(eng, sem, it, per_pass, const):
            if not isinstance(it, int):
                assert PEELED * per_pass + const > 0
                eng.wait_ge(sem, per_pass * it + const)
            elif per_pass * it + const > 0:
                eng.wait_ge(sem, per_pass * it + const)

        def steps(eng, step, last):
            for s in range(8 * PEELED):
                step(s // 8, s % 8)
            with eng.Fori(PEELED, PASSES) as it:
                for r in range(8):
                    step(it, r)
            for r in range(last + 1 - HEADS):
                step(PASSES, r)

        def there(it, r):
            return not isinstance(it, int) or 0 <= 8 * it + r < HEADS

        @block.sync
        def _(sp):
            def load_quad(it, j):
                for r in range(4 * j, 4 * j + 4):
                    sl = r % 4
                    ge(sp, st_done, it, 16, 2 * (r - 4) + 2)
                    q, k = stacks_q[8 * it + r], stacks_k[8 * it + r]
                    if two:
                        sp.dma_start(qa[:, sl, :].bitcast(F32), q).then_inc(loaded[sl], 16)
                        sp.dma_start(ka[0:D2, sl, :].bitcast(F32), k[0:D2, :]).then_inc(loaded[sl], 16)
                        sp.dma_start(ka[D2:P, sl, :].bitcast(F32), k[0:D2, :]).then_inc(loaded[sl], 16)
                        sp.dma_start(qm[0:D2, sl, :].bitcast(F32), q[0:D2, :]).then_inc(loaded[sl], 16)
                        sp.dma_start(km[0:D2, sl, :].bitcast(F32), k[D2:P, :]).then_inc(loaded[sl], 16)
                    else:
                        sp.dma_start(qm[0:SP1, sl, :].bitcast(F32), q).then_inc(loaded[sl], 16)
                        sp.dma_start(km[0:SP1, sl, :].bitcast(F32), k).then_inc(loaded[sl], 16)
                ge(sp, pv_done, it, 8, 4 * j - 4)
                src = values_d[2 * it + j].rearrange("(kb p) d -> p kb d", p=P)
                if two:
                    sp.dma_start(vals[:, j, :, :, :].rearrange("p kb h d -> p kb (h d)"), src).then_inc(v_loaded[j], 16)
                else:
                    for kb in range(SB):
                        sp.dma_start(vals[:, j, kb, :, 0:D1], src[:, kb, :].rearrange("p (h d) -> p h d", h=4))\
                          .then_inc(v_loaded[j], 16)

            sp.wait_ge(set_up, NSET)
            for n in range(2 * PEELED):
                load_quad(n // 2, n % 2)
            with sp.Fori(PEELED, PASSES) as it:
                load_quad(it, 0)
                load_quad(it, 1)

        @block.gpsimd
        def _(pool):
            pool.memset(km[KR:KR + 1, :, :].bitcast(F32), 1.0).then_inc(set_up, 1)
            pool.wait_ge(set_up, 1)
            if two:
                pool.memset(ones[:, :], 1.0).then_inc(set_up, 1)
                pool.wait_ge(set_up, 2)
                pool.memset(ssb[64:P, :, 0:P], 0.0).then_inc(set_up, 1)
            else:
                pool.memset(km[32:KR, :, :].bitcast(F32), 0.0).then_inc(set_up, 1)
                pool.wait_ge(set_up, 2)
                pool.memset(qm[32:KR, :, :].bitcast(F32), 0.0).then_inc(set_up, 1)
                pool.wait_ge(set_up, 3)
                pool.memset(vals[:, :, :, :, :], 1.0).then_inc(set_up, 1)

            def store(it, n):
                sl = n % 2
                i = 2 * OUTS * it + n
                pool.wait_ge(o_copied, i + 1)
                if two:
                    pool.dma_start(out_d[i], osb[:, sl, :]).then_inc(stored[sl], 16)
                    for par in range(2):
                        pool.dma_start(sums_d[par, :, i, :], ssb[64 * par:64 * par + 64:32, sl, :]).then_inc(stored[sl], 16)
                else:
                    for j in range(4):
                        pool.dma_start(out_d[i, j], osb[32 * j:32 * j + D1, sl, :]).then_inc(stored[sl], 16)
                    pool.dma_start(sums_d[i], osb[D1:P:32, sl, :]).then_inc(stored[sl], 16)

            with pool.Fori(0, PASSES) as it:
                for n in range(2 * OUTS):
                    store(it, n)
            for sl in range(2):
                pool.wait_ge(stored[sl], NSTORE * 16 * PASSES * OUTS)

        @block.tensor
        def _(pe):
            def score(out, sl, qb, n):
                q, k = slice(P * qb, P * qb + P), slice(0, n)
                if two:
                    pe.matmul(out, qa[:, sl, q], ka[:, sl, k], start=True, stop=False)
                    return pe.matmul(out, qm[0:D2, sl, q], km[0:D2, sl, k], start=False, stop=True)
                return pe.matmul(out, qm[0:KR, sl, q], km[0:KR, sl, k], start=True, stop=True)

            def shifted(sl, kb):
                out = st[:, KCOL[kb]:KCOL[kb] + KLEN[kb]]
                k, q = slice(P * kb, P * kb + P), slice(P * kb, S)
                if two:
                    pe.matmul(out, ka[:, sl, k], qa[:, sl, q], start=True, stop=False)
                pe.matmul(out, km[:, sl, k], qm[:, sl, q], start=not two, stop=False)
                return pe.matmul(out[:, 0:P], c.ident_b[:, :], c.mask_kq[:, :], start=False, stop=True)

            def step(it, r):
                if there(it, r):
                    sl = r % 4
                    pe.wait_ge(loaded[sl], 16 * NLOAD * (2 * it + r // 4 + 1))
                    ge(pe, reduced, it, 24, 3 * r - (0 if two else 2))
                    score(sc[0][:, :], sl, 3, S).then_inc(scored, 1)
                    ge(pe, reduced, it, 24, 3 * r - 1)
                    score(sc[1][:, 0:3 * P], sl, 2, 3 * P)
                    score(sc[1][:, 3 * P:S], sl, 0, P).then_inc(scored, 1)
                if there(it, r - 2):
                    sl = (r - 2) % 4
                    ge(pe, row_set, it, 8, r - 1)
                    ge(pe, exp_done, it, 16, 2 * (r - 2) - 1)
                    shifted(sl, 0)
                    shifted(sl, 1)
                    shifted(sl, 3).then_inc(st_done, 1)
                    ge(pe, exp_done, it, 16, 2 * (r - 2))
                    shifted(sl, 2).then_inc(st_done, 1)
                if there(it, r):
                    ge(pe, reduced, it, 24, 3 * r + (1 if two else 0))
                    score(sc[2][:, 0:2 * P], r % 4, 1, 2 * P).then_inc(scored, 1)
                if there(it, r - 1):
                    h = r - 1
                    ge(pe, maxed, it, 8, h + 1)
                    ge(pe, row_set, it, 8, h)
                    for qb in range(SB):
                        mm = pe.matmul(mrow[0:1, P * qb:P * qb + P], mxr[:, h % 2, qb:qb + 1], c.ident_r[:, :],
                                       start=True, stop=True)
                    mm.then_inc(turned, 1)
                if there(it, r - 6):
                    n, j = (r - 6) // 4, (r - 6) % 4
                    if j == 0:
                        pe.wait_ge(v_loaded[n % 2], 16 * NV * (it + n // 2 + 1))
                    if two:
                        pair = j // 2
                        ge(pe, exp_done, it, 16, 2 * (4 * n + 2 * pair + 2))
                        if j % 2 == 0:
                            ge(pe, o_copied, it, 4, 2 * n + pair)
                        kbs = ((0, 1), (2, 3))[j % 2]

                        def exps(hh, kb):
                            return probs[:, (4 * n + 2 * pair + hh) % 8, KCOL[kb]:KCOL[kb] + KLEN[kb]]

                        for kb in kbs:
                            for hh in range(2):
                                pe.matmul(ob[D2 * hh:D2 * hh + D2, P * kb:S], vals[:, n % 2, kb, 2 * pair + hh, :],
                                          exps(hh, kb), start=(kb == 0), stop=(kb == SB - 1))
                        for kb in kbs:
                            for hh in range(2):
                                row = 64 * (kb % 2) + 32 * hh
                                mm = pe.matmul(sums[row:row + 32, P * kb:S], ones[:, :], exps(hh, kb),
                                               start=(kb < 2), stop=(kb >= 2), tile_position=(0, row))
                    else:
                        ge(pe, exp_done, it, 16, 2 * (4 * n + 4))
                        if j == 0:
                            ge(pe, o_copied, it, 2, n)
                        for hq in range(4):
                            mm = pe.matmul(ob[32 * hq:32 * hq + 32, P * j:S], vals[:, n % 2, j, hq, :],
                                           probs[:, (4 * n + hq) % 8, KCOL[j]:KCOL[j] + KLEN[j]],
                                           start=(j == 0), stop=(j == SB - 1), tile_position=(0, 32 * hq))
                    mm.then_inc(pv_done, 1)

            pe.wait_ge(set_up, NSET)
            steps(pe, step, HEADS + 5)

        @block.scalar
        def _(act):
            if two:
                for k in range(DC):
                    act.dma_start(c.w1[:, :, FF * k:FF * k + FF], t["L0_ffn_re_w1"][:, P * k:P * k + P, :]
                                  .rearrange("e p n -> p e n")).then_inc(c.w1_in, 16)
                act.dma_start(c.w1[:, :, DC * FF:], t["L0_ffn_re_b1"]).then_inc(c.w1_in, 16)

            def step(it, r):
                if there(it, r - 2):
                    h = r - 2
                    n = (h - 8) // 4
                    ge(act, pv_done, it, 8, 4 * n + 4)
                    ge(act, st_done, it, 16, 2 * h + 1)
                    act.activation(probs[:, h % 8, 0:2 * S], st[:, 0:2 * S], ACT.Exp).then_inc(exp_done, 1)
                    ge(act, st_done, it, 16, 2 * h + 2)
                    act.activation(probs[:, h % 8, 2 * S:PCOLS], st[:, 2 * S:PCOLS], ACT.Exp).then_inc(exp_done, 1)
                if there(it, r - 1):
                    h = r - 1
                    ge(act, turned, it, 8, h + 1)
                    act.activation(qm[KR:KR + 1, h % 4, :], mrow[0:1, :], ACT.Copy).then_inc(row_set, 1)
                if (r - 6) % (4 // OUTS) == 4 // OUTS - 1 and there(it, r - 6):
                    p = r - 6
                    n = p // (4 // OUTS)
                    ge(act, pv_done, it, 8, p + 1)
                    ge(act, stored[n % 2], it, 16 * NSTORE * OUTS, 16 * NSTORE * (n // 2))
                    if two:
                        act.activation(osb[:, n % 2, :], ob[:, :], ACT.Copy)
                        act.activation(ssb[0:64, n % 2, :], sums[0:64, :], ACT.Copy)
                        act.activation(ssb[64:P, n % 2, P:S], sums[64:P, P:S], ACT.Copy).then_inc(o_copied, 1)
                    else:
                        act.activation(osb[:, n % 2, :], ob[:, :], ACT.Copy).then_inc(o_copied, 1)

            steps(act, step, HEADS + 5)

        @block.vector
        def _(dve):
            def largest(it, r, src, qb):
                n = P * qb + P
                dve.nop(nofuse=True)
                return dve.tensor_tensor_reduce(
                    out=junk[:, qb, 0:n], in0=src, in1=c.mask_qk[:, S - n:S], scale=1.0, scalar=-3e38,
                    op0=ALU.add, op1=ALU.max, accum_out=mx[:, r % 2, qb:qb + 1])

            def step(it, r):
                if there(it, r):
                    ge(dve, scored, it, 24, 3 * r + 1)
                    largest(it, r, sc[0][:, :], 3).then_inc(reduced, 1)
                    ge(dve, scored, it, 24, 3 * r + 2)
                    largest(it, r, sc[1][:, 0:3 * P], 2)
                    largest(it, r, sc[1][:, 3 * P:S], 0).then_inc(reduced, 1)
                    ge(dve, scored, it, 24, 3 * r + 3)
                    largest(it, r, sc[2][:, 0:2 * P], 1).then_inc(reduced, 1)
                    ge(dve, reduced, it, 24, 3 * r + 3)
                    ge(dve, turned, it, 8, r - 1)
                    dve.tensor_copy(mxr[:, r % 2, :], mx[:, r % 2, :]).then_inc(maxed, 1)

            steps(dve, step, HEADS - 1)

class Tally:

    def __init__(self, sem):
        self.sem, self.n = sem, 0

    def add(self, instruction, by=1):
        self.n += by
        instruction.then_inc(self.sem, by)
        return self.n


def inverse_root(dve, r, cols, tick, rooted, n):
    v, root, inv, out = (r[:, i, cols] for i in range(4))
    dve.wait_ge(rooted, n)
    k = tick.add(dve.reciprocal(inv, root))
    dve.wait_ge(tick.sem, k)
    k = tick.add(dve.tensor_mul(out, inv, inv))
    dve.wait_ge(tick.sem, k)
    k = tick.add(dve.tensor_mul(out, out, v))
    dve.wait_ge(tick.sem, k)
    k = tick.add(dve.tensor_scalar(out, out, -0.5, 1.5, ALU.mult, ALU.add))
    dve.wait_ge(tick.sem, k)
    k = tick.add(dve.tensor_mul(out, out, inv))
    dve.wait_ge(tick.sem, k)


def project2(nc, c, t):
    a = Alloc(nc, "p2")
    with a.stack:
        sraw = a.sb("sraw", [P, QUADS * 4 * S // P])
        srec = a.sb("srec", [P, QUADS * 4 * S // P])
        oT, rT = a.sb("oT", [P, 2, DC, S]), a.sb("rT", [P, 2, DC, S])
        wo = a.sb("wo", [P, DC, D])
        bo, g1 = a.sb("bo", [P, D]), a.sb("g1", [P, D])
        x = a.sb("x", [P, 2, SB, D])
        x1, xf, xn = (a.sb(n, [P, 2, SB, D]) for n in ("x1", "xf", "xn"))
        sq = a.sb("sq", [P, D])
        stats, mv = a.sb("stats", [P, TILES, 6]), a.sb("mv", [P, TILES, 2])
        r1, r2 = a.sb("r1", [P, 4, TILES]), a.sb("r2", [P, 4, TILES])
        ssum = a.sb("ssum", [P, TILES])
        xh, xlo = a.sb("xh", [P, DC, TOK], F32R), a.sb("xlo", [P, DC, TOK], F32R)
        w = a.sb("w", [P, DC, W2])
        wh = [a.sb(f"wh{i}", [P, DC, W2], F32R) for i in range(3)]
        wl = [a.sb(f"wl{i}", [P, DC, W2], F32R) for i in range(3)]
        bqk = a.sb("bqk", [P, 2, W2 // P])
        bv = a.sb("bv", [P, W2])
        prod = a.sb("prod", [P, 4, S])
        rot = a.sb("rot", [P, 2, 2, S])
        rh, rl = a.sb("rh", [P, 2, 2, S], F32R), a.sb("rl", [P, 2, 2, S], F32R)
        vout = a.sb("vout", [P, 2, W2])
        op = [a.ps("op0"), a.ps("op1")]
        tp = [a.ps("tp0"), a.ps("tp1")]
        ub = [a.ps(f"ub{i}") for i in range(4)]

        s_in, r_out, w_in, small_in = (a.sem(n) for n in ("s_in", "r_out", "w_in", "small_in"))
        o_in = [a.sem(f"o_in{i}") for i in range(B)]
        x_in = [a.sem(f"x_in{i}") for i in range(B)]
        srec_done, o_scaled, xb_done = (a.sem(n) for n in ("srec_done", "o_scaled", "xb_done"))
        projected, x1_done, xn_done, root_asked, rooted, squared = (a.sem(n) for n in (
            "projected", "x1_done", "xn_done", "root_asked", "rooted", "squared"))
        t_done, h_copied, parts_done, split_h, split_l = (a.sem(n) for n in (
            "t_done", "h_copied", "parts_done", "split_h", "split_l"))
        unit_done, prods, rotated, rot_h, rot_la, rot_lb = (a.sem(n) for n in (
            "unit_done", "prods", "rotated", "rot_h", "rot_la", "rot_lb"))
        xf_done = a.sem("xf_done")
        v_mul, v_full, tick_s = a.sem("v_mul"), a.sem("v_full"), a.sem("tick")
        u_out = [a.sem(f"u_out{i}") for i in range(2)]
        v_out = [a.sem(f"v_out{i}") for i in range(2)]
        r_st = [a.sem(f"resid_out{i}") for i in range(2)]
        block = a.stack.enter_context(nc.Block())
        WNAMES = ["L0_ffn_q_w", "L0_ffn_k_w", "L0_ffn_v_w"]
        UNITS = 8

        @block.sync
        def _(sp):
            sp.dma_start(sraw[:, :], t["s1"].rearrange("q h (a n) -> (q h a) n", n=QUADS * 4 * S // P)).then_inc(s_in, 16)
            sp.wait_ge(srec_done, 1)
            sp.dma_start(t["r1"].rearrange("q h (a n) -> (q h a) n", n=QUADS * 4 * S // P), srec[:, :]).then_inc(r_out, 16)
            sp.wait_ge(r_out, 16)

            def load(b):
                if b >= 2:
                    sp.wait_ge(projected, SB * (b - 1))
                    sp.wait_ge(x1_done, SB * (b - 1))
                for m in range(DC):
                    q = SB * b + 2 * m
                    sp.dma_start(oT[:, b % 2, m, :], t["o1"][q:q + 2].rearrange("q h d n -> (q h d) n")).then_inc(o_in[b], 16)
                    for j in range(2):
                        for hh in range(4):
                            p0 = 64 * j + D1 * hh
                            sp.dma_start(rT[p0:p0 + D1, b % 2, m, :], t["r1"][q + j, hh:hh + 1, :].to_broadcast([D1, S]))\
                              .then_inc(o_in[b], 16)
                sp.dma_start(x[:, b % 2, :, :], t["x"][b].rearrange("(s p) d -> p s d", p=P)).then_inc(x_in[b], 16)

            load(0)
            load(1)
            for b in range(B):
                sp.wait_ge(xn_done, SB * (b + 1))
                for src, name in ((x1, "x1"), (xn, "xn")):
                    sp.dma_start(t[name][SB * b:SB * b + SB].rearrange("s p d -> p s d"), src[:, b % 2, :, :])\
                      .then_inc(r_st[b % 2], 16)
                if b + 2 < B:
                    load(b + 2)
                for u in range(UNITS * b, UNITS * b + UNITS):
                    g, is_k = u % UNITS // 2, u % 2
                    dst = t["ks2" if is_k else "qs2"][b * H + 4 * g:b * H + 4 * g + 4]
                    sp.wait_ge(rot_h, 2 * (u + 1))
                    for half in range(2):
                        sp.dma_start(dst[:, 32 * half:32 * half + 32, :], rh[:, u % 2, half, :].bitcast(F32))\
                          .then_inc(u_out[u % 2], 16)
                    sp.wait_ge(rot_la, u + 1)
                    sp.dma_start(dst[:, 64:96, :], rl[:, u % 2, 0, :].bitcast(F32)).then_inc(u_out[u % 2], 16)
                    sp.wait_ge(rot_lb, u + 1)
                    sp.dma_start(dst[:, 96:128, :], rl[:, u % 2, 1, :].bitcast(F32)).then_inc(u_out[u % 2], 16)
                for i in range(SB * b, SB * b + SB):
                    sp.wait_ge(v_full, 2 * (i + 1))
                    sp.dma_start(t["vs2"][SB * b:SB * b + SB, P * (i % SB):P * (i % SB) + P, :].rearrange("g p d -> p g d"),
                                 vout[:, i % 2, :].rearrange("p (g d) -> p g d", g=4)).then_inc(v_out[i % 2], 16)
            for i in range(2):
                sp.wait_ge(r_st[i], 16 * 2 * B // 2)
                sp.wait_ge(u_out[i], 16 * 4 * UNITS * B // 2)
                sp.wait_ge(v_out[i], 16 * TILES // 2)

        @block.scalar
        def _(act):
            act.dma_start(wo[:, :, :], t["L0_xattn_wo"].rearrange("(k p) n -> p k n", p=P)).then_inc(small_in, 16)
            act.dma_start(bo[:, :], t["L0_xattn_bo"].to_broadcast([P, D])).then_inc(small_in, 16)
            act.dma_start(g1[:, :], t["L0_ffn_gamma1"].to_broadcast([P, D])).then_inc(small_in, 16)
            act.dma_start(bqk[:, 0, :], t["L0_ffn_q_b"]).then_inc(small_in, 16)
            act.dma_start(bqk[:, 1, :], t["L0_ffn_k_b"]).then_inc(small_in, 16)
            act.dma_start(bv[:, :], t["L0_ffn_v_b"].to_broadcast([P, W2])).then_inc(small_in, 16)
            for i, n in enumerate(WNAMES):
                if i:
                    act.wait_ge(split_l, i)
                act.dma_start(w[:, :, :], t[n].rearrange("(k p) n -> p k n", p=P)).then_inc(w_in, 16)

            def pre(b):
                cols = slice(SB * b, SB * b + SB)
                act.wait_ge(root_asked, 2 * b + 1)
                act.activation(r1[:, 1, cols], r1[:, 0, cols], ACT.Sqrt).then_inc(rooted, 1)
                for i in range(SB):
                    n = SB * b + i
                    act.wait_ge(xf_done, n + 1)
                    if n:
                        act.wait_ge(squared, n)
                    act.activation(sq[:, :], xf[:, b % 2, i, :], ACT.Square, accum_out=ssum[:, n:n + 1]).then_inc(squared, 1)
                act.wait_ge(root_asked, 2 * b + 2)
                act.activation(r2[:, 1, cols], r2[:, 0, cols], ACT.Sqrt).then_inc(rooted, 1)

            def post(b):
                for k in range(DC):
                    n = DC * b + k
                    act.wait_ge(t_done, n + 1)
                    act.activation(xh[:, k, S * b:S * b + S], tp[k][:, :], ACT.Copy).then_inc(h_copied, 1)
                for u in range(UNITS * b, UNITS * b + UNITS):
                    for half in range(2):
                        act.wait_ge(rotated, 2 * u + half + 1)
                        if u >= 2 and not half:
                            act.wait_ge(u_out[u % 2], 16 * 4 * (u // 2))
                        act.activation(rh[:, u % 2, half, :], rot[:, u % 2, half, :], ACT.Copy).then_inc(rot_h, 1)

            pre(0)
            for b in range(B):
                if b + 1 < B:
                    pre(b + 1)
                post(b)

        @block.tensor
        def _(pe):
            def outputs(b):
                pe.wait_ge(small_in, 16 * 6)
                for i in range(SB):
                    n = SB * b + i
                    bank = op[i // 2]
                    for m in range(DC):
                        pe.wait_ge(o_scaled, DC * b + m + 1)
                        if n >= SB and i % 2 == 0 and m == 0:
                            pe.wait_ge(x1_done, n - 2)
                        mm = pe.matmul(bank[:, D * (i % 2):D * (i % 2) + D], oT[:, b % 2, m, P * i:P * i + P],
                                       wo[:, m, :], start=(m == 0), stop=(m == DC - 1))
                    mm.then_inc(projected, 1)

            def turn(b):
                pe.wait_ge(xn_done, SB * (b + 1))
                if b:
                    pe.wait_ge(v_full, 2 * SB * b)
                for k in range(DC):
                    for i in range(SB):
                        mm = pe.transpose(tp[k][:, P * i:P * i + P], xn[:, b % 2, i, P * k:P * k + P], c.ident[:, :])
                    mm.then_inc(t_done, 1)

            def unit(u):
                b, g, i = u // UNITS, u % UNITS // 2, u % 2
                pe.wait_ge(split_l, i + 1)
                toks = slice(S * b, S * b + S)
                if u >= 2:
                    pe.wait_ge(prods, 4 * (u - 1))
                for half in range(2):
                    cols = slice(2 * P * g + P * half, 2 * P * g + P * half + P)
                    bank = ub[2 * (u % 2) + half]
                    n = 0
                    for k in range(DC):
                        for wt, xt in ((wh[i], xh), (wh[i], xlo), (wl[i], xh)):
                            mm = pe.matmul(bank[:, :], wt[:, k, cols], xt[:, k, toks], start=(n == 0), stop=(n == 5))
                            n += 1
                mm.then_inc(unit_done, 1)

            def values(b):
                pe.wait_ge(split_l, 3)
                for i in range(SB * b, SB * b + SB):
                    for half in range(2):
                        n = 2 * i + half
                        if n > 2 * SB * b + 1:
                            pe.wait_ge(v_full, n - 1)
                        k3 = 0
                        for k in range(DC):
                            for xt, wt in ((xh, wh[2]), (xh, wl[2]), (xlo, wh[2])):
                                mm = pe.matmul(tp[half][:, :], xt[:, k, P * i:P * i + P], wt[:, k, S * half:S * half + S],
                                               start=(k3 == 0), stop=(k3 == 5))
                                k3 += 1
                        mm.then_inc(v_mul, 1)

            outputs(0)
            for b in range(B):
                if b + 1 < B:
                    outputs(b + 1)
                turn(b)
                pe.wait_ge(parts_done, DC * (b + 1))
                for u in range(UNITS * b, UNITS * b + UNITS):
                    unit(u)
                values(b)

        @block.gpsimd
        def _(pool):
            def pre(b):
                pool.wait_ge(o_in[b], 16 * 9 * DC)
                for m in range(DC):
                    pool.tensor_tensor(oT[:, b % 2, m, :], oT[:, b % 2, m, :], rT[:, b % 2, m, :], ALU.mult).then_inc(o_scaled, 1)
                pool.wait_ge(x_in[b], 16)
                pool.wait_ge(small_in, 16 * 6)
                for i in range(SB):
                    pool.tensor_tensor(x[:, b % 2, i, :], x[:, b % 2, i, :], bo[:, :], ALU.add).then_inc(xb_done, 1)

            def post(b):
                for u in range(UNITS * b, UNITS * b + UNITS):
                    if u >= 2:
                        pool.wait_ge(rot_la, u - 1)
                        pool.wait_ge(rot_h, 2 * (u - 1))
                        pool.wait_ge(rot_lb, u - 1)
                    pool.wait_ge(prods, 4 * u + 2)
                    pool.tensor_tensor(rot[:, u % 2, 0, :], prod[:, 0, :], prod[:, 1, :], ALU.subtract).then_inc(rotated, 1)
                    pool.wait_ge(prods, 4 * u + 4)
                    pool.tensor_tensor(rot[:, u % 2, 1, :], prod[:, 2, :], prod[:, 3, :], ALU.add).then_inc(rotated, 1)
                    pool.wait_ge(rot_h, 2 * u + 2)
                    pool.wait_ge(rotated, 2 * u + 2)
                    if u >= 2:
                        pool.wait_ge(u_out[u % 2], 16 * 4 * (u // 2))
                    pool.tensor_tensor(rl[:, u % 2, 1, :], rot[:, u % 2, 1, :], rh[:, u % 2, 1, :].bitcast(F32), ALU.subtract)\
                        .then_inc(rot_lb, 1)

            pre(0)
            for b in range(B):
                if b + 1 < B:
                    pre(b + 1)
                post(b)

        @block.vector
        def _(dve):
            tick = Tally(tick_s)

            dve.wait_ge(s_in, 16)
            dve.reciprocal(srec[:, :], sraw[:, :]).then_inc(srec_done, 1)

            def split(i):
                dve.wait_ge(w_in, 16 * (i + 1))
                dve.tensor_copy(wh[i][:, :, :], w[:, :, :]).then_inc(split_h, 1)
                dve.wait_ge(split_h, i + 1)
                dve.tensor_sub(wl[i][:, :, :], w[:, :, :], wh[i][:, :, :].bitcast(F32)).then_inc(split_l, 1)

            def pre(b):
                cols = slice(SB * b, SB * b + SB)
                if b >= 2:
                    dve.wait_ge(r_st[b % 2], 32 * (b // 2))
                for i in range(SB):
                    n = SB * b + i
                    dve.wait_ge(projected, SB * b + 2 * (i // 2) + 2)
                    dve.wait_ge(xb_done, n + 1)
                    dve.tensor_add(x1[:, b % 2, i, :], op[i // 2][:, D * (i % 2):D * (i % 2) + D], x[:, b % 2, i, :])\
                       .then_inc(x1_done, 1)
                    dve.wait_ge(x1_done, n + 1)
                    k = tick.add(dve.bn_stats(stats[:, n, :], x1[:, b % 2, i, :]))
                    dve.wait_ge(tick_s, k)
                    k = tick.add(dve.bn_aggr(mv[:, n, :], stats[:, n, :]))
                dve.wait_ge(tick_s, k)
                dve.tensor_scalar(r1[:, 0, cols], mv[:, cols, 1], EPS, None, ALU.add).then_inc(root_asked, 1)
                dve.wait_ge(root_asked, 2 * b + 1)
                inverse_root(dve, r1, cols, tick, rooted, 2 * b + 1)
                for i in range(SB):
                    n = SB * b + i
                    dve.tensor_scalar(xf[:, b % 2, i, :], x1[:, b % 2, i, :], mv[:, n, 0:1], r1[:, 3, n:n + 1],
                                      ALU.subtract, ALU.mult).then_inc(xf_done, 1)
                dve.wait_ge(squared, SB * (b + 1))
                dve.tensor_scalar(r2[:, 0, cols], ssum[:, cols], 1.0 / D, EPS, ALU.mult, ALU.add).then_inc(root_asked, 1)
                dve.wait_ge(root_asked, 2 * b + 2)
                inverse_root(dve, r2, cols, tick, rooted, 2 * b + 2)
                dve.wait_ge(small_in, 16 * 6)
                for i in range(SB):
                    n = SB * b + i
                    dve.scalar_tensor_tensor(out=xn[:, b % 2, i, :], in0=xf[:, b % 2, i, :], scalar=r2[:, 3, n:n + 1],
                                             in1=g1[:, :], op0=ALU.mult, op1=ALU.mult).then_inc(xn_done, 1)

            def post(b):
                for k in range(DC):
                    toks = slice(S * b, S * b + S)
                    dve.wait_ge(h_copied, DC * b + k + 1)
                    dve.tensor_sub(xlo[:, k, toks], tp[k][:, :], xh[:, k, toks].bitcast(F32)).then_inc(parts_done, 1)
                for u in range(UNITS * b, UNITS * b + UNITS):
                    g, is_k = u % UNITS // 2, u % 2
                    dve.wait_ge(unit_done, u + 1)
                    cos, sin = (c.cos, c.sin) if is_k else (c.cos_q, c.sin_q)
                    for n, (half, table) in enumerate(((0, cos), (1, sin), (0, sin), (1, cos))):
                        if u:
                            dve.wait_ge(rotated, 2 * (u - 1) + n // 2 + 1)
                        dve.scalar_tensor_tensor(out=prod[:, n, :], in0=ub[2 * (u % 2) + half][:, :],
                                                 scalar=bqk[:, is_k, 2 * g + half:2 * g + half + 1], in1=table[:, :],
                                                 op0=ALU.add, op1=ALU.mult).then_inc(prods, 1)
                    if u % UNITS:
                        low(u - 1)
                low(UNITS * b + UNITS - 1)
                for i in range(SB * b, SB * b + SB):
                    for half in range(2):
                        dve.wait_ge(v_mul, 2 * i + half + 1)
                        if i >= 2 and not half:
                            dve.wait_ge(v_out[i % 2], 16 * (i // 2))
                        dve.tensor_add(vout[:, i % 2, S * half:S * half + S], tp[half][:, :], bv[:, S * half:S * half + S])\
                           .then_inc(v_full, 1)

            def low(u):
                dve.wait_ge(rot_h, 2 * u + 1)
                if u >= 2:
                    dve.wait_ge(u_out[u % 2], 16 * 4 * (u // 2))
                dve.tensor_sub(rl[:, u % 2, 0, :], rot[:, u % 2, 0, :], rh[:, u % 2, 0, :].bitcast(F32)).then_inc(rot_la, 1)

            for i in range(3):
                split(i)
            pre(0)
            for b in range(B):
                if b + 1 < B:
                    pre(b + 1)
                post(b)

def mix(nc, c, t):
    a = Alloc(nc, "mx")
    with a.stack:
        CH = W2 // P
        RING = 4
        s_even, s_odd = a.sb("s_even", [2 * B * H // 2, S]), a.sb("s_odd", [2 * B * H // 2, S])
        oT, rT = a.sb("oT", [P, RING, S]), a.sb("rT", [P, RING, S])
        ow = a.sb("ow", [P, CH, D])
        ob, g2, sb2 = (a.sb(n, [P, D]) for n in ("ob", "g2", "sb2"))
        rb, sb1 = a.sb("rb", [P, E]), a.sb("sb1", [P, FF // P])
        rw = a.sb("rw", [P, DC, E])
        sw1, sw2 = a.sb("sw1", [P, DC, FF]), a.sb("sw2", [P, FF // P, D])
        ao, an = a.sb("ao", [P, 2, SB, D]), a.sb("an", [P, 2, SB, D])
        sq = a.sb("sq", [P, D])
        ssum, r2 = a.sb("ssum", [P, TILES]), a.sb("r2", [P, 4, TILES])
        anT = a.sb("anT", [P, DC, S])
        hid = a.sb("hid", [P, FF // P, S])
        op, tp, hp, yp = ([a.ps(f"{n}{i}") for i in range(2)] for n in ("op", "tp", "hp", "yp"))
        s_in, srec_done, r_out, small_in, x1_in = (a.sem(n) for n in ("s_in", "srec_done", "r_out", "small_in", "x1_in"))
        o_in = [a.sem(f"o_in{i}") for i in range(RING)]
        xn_in = [a.sem(f"xn_in{i}") for i in range(2)]
        an_out = [a.sem(f"an_out{i}") for i in range(2)]
        o_scaled, chunk_done, xb_done, ao_done, squared, root_asked, rooted, an_done = (a.sem(n) for n in (
            "o_scaled", "chunk_done", "xb_done", "ao_done", "squared", "root_asked", "rooted", "an_done"))
        t_done, t_copied, l_mul, l_done, h_mul, h_done, y_mul, y_done, base_step, tick_s = (a.sem(n) for n in (
            "t_done", "t_copied", "l_mul", "l_done", "h_mul", "h_done", "y_mul", "y_done", "base_step", "tick"))
        block = a.stack.enter_context(nc.Block())
        NSMALL = 9

        def flat(x):
            return x.rearrange("p i d -> p (i d)")

        @block.sync
        def _(sp):
            sp.dma_start(s_even[:, :], t["s2"][0].rearrange("h p n -> (h p) n")).then_inc(s_in, 16)
            sp.dma_start(s_odd[:, :], t["s2"][1].rearrange("h p n -> (h p) n")).then_inc(s_in, 16)
            sp.wait_ge(srec_done, 2)
            sp.dma_start(t["r2"].rearrange("h p n -> (h p) n"), s_even[:, :]).then_inc(r_out, 16)

            def batch(b):
                if b >= 2:
                    sp.wait_ge(base_step, 3 * (b - 1))
                sp.dma_start(ao[:, b % 2, :, :], t["xn"][SB * b:SB * b + SB].rearrange("s p d -> p s d")).then_inc(xn_in[b % 2], 16)
                for g in range(CH * b, CH * b + CH):
                    if g >= RING:
                        sp.wait_ge(chunk_done, g - RING + 1)
                    sp.dma_start(oT[:, g % RING, :], t["o2"][g]).then_inc(o_in[g % RING], 16)
                    if g == 0:
                        sp.wait_ge(r_out, 16)
                    for h in range(2):
                        sp.dma_start(rT[D2 * h:D2 * h + D2, g % RING, :], t["r2"][h, g:g + 1, :].to_broadcast([D2, S]))\
                          .then_inc(o_in[g % RING], 16)

            batch(0)
            for b in range(B):
                if b + 1 < B:
                    batch(b + 1)
                sp.wait_ge(an_done, SB * (b + 1))
                sp.dma_start(t["an"][P * SB * b:P * SB * (b + 1), :].rearrange("(s p) d -> p s d", p=P), an[:, b % 2, :, :])\
                  .then_inc(an_out[b % 2], 16)
            for i in range(2):
                sp.wait_ge(an_out[i], 16 * B // 2)

        @block.scalar
        def _(act):
            for dst, name, pat in ((ow, "L0_ffn_o_w", "(k p) n -> p k n"), (rw, "L0_ffn_router_w", "(k p) n -> p k n"),
                                   (sw1, "L0_ffn_sh_w1", "(k p) n -> p k n"), (sw2, "L0_ffn_sh_w2", "(k p) n -> p k n")):
                act.dma_start(dst[:, :, :], t[name].rearrange(pat, p=P)).then_inc(small_in, 16)
            for dst, name in ((ob, "L0_ffn_o_b"), (g2, "L0_ffn_gamma2"), (sb2, "L0_ffn_sh_b2"), (rb, "L0_ffn_router_b")):
                act.dma_start(dst[:, :], t[name].to_broadcast([P, dst.shape[1]])).then_inc(small_in, 16)
            act.dma_start(sb1[:, :], t["L0_ffn_sh_b1"]).then_inc(small_in, 16)
            act.dma_start(c.base[:, :, :], t["x1"].rearrange("s p d -> p s d")).then_inc(x1_in, 16)
            for m in range(FF // P):
                act.dma_start(c.w2[:, :, m, :], t["L0_ffn_re_w2"][:, P * m:P * m + P, :].rearrange("e p n -> p e n"))\
                   .then_inc(c.w2_in, 16)

            def pre(b):
                for i in range(SB):
                    n = SB * b + i
                    act.wait_ge(ao_done, 2 * b + i // 2 + 1)
                    if n:
                        act.wait_ge(squared, n)
                    act.activation(sq[:, :], ao[:, b % 2, i, :], ACT.Square, accum_out=ssum[:, n:n + 1]).then_inc(squared, 1)
                act.wait_ge(root_asked, b + 1)
                cols = slice(SB * b, SB * b + SB)
                act.activation(r2[:, 1, cols], r2[:, 0, cols], ACT.Sqrt).then_inc(rooted, 1)

            def post(b):
                for k in range(DC):
                    act.wait_ge(t_done, DC * b + k + 1)
                    if b:
                        act.wait_ge(h_mul, 2 * b)
                    act.activation(anT[:, k, :], tp[k][:, :], ACT.Copy).then_inc(t_copied, 1)
                for m in range(FF // P):
                    act.wait_ge(h_mul, 2 * b + m + 1)
                    if b:
                        act.wait_ge(y_mul, 2 * b)
                    act.activation(hid[:, m, :], hp[m][:, :], ACT.Gelu, bias=sb1[:, m:m + 1]).then_inc(h_done, 1)

            pre(0)
            for b in range(B):
                post(b)
                if b + 1 < B:
                    pre(b + 1)

        @block.tensor
        def _(pe):
            def outputs(b):
                if b:
                    pe.wait_ge(ao_done, 2 * b)
                for m in range(CH):
                    g = CH * b + m
                    pe.wait_ge(o_scaled, g + 1)
                    for i in range(SB):
                        mm = pe.matmul(op[i // 2][:, D * (i % 2):D * (i % 2) + D], oT[:, g % RING, P * i:P * i + P],
                                       ow[:, m, :], start=(m == 0 and i % 2 == 0), stop=(m == CH - 1 and i % 2 == 1))
                    mm.then_inc(chunk_done, 1)

            pe.wait_ge(small_in, 16 * NSMALL)
            outputs(0)
            for b in range(B):
                if b + 1 < B:
                    outputs(b + 1)
                pe.wait_ge(an_done, SB * (b + 1))
                if b:
                    pe.wait_ge(l_done, b)
                for k in range(DC):
                    for i in range(SB):
                        mm = pe.transpose(tp[k][:, P * i:P * i + P], an[:, b % 2, i, P * k:P * k + P], c.ident[:, :])
                    mm.then_inc(t_done, 1)
                pe.wait_ge(t_copied, DC * (b + 1))
                for i in range(SB):
                    for k in range(DC):
                        mm = pe.matmul(tp[0][:, 32 * i:32 * i + E], anT[:, k, P * i:P * i + P], rw[:, k, :],
                                       start=(k == 0), stop=(k == DC - 1))
                mm.then_inc(l_mul, 1)
                for m in range(FF // P):
                    if b:
                        pe.wait_ge(h_done, 2 * (b - 1) + m + 1)
                    for k in range(DC):
                        mm = pe.matmul(hp[m][:, :], sw1[:, k, P * m:P * m + P], anT[:, k, :],
                                       start=(k == 0), stop=(k == DC - 1))
                    mm.then_inc(h_mul, 1)
                pe.wait_ge(h_done, 2 * (b + 1))
                for j in range(2):
                    if b:
                        pe.wait_ge(y_done, 2 * (b - 1) + j + 1)
                    for i in (2 * j, 2 * j + 1):
                        for m in range(FF // P):
                            mm = pe.matmul(yp[j][:, D * (i % 2):D * (i % 2) + D], hid[:, m, P * i:P * i + P], sw2[:, m, :],
                                           start=(m == 0), stop=(m == FF // P - 1))
                    mm.then_inc(y_mul, 1)

        @block.gpsimd
        def _(pool):
            def bias(b):
                pool.wait_ge(xn_in[b % 2], 16 * (b // 2 + 1))
                for j in range(SB):
                    pool.tensor_tensor(ao[:, b % 2, j, :], ao[:, b % 2, j, :], ob[:, :], ALU.add).then_inc(xb_done, 1)

            def scale(b):
                for g in range(CH * b, CH * b + CH):
                    pool.wait_ge(o_in[g % RING], 48 * (g // RING + 1))
                    pool.tensor_tensor(oT[:, g % RING, :], oT[:, g % RING, :], rT[:, g % RING, :], ALU.mult).then_inc(o_scaled, 1)

            def base(b):
                tiles = c.base[:, SB * b:SB * b + SB, :]
                if b == 0:
                    pool.wait_ge(x1_in, 16)
                pool.tensor_tensor(tiles, tiles, sb2[:, :].rearrange("p (o d) -> p o d", o=1).to_broadcast([P, SB, D]), ALU.add)\
                    .then_inc(base_step, 1)
                pool.wait_ge(ao_done, 2 * (b + 1))
                pool.wait_ge(base_step, 3 * b + 1)
                pool.tensor_tensor(flat(tiles), flat(tiles), flat(ao[:, b % 2, :, :]), ALU.add).then_inc(base_step, 1)
                pool.wait_ge(an_done, SB * (b + 1))
                pool.wait_ge(base_step, 3 * b + 2)
                pool.tensor_tensor(flat(tiles), flat(tiles), flat(an[:, b % 2, :, :]), ALU.add).then_inc(base_step, 1)

            pool.wait_ge(small_in, 16 * NSMALL)
            bias(0)
            scale(0)
            for b in range(B):
                if b + 1 < B:
                    bias(b + 1)
                    scale(b + 1)
                base(b)

        @block.vector
        def _(dve):
            tick = Tally(tick_s)
            dve.wait_ge(s_in, 32)
            dve.tensor_add(s_even[:, :], s_even[:, :], s_odd[:, :]).then_inc(srec_done, 1)
            dve.wait_ge(srec_done, 1)
            dve.reciprocal(s_even[:, :], s_even[:, :]).then_inc(srec_done, 1)
            dve.wait_ge(small_in, 16 * NSMALL)

            def outputs(b):
                dve.wait_ge(chunk_done, CH * (b + 1))
                dve.wait_ge(xb_done, SB * (b + 1))
                for j in range(2):
                    tiles = flat(ao[:, b % 2, 2 * j:2 * j + 2, :])
                    dve.tensor_add(tiles, tiles, op[j][:, :]).then_inc(ao_done, 1)

            def norm(b):
                cols = slice(SB * b, SB * b + SB)
                dve.wait_ge(squared, SB * (b + 1))
                dve.tensor_scalar(r2[:, 0, cols], ssum[:, cols], 1.0 / D, EPS, ALU.mult, ALU.add).then_inc(root_asked, 1)
                dve.wait_ge(root_asked, b + 1)
                inverse_root(dve, r2, cols, tick, rooted, b + 1)
                if b >= 2:
                    dve.wait_ge(an_out[b % 2], 16 * (b // 2))
                    dve.wait_ge(base_step, 3 * (b - 1))
                for i in range(SB):
                    n = SB * b + i
                    dve.scalar_tensor_tensor(out=an[:, b % 2, i, :], in0=ao[:, b % 2, i, :], scalar=r2[:, 3, n:n + 1],
                                             in1=g2[:, :], op0=ALU.mult, op1=ALU.mult).then_inc(an_done, 1)

            outputs(0)
            norm(0)
            for b in range(B):
                if b + 1 < B:
                    outputs(b + 1)
                dve.wait_ge(l_mul, b + 1)
                dve.tensor_tensor(c.logits[:, SB * b:SB * b + SB, :],
                                  tp[0][:, 0:32 * SB].rearrange("p (i e) -> p i e", e=32)[:, :, 0:E],
                                  rb[:, :].rearrange("p (o e) -> p o e", o=1).to_broadcast([P, SB, E]), ALU.add).then_inc(l_done, 1)
                dve.wait_ge(base_step, 3 * (b + 1))
                for j in range(2):
                    tiles = flat(c.base[:, SB * b + 2 * j:SB * b + 2 * j + 2, :])
                    dve.wait_ge(y_mul, 2 * b + j + 1)
                    dve.tensor_add(tiles, tiles, yp[j][:, :]).then_inc(y_done, 1)
                if b + 1 < B:
                    norm(b + 1)



def route(nc, c, t):
    a = Alloc(nc, "rt")
    with a.stack:
        IX = NT + 2
        lg, ex, pos = (a.sb(n, [P, TILES, E]) for n in ("lg", "ex", "pos"))
        mx, tot, inv = (a.sb(n, [P, TILES]) for n in ("mx", "tot", "inv"))
        idx = a.sb("idx", [P, TILES, 8], U32)
        idxf = a.sb("idxf", [P, TILES, TOPK])
        oh, picked = a.sb("oh", [P, TOPK, TILES, E]), a.sb("picked", [P, TOPK, TILES, E])
        member = a.sb("member", [P, TILES, E], BF16)
        gate = a.sb("gate", [P, TILES, E])
        gateT = a.sb("gateT", [E, TOK])
        b2 = a.sb("b2", [E, D])
        counts = a.sb("counts", [P, E])
        over = a.sb("over", [P, E, TILES])
        nt, ct, start = (a.sb(n, [P, E]) for n in ("nt", "ct", "start"))
        tri = a.sb("tri", [P, E, E])
        spread = a.sb("spread", [P, E, E])
        slotf, rowf, tilef = (a.sb(n, [P, TOPK, TILES]) for n in ("slotf", "rowf", "tilef"))
        sloti, rowi, tilei = (a.sb(n, [P, TOPK, TILES], I32) for n in ("sloti", "rowi", "tilei"))
        e_no, j_no, t_no, row_no, p_no = (a.sb(n, s, I32) for n, s in (
            ("e_no", [P, E]), ("j_no", [P, TILES]), ("t_no", [P, TILES]), ("row_no", [P, P]), ("p_no", [P, 1])))
        e_nof, j_nof, t_nof, row_nof, p_nof = (a.sb(n + "f", s) for n, s in (
            ("e_no", [P, E]), ("j_no", [P, TILES]), ("t_no", [P, TILES]), ("row_no", [P, P]), ("p_no", [P, 1])))
        upper, ones = a.sb("upper", [P, P], BF16), a.sb("ones", [P, P], BF16)
        hot_row, hot_tile = a.sb("hot_row", [P, 4, P], F32R), a.sb("hot_tile", [P, 4, NT], F32R)
        of_tile, cmp = a.sb("of_tile", [P, 1]), a.sb("cmp", [P, E])
        rank_b, count_b, ids_b, row_b = (a.ps(n) for n in ("rank", "count", "ids", "row"))
        gt_b = [a.ps("gt0"), a.ps("gt1")]
        bb = [a.ps("bb0"), a.ps("bb1")]
        set_up, numbers, exped, tick_s, member_done, ranked, hot_r, hot_t, placed, b2_in = (a.sem(n) for n in (
            "set_up", "numbers", "exped", "tick", "member_done", "ranked", "hot_r", "hot_t", "placed", "b2_in"))
        l_ready, tile_of, rowed, gate_ready, g_turned, g_copied, b_mul, b_added = (a.sem(n) for n in (
            "l_ready", "tile_of", "rowed", "gate_ready", "g_turned", "g_copied", "b_mul", "b_added"))
        slots_known = a.sem("slots_known")
        block = a.stack.enter_context(nc.Block())
        STEPS = TOPK * TILES

        def over_tiles(x, n=TILES):
            return x.rearrange("p (o e) -> p o e", o=1).to_broadcast([P, n, E])

        def over_experts(x):
            return x.rearrange("p (i o) -> p i o", o=1).to_broadcast([P, TILES, E])

        @block.sync
        def _(sp):
            sp.dma_start(b2[:, :], t["L0_ffn_re_b2"]).then_inc(b2_in, 16)

        @block.gpsimd
        def _(pool):
            pool.iota(e_no[:, :], pattern=[[1, E]], base=0, channel_multiplier=0).then_inc(set_up, 1)
            pool.iota(j_no[:, :], pattern=[[P, TILES]], base=0, channel_multiplier=0).then_inc(set_up, 1)
            pool.iota(t_no[:, :], pattern=[[P, TILES]], base=0, channel_multiplier=1).then_inc(set_up, 1)
            pool.iota(row_no[:, :], pattern=[[1, P]], base=0, channel_multiplier=0).then_inc(set_up, 1)
            pool.iota(p_no[:, :], pattern=[[0, 1]], base=0, channel_multiplier=1).then_inc(set_up, 1)
            for m in (upper[:, :], tri[:, :, :], ones[:, :]):
                pool.wait_ge(set_up, 5)
                pool.memset(m, 1.0).then_inc(set_up, 1)
            pool.wait_ge(set_up, 8)
            pool.affine_select(out=upper[:, :], in_=upper[:, :], compare_op=ALU.is_gt, fill=0.0, base=0,
                               pattern=[[1, P]], channel_multiplier=-1).then_inc(set_up, 1)
            pool.affine_select(out=tri[:, :, :], in_=tri[:, :, :], compare_op=ALU.is_ge, fill=0.0, base=0,
                               pattern=[[1, E], [-1, E]], channel_multiplier=0).then_inc(set_up, 1)
            pool.wait_ge(placed, 1)
            pool.wait_ge(numbers, 5)
            for n in range(STEPS):
                k, i = n // TILES, n % TILES
                if n >= 4:
                    pool.wait_ge(ranked, n - 1)
                pool.tensor_scalar(hot_tile[:, n % 4, :], row_nof[:, 0:NT], tilef[:, k, i:i + 1], t_nof[:, i:i + 1],
                                   ALU.is_equal, ALU.mult).then_inc(hot_t, 1)

        @block.scalar
        def _(act):
            act.wait_ge(l_ready, 1)
            act.activation(ex[:, :, :], lg[:, :, :], ACT.Exp).then_inc(exped, 1)
            for b in range(B):
                act.wait_ge(g_turned, b + 1)
                act.activation(gateT[:, S * b:S * b + S], gt_b[b % 2][0:E, :], ACT.Copy).then_inc(g_copied, 1)

        @block.tensor
        def _(pe):
            pe.wait_ge(set_up, 10)
            pe.wait_ge(member_done, 1)
            pe.matmul(rank_b[:, 0:TILES * E], upper[:, :], member[:, :, :], start=True, stop=False)
            for i in range(TILES - 1):
                mm = pe.matmul(rank_b[:, E * (i + 1):E * TILES], ones[:, :], over_tiles(member[:, i, :], TILES - 1 - i),
                               start=False, stop=(i == TILES - 2))
            for i in range(TILES):
                mm = pe.matmul(count_b[:, 0:E], ones[:, :], member[:, i, :], start=(i == 0), stop=(i == TILES - 1))
            mm.then_inc(ranked, 1)
            pe.wait_ge(gate_ready, 1)
            for b in range(B):
                if b >= 2:
                    pe.wait_ge(g_copied, b - 1)
                for i in range(SB):
                    mm = pe.transpose(gt_b[b % 2][0:E, P * i:P * i + P], gate[:, SB * b + i, :], c.ident[:, :])
                mm.then_inc(g_turned, 1)
            pe.wait_ge(tile_of, 1)
            pe.matmul(row_b[0:1, 0:P], of_tile[:, :], c.ident[:, :], start=True, stop=True).then_inc(rowed, 1)
            for n in range(STEPS):
                pe.wait_ge(hot_r, n + 1)
                pe.wait_ge(hot_t, n + 1)
                pe.matmul(ids_b[:, 0:NT], hot_row[:, n % 4, :], hot_tile[:, n % 4, :], start=(n == 0),
                          stop=(n == STEPS - 1)).then_inc(ranked, 1)
            pe.wait_ge(b2_in, 16)
            for j in range(TILES // 2):
                pe.wait_ge(g_copied, j // 2 + 1)
                if j >= 2:
                    pe.wait_ge(b_added, j - 1)
                for i in (2 * j, 2 * j + 1):
                    mm = pe.matmul(bb[j % 2][:, D * (i % 2):D * (i % 2) + D], gateT[:, P * i:P * i + P], b2[:, :],
                                   start=True, stop=True)
                mm.then_inc(b_mul, 1)

        @block.vector
        def _(dve):
            tick = Tally(tick_s)

            def then(instruction):
                dve.wait_ge(tick_s, tick.add(instruction))

            then(dve.tensor_reduce(mx[:, :], c.logits[:, :, :], AX.X, ALU.max))
            dve.tensor_tensor(lg[:, :, :], c.logits[:, :, :], over_experts(mx[:, :]), ALU.subtract).then_inc(l_ready, 1)
            dve.wait_ge(set_up, 10)
            for dst, src in ((e_nof, e_no), (j_nof, j_no), (t_nof, t_no), (row_nof, row_no), (p_nof, p_no)):
                dve.tensor_copy(dst[:, :], src[:, :]).then_inc(numbers, 1)
            dve.wait_ge(exped, 1)
            then(dve.tensor_reduce(tot[:, :], ex[:, :, :], AX.X, ALU.add))
            then(dve.reciprocal(inv[:, :], tot[:, :]))
            then(dve.tensor_tensor(ex[:, :, :], ex[:, :, :], over_experts(inv[:, :]), ALU.mult))
            for i in range(TILES):
                k = tick.add(dve.max(c.gates[:, i, :], ex[:, i, :]))
            dve.wait_ge(tick_s, k)
            for i in range(TILES):
                k = tick.add(dve.max_index(idx[:, i, :], c.gates[:, i, :], ex[:, i, :]))
            dve.wait_ge(tick_s, k)
            then(dve.tensor_copy(idxf[:, :, :], idx[:, :, 0:TOPK]))
            dve.wait_ge(numbers, 5)
            for k in range(TOPK):
                n = tick.add(dve.tensor_tensor(oh[:, k, :, :], over_tiles(e_nof[:, :]), over_experts(idxf[:, :, k]), ALU.is_equal))
            dve.wait_ge(tick_s, n)
            then(dve.tensor_add(member[:, :, :], oh[:, 0, :, :], oh[:, 1, :, :]))
            dve.tensor_add(member[:, :, :], member[:, :, :], oh[:, 2, :, :]).then_inc(member_done, 1)
            for k in range(TOPK):
                n = tick.add(dve.tensor_tensor(picked[:, k, :, :], oh[:, k, :, :], over_experts(c.gates[:, :, k]), ALU.mult))
            dve.wait_ge(tick_s, n)
            then(dve.tensor_add(gate[:, :, :], picked[:, 0, :, :], picked[:, 1, :, :]))
            then(dve.tensor_add(gate[:, :, :], gate[:, :, :], picked[:, 2, :, :]))
            dve.nop(nofuse=True).then_inc(gate_ready, 1)
            dve.wait_ge(ranked, 1)
            then(dve.tensor_copy(counts[:, :], count_b[:, 0:E]))
            then(dve.tensor_tensor(over[:, :, :], counts[:, :].rearrange("p (e o) -> p e o", o=1).to_broadcast([P, E, TILES]),
                                   j_nof[:, :].rearrange("p (o j) -> p o j", o=1).to_broadcast([P, E, TILES]), ALU.is_gt))
            then(dve.tensor_reduce(nt[:, :], over[:, :, :], AX.X, ALU.add))
            then(dve.tensor_tensor(spread[:, :, :], tri[:, :, :], over_tiles(nt[:, :], E), ALU.mult))
            then(dve.tensor_reduce(ct[:, :], spread[:, :, :], AX.X, ALU.add))
            then(dve.tensor_scalar(cmp[:, :], ct[:, :], p_nof[:, 0:1], None, ALU.is_le))
            then(dve.tensor_reduce(of_tile[:, :], cmp[:, :], AX.X, ALU.add))
            dve.tensor_scalar(of_tile[:, :], of_tile[:, :], float(E - 1), None, ALU.min).then_inc(tile_of, 1)
            then(dve.tensor_sub(start[:, :], ct[:, :], nt[:, :]))
            then(dve.tensor_scalar(start[:, :], start[:, :], float(P), None, ALU.mult))
            then(dve.tensor_tensor(pos[:, :, :], rank_b[:, 0:TILES * E].rearrange("p (i e) -> p i e", e=E),
                                   over_tiles(start[:, :]), ALU.add))
            for k in range(TOPK):
                n = tick.add(dve.tensor_tensor(picked[:, k, :, :], oh[:, k, :, :], pos[:, :, :], ALU.mult))
            dve.wait_ge(tick_s, n)
            then(dve.tensor_reduce(slotf[:, :, :], picked[:, :, :, :], AX.X, ALU.add))
            then(dve.tensor_copy(sloti[:, :, :], slotf[:, :, :]))
            k = tick.add(dve.tensor_scalar(rowi[:, :, :], sloti[:, :, :], P - 1, None, ALU.bitwise_and))
            then(dve.tensor_scalar(tilei[:, :, :], sloti[:, :, :], 7, None, ALU.logical_shift_right))
            k = tick.add(dve.tensor_copy(rowf[:, :, :], rowi[:, :, :]))
            then(dve.tensor_copy(tilef[:, :, :], tilei[:, :, :]))
            then(dve.scalar_tensor_tensor(out=slotf[:, :, :], in0=rowf[:, :, :], scalar=float(NT), in1=tilef[:, :, :],
                                          op0=ALU.mult, op1=ALU.add))
            dve.tensor_copy(c.slots[:, :, :], slotf[:, :, :]).then_inc(placed, 1)
            dve.wait_ge(placed, 1)
            for n in range(STEPS):
                k, i = n // TILES, n % TILES
                if n >= 4:
                    dve.wait_ge(ranked, n - 2)
                dve.tensor_scalar(hot_row[:, n % 4, :], row_nof[:, :], rowf[:, k, i:i + 1], None, ALU.is_equal).then_inc(hot_r, 1)
            dve.wait_ge(rowed, 1)
            dve.tensor_copy(c.experts[:, :], row_b[0:1, 0:P]).then_inc(slots_known, 1)
            dve.wait_ge(ranked, STEPS + 1)
            dve.tensor_copy(c.ids[:, :], ids_b[:, 0:NT]).then_inc(slots_known, 1)
            for j in range(TILES // 2):
                dve.wait_ge(b_mul, j + 1)
                tiles = c.base[:, 2 * j:2 * j + 2, :].rearrange("p i d -> p (i d)")
                dve.tensor_add(tiles, tiles, bb[j % 2][:, :]).then_inc(b_added, 1)
            dve.wait_ge(b_added, TILES // 2)


def experts(nc, c, t):
    a = Alloc(nc, "ex")
    with a.stack:
        MC = FF // P
        PASSES = NT // 4
        PEELED = 2
        idc = a.sb("idc", [P, 4], I32)
        xg = a.sb("xg", [P, 4, D])
        w1 = a.sb("w1", [P, 2, DC * FF + MC])
        xT, hid = a.sb("xT", [P, 2, DC, P]), a.sb("hid", [P, 2, MC, P])
        y = a.sb("y", [P, 4, D])
        tb, hb, yb = ([a.ps(f"{n}{i}") for i in range(2)] for n in ("tb", "hb", "yb"))
        gathered = [a.sem(f"gathered{i}") for i in range(4)]
        stored = [a.sem(f"stored{i}") for i in range(4)]
        id_set, turned, x_copied, w_copied, h_mul, h_done, y_mul, y_copied = (a.sem(n) for n in (
            "id_set", "turned", "x_copied", "w_copied", "h_mul", "h_done", "y_mul", "y_copied"))
        block = a.stack.enter_context(nc.Block())

        def ge(eng, sem, it, per_pass, const):
            if not isinstance(it, int):
                assert PEELED * per_pass + const > 0
                eng.wait_ge(sem, per_pass * it + const)
            elif per_pass * it + const > 0:
                eng.wait_ge(sem, per_pass * it + const)

        def steps(eng, step, last):
            for s in range(4 * PEELED):
                step(s // 4, s % 4)
            with eng.Fori(PEELED, PASSES) as it:
                for r in range(4):
                    step(it, r)
            for r in range(last + 1 - 4 * PASSES):
                step(PASSES, r)

        def there(it, r):
            return not isinstance(it, int) or 0 <= 4 * it + r < NT

        ye = t["ye"].rearrange("(p n) d -> n p d", n=NT)

        @block.gpsimd
        def _(pool):
            def step(it, r):
                sl = r % 4
                ge(pool, turned, it, 4, r - 3)
                pool.tensor_copy(idc[:, sl:sl + 1], c.ids[:, bass.ds(4 * it + r, 1)]).then_inc(id_set, 1)
                ge(pool, id_set, it, 4, r + 1)
                pool.nop(nofuse=True)
                pool.indirect_dma_start(out=xg[:, sl, :], out_offset=None, in_=t["an"],
                                        in_offset=bass.IndirectOffsetOnAxis(ap=idc[:, sl:sl + 1], axis=0)).then_inc(gathered[sl], 16)

            steps(pool, step, NT - 1)

        @block.sync
        def _(sp):
            def step(it, r):
                ge(sp, y_copied, it, 4, r + 1)
                sp.dma_start(ye[4 * it + r], y[:, r % 4, :]).then_inc(stored[r % 4], 16)

            steps(sp, step, NT - 1)
            for i in range(4):
                sp.wait_ge(stored[i], 16 * ((NT - 1 - i) // 4 + 1))

        @block.tensor
        def _(pe):
            def step(it, r):
                if there(it, r):
                    sl = r % 4
                    ge(pe, gathered[sl], it, 16, 16)
                    ge(pe, x_copied, it, 4, r - 1)
                    for k in range(DC):
                        mm = pe.transpose(tb[r % 2][:, P * k:P * k + P], xg[:, sl, P * k:P * k + P], c.ident[:, :])
                    mm.then_inc(turned, 1)
                if there(it, r - 1):
                    n = r - 1
                    ge(pe, x_copied, it, 4, n + 1)
                    ge(pe, w_copied, it, 4, n + 1)
                    ge(pe, h_done, it, 4, n - 1)
                    for m in range(MC):
                        for k in range(DC):
                            mm = pe.matmul(hb[n % 2][:, P * m:P * m + P], w1[:, n % 2, FF * k + P * m:FF * k + P * m + P],
                                           xT[:, n % 2, k, :], start=(k == 0), stop=(k == DC - 1))
                    mm.then_inc(h_mul, 1)
                if there(it, r - 2):
                    n = r - 2
                    e = pe.value_load(c.experts[0:1, bass.ds(4 * it + n, 1)], min_val=0, max_val=E - 1)
                    ge(pe, h_done, it, 4, n + 1)
                    ge(pe, y_copied, it, 4, n - 1)
                    for m in range(MC):
                        mm = pe.matmul(yb[n % 2][:, 0:D], hid[:, n % 2, m, :], c.w2[:, bass.ds(e, 1), m, :],
                                       start=(m == 0), stop=(m == MC - 1))
                    mm.then_inc(y_mul, 1)

            pe.wait_ge(c.w2_in, 16 * MC)
            steps(pe, step, NT + 1)

        @block.scalar
        def _(act):
            def step(it, r):
                if there(it, r - 1):
                    n = r - 1
                    ge(act, h_mul, it, 4, n + 1)
                    ge(act, y_mul, it, 4, n - 1)
                    for m in range(MC):
                        mm = act.activation(hid[:, n % 2, m, :], hb[n % 2][:, P * m:P * m + P], ACT.Gelu,
                                            bias=w1[:, n % 2, DC * FF + m:DC * FF + m + 1])
                    mm.then_inc(h_done, 1)
                if there(it, r - 2):
                    n = r - 2
                    ge(act, y_mul, it, 4, n + 1)
                    ge(act, stored[n % 4], it, 16, 16 * (n // 4))
                    act.activation(y[:, n % 4, :], yb[n % 2][:, 0:D], ACT.Copy).then_inc(y_copied, 1)

            steps(act, step, NT + 1)

        @block.vector
        def _(dve):
            def step(it, r):
                e = dve.value_load(c.experts[0:1, bass.ds(4 * it + r, 1)], min_val=0, max_val=E - 1)
                ge(dve, h_done, it, 4, r - 1)
                dve.tensor_copy(w1[:, r % 2, :], c.w1[:, bass.ds(e, 1), :].rearrange("p o n -> p (o n)")).then_inc(w_copied, 1)
                ge(dve, turned, it, 4, r + 1)
                dve.tensor_copy(xT[:, r % 2, :, :].rearrange("p k n -> p (k n)"), tb[r % 2][:, 0:DC * P]).then_inc(x_copied, 1)

            dve.wait_ge(c.w1_in, 16 * (DC + 1))
            steps(dve, step, NT - 1)


def combine(nc, c, t, out):
    a = Alloc(nc, "cb")
    with a.stack:
        RING = 4
        y = a.sb("y", [P, RING, TOPK, D])
        gathered = [a.sem(f"gathered{i}") for i in range(RING)]
        summed, out_s = a.sem("summed"), a.sem("out")
        block = a.stack.enter_context(nc.Block())

        @block.gpsimd
        def _(pool):
            for i in range(TILES):
                if i >= RING:
                    pool.wait_ge(summed, TOPK * (i - RING + 1))
                for k in range(TOPK):
                    pool.indirect_dma_start(out=y[:, i % RING, k, :], out_offset=None, in_=t["ye"],
                                            in_offset=bass.IndirectOffsetOnAxis(ap=c.slots[:, k, i:i + 1], axis=0))\
                        .then_inc(gathered[i % RING], 16)

        @block.vector
        def _(dve):
            for i in range(TILES):
                dve.wait_ge(gathered[i % RING], 16 * TOPK * (i // RING + 1))
                for k in range(TOPK):
                    if k:
                        dve.wait_ge(summed, TOPK * i + k)
                    dve.scalar_tensor_tensor(out=c.base[:, i, :], in0=y[:, i % RING, k, :], scalar=c.gates[:, i, k:k + 1],
                                             in1=c.base[:, i, :], op0=ALU.mult, op1=ALU.add).then_inc(summed, 1)

        @block.sync
        def _(sp):
            for i in range(TILES):
                sp.wait_ge(summed, TOPK * (i + 1))
                sp.dma_start(out[i // SB, P * (i % SB):P * (i % SB) + P, :], c.base[:, i, :]).then_inc(out_s, 16)
            sp.wait_ge(out_s, 16 * TILES)





NAMES = ["x", "ctx_1024", "L0_xattn_wq", "L0_xattn_bq", "L0_xattn_wk", "L0_xattn_bk", "L0_xattn_wv",
         "L0_xattn_bv", "L0_xattn_wo", "L0_xattn_bo", "L0_ffn_theta", "L0_ffn_gamma1", "L0_ffn_gamma2",
         "L0_ffn_q_w", "L0_ffn_q_b", "L0_ffn_k_w", "L0_ffn_k_b", "L0_ffn_v_w", "L0_ffn_v_b", "L0_ffn_o_w",
         "L0_ffn_o_b", "L0_ffn_router_w", "L0_ffn_router_b", "L0_ffn_sh_w1", "L0_ffn_sh_b1", "L0_ffn_sh_w2",
         "L0_ffn_sh_b2", "L0_ffn_re_w1", "L0_ffn_re_b1", "L0_ffn_re_w2", "L0_ffn_re_b2"]


def program(nc, t, out):
    def scratch(name, shape, dt=F32):
        t[name] = nc.dram_tensor(name, shape, dt).ap()

    scratch("qs1", (B * H, SP1, S))
    scratch("ks1", (B * H, SP1, S))
    scratch("vs1", (QUADS, S, 4 * D1))
    scratch("o1", (QUADS, 4, D1, S))
    scratch("qs2", (B * H, 2 * D2, S))
    scratch("ks2", (B * H, 2 * D2, S))
    scratch("vs2", (QUADS, S, 4 * D2))
    scratch("o2", (B * H // 2, 2 * D2, S))
    scratch("s1", (QUADS, 4, S))
    scratch("s2", (2, 2, B * H // 2, S))
    scratch("r2", (2, B * H // 2, S))
    scratch("an", (TOK, D))
    scratch("ye", (P * NT, D))
    scratch("r1", (QUADS, 4, S))
    scratch("x1", (TILES, P, D))
    scratch("xn", (TILES, P, D))
    c = Alloc(nc, "keep")
    c.keep = c
    with c.stack:
        c.w1_in, c.w2_in = c.sem("w1_in"), c.sem("w2_in")
        make_identities(nc, c)
        rope = Alloc(nc, "rope")
        with rope.stack:
            make_tables(nc, c, rope, t)
            project1(nc, c, t)
            attention(nc, c, t, False)
            project2(nc, c, t)
        c.w1 = c.sb("w1", [P, E, DC * FF + FF // P])
        attention(nc, c, t, True)
        c.w2 = c.sb("w2", [P, E, FF // P, D])
        c.base = c.sb("base", [P, TILES, D])
        c.logits = c.sb("logits", [P, TILES, E])
        mix(nc, c, t)
        c.gates = c.sb("gates", [P, TILES, 8])
        c.slots = c.sb("slots", [P, TOPK, TILES], I32)
        c.ids = c.sb("ids", [P, NT], I32)
        c.experts = c.sb("experts", [1, P], I32)
        route(nc, c, t)
        experts(nc, c, t)
        combine(nc, c, t, out)


def kernel(**inputs):
    import concourse.bacc as bacc
    from concourse.bass_utils import run_bass_kernel_spmd

    x = {n: np.asarray(inputs[n]) for n in NAMES}
    for n in ("L0_xattn_bq", "L0_xattn_bk"):
        x[n] = x[n].reshape(DC, P).T
    for n in ("L0_ffn_q_w", "L0_ffn_k_w", "L0_ffn_q_b", "L0_ffn_k_b"):
        w = x[n].reshape(-1, 4, 4, D2 // 2, 2)
        x[n] = np.moveaxis(w, 4, 2).reshape(x[n].shape)
    for n in ("L0_ffn_q_b", "L0_ffn_k_b"):
        x[n] = x[n].reshape(W2 // P, P).T
    x["L0_ffn_sh_b1"] = x["L0_ffn_sh_b1"].reshape(FF // P, P).T
    x["L0_ffn_re_b1"] = np.moveaxis(x["L0_ffn_re_b1"].reshape(E, FF // P, P), 2, 0)
    x["L0_ffn_theta"] = x["L0_ffn_theta"].reshape(-1, 1)
    x = {n: v.reshape(1, -1) if v.ndim == 1 else v for n, v in x.items()}
    nc = bacc.Bacc("TRN2", target_bir_lowering=False, num_devices=1)
    arrays, t = {}, {}
    for n in NAMES:
        arrays[f"in_{n}"] = v = np.ascontiguousarray(x[n])
        t[n] = nc.dram_tensor(f"in_{n}", v.shape, mybir.dt.from_np(v.dtype), kind="ExternalInput").ap()
    out = nc.dram_tensor("out", (B, S, D), F32, kind="ExternalOutput").ap()
    program(nc, t, out)
    r = run_bass_kernel_spmd(nc, [arrays], core_ids=[0])
    return r.results[0]["out"]
```

```python
from contextlib import ExitStack

import numpy as np

import concourse.bass as bass
from concourse import mybir
from concourse.alu_op_type import AluOpType as ALU

F32 = mybir.dt.float32
F32R = mybir.dt.float32r
BF16 = mybir.dt.bfloat16
I32 = mybir.dt.int32
U32 = mybir.dt.uint32
ACT = mybir.ActivationFunctionType
AX = mybir.AxisListType

P = 128
B, S, D = 4, 512, 256
TOK = B * S
TILES = TOK // P
SB = S // P
DC = D // P
H = 16
D1 = D // H
D2 = 64
W2 = H * D2
QUADS = B * H // 4
E = 31
TOPK = 3
FF = 256
NT = (TOK * TOPK + E * (P - 1)) // P
EPS = 1e-5
MASKED = -1e30
TWO_PI = 2 * np.pi
TWO_PI_1 = 6.28125
TWO_PI_2 = float(np.round((TWO_PI - TWO_PI_1) * 2 ** 20) / 2 ** 20)
TWO_PI_3 = TWO_PI - TWO_PI_1 - TWO_PI_2
PI_BELOW = 3.1415925
ROUNDER = 1.5 * 2 ** 23
SP1 = 3 * D1
KCOL = [0, 512, 1024, 896]
KLEN = [S - P * kb for kb in range(SB)]
PCOLS = sum(KLEN)


class Alloc:

    def __init__(self, nc, tag):
        self.nc, self.tag, self.stack, self.sems = nc, tag, ExitStack(), []
        self.stack.callback(self.clear)

    def clear(self):
        if self.sems:
            self.nc.clear_and_free_semaphores(self.sems)
            self.nc.all_engine_barrier()

    def sb(self, name, shape, dt=F32):
        return self.stack.enter_context(self.nc.sbuf_tensor(f"{self.tag}_{name}", shape, dt))

    def ps(self, name, cols=512):
        return self.stack.enter_context(self.nc.psum_tensor(f"{self.tag}_{name}", [P, cols], F32))

    def sem(self, name):
        self.sems.append(self.nc.alloc_semaphore(f"{self.tag}_{name}"))
        return self.sems[-1]


def make_identities(nc, c):
    a = Alloc(nc, "const")
    c.ident = c.sb("ident", [P, P])
    c.ident_r = c.sb("ident_r", [P, P], F32R)
    c.ident_b = c.sb("ident_b", [P, P], BF16)
    c.mask_kq = c.sb("mask_kq", [P, P], BF16)
    c.mask_qk = c.sb("mask_qk", [P, S])
    with a.stack:
        filled, shaped, turned = a.sem("filled"), a.sem("shaped"), a.sem("turned")
        block = a.stack.enter_context(nc.Block())

        @block.gpsimd
        def _(pool):
            pool.memset(c.ident[:, :], 0.0).then_inc(filled, 1)
            pool.memset(c.ident_b[:, :], 0.0).then_inc(filled, 1)
            pool.memset(c.mask_kq[:, :], 0.0).then_inc(filled, 1)
            pool.memset(c.mask_qk[:, :], 0.0).then_inc(filled, 1)
            pool.wait_ge(filled, 4)
            for m in (c.ident, c.ident_b):
                pool.affine_select(out=m[:, :], in_=m[:, :], compare_op=ALU.not_equal, fill=1.0, base=0,
                                   pattern=[[-1, P]], channel_multiplier=1).then_inc(shaped, 1)
            pool.affine_select(out=c.mask_kq[:, :], in_=c.mask_kq[:, :], compare_op=ALU.is_ge, fill=MASKED,
                               base=0, pattern=[[1, P]], channel_multiplier=-1).then_inc(shaped, 1)
            pool.affine_select(out=c.mask_qk[:, S - P:S], in_=c.mask_qk[:, S - P:S], compare_op=ALU.is_ge,
                               fill=MASKED, base=0, pattern=[[-1, P]], channel_multiplier=1).then_inc(shaped, 1)

        @block.vector
        def _(dve):
            dve.wait_ge(shaped, 1)
            dve.tensor_scalar(c.ident_r[:, :], c.ident[:, :], -1.0, None, ALU.mult).then_inc(turned, 1)
            dve.wait_ge(turned, 1)
            dve.wait_ge(shaped, 4)


def make_tables(nc, c, rope, t):
    a = Alloc(nc, "table")
    c.cos, c.sin, c.cos_q, c.sin_q = (rope.sb(n, [P, S]) for n in ("cos", "sin", "cos_q", "sin_q"))
    with a.stack:
        counted, turned = a.sem("counted"), a.sem("turned")
        theta_in, reduced, sine, scaled_done = (a.sem(n) for n in ("theta_in", "reduced", "sine", "scaled_done"))
        theta, angle, whole, turn = a.sb("theta", [P, 1]), a.sb("angle", [P, S]), a.sb("whole", [P, S]), a.sb("turn", [P, 2, S])
        count = a.sb("count", [P, S], I32)
        block = a.stack.enter_context(nc.Block())

        @block.gpsimd
        def _(pool):
            pool.iota(count[:, :], pattern=[[1, S]], base=0, channel_multiplier=0).then_inc(counted, 1)

        @block.sync
        def _(sp):
            for h in range(4):
                sp.dma_start(theta[32 * h:32 * h + 32, :], t["L0_ffn_theta"]).then_inc(theta_in, 16)

        @block.scalar
        def _(act):
            for n, (table, scaled) in enumerate(((c.sin, c.sin_q), (c.cos, c.cos_q))):
                act.wait_ge(reduced, n + 1)
                act.activation(table[:, :], turn[:, n, :], ACT.Sin).then_inc(sine, 1)
                act.wait_ge(sine, n + 1)
                act.activation(scaled[:, :], table[:, :], ACT.Copy, scale=D2 ** -0.5).then_inc(scaled_done, 1)

        @block.vector
        def _(dve):
            dve.wait_ge(counted, 1)
            dve.tensor_copy(angle[:, :], count[:, :]).then_inc(turned, 1)
            dve.wait_ge(theta_in, 64)
            dve.wait_ge(turned, 1)
            dve.tensor_scalar(angle[:, :], angle[:, :], theta[:, 0:1], None, ALU.mult).then_inc(turned, 1)
            dve.wait_ge(turned, 2)
            n = 2
            for i, quarter in enumerate((0.0, 0.25)):
                tr = turn[:, i, :]
                steps = [lambda: dve.tensor_scalar(whole[:, :], angle[:, :], 1.0 / TWO_PI, quarter, ALU.mult, ALU.add),
                         lambda: dve.tensor_scalar(whole[:, :], whole[:, :], ROUNDER, None, ALU.add),
                         lambda: dve.tensor_scalar(whole[:, :], whole[:, :], -ROUNDER, None, ALU.add),
                         lambda: dve.scalar_tensor_tensor(out=tr, in0=whole[:, :], scalar=-TWO_PI_1, in1=angle[:, :],
                                                          op0=ALU.mult, op1=ALU.add),
                         lambda: dve.scalar_tensor_tensor(out=tr, in0=whole[:, :], scalar=-TWO_PI_2, in1=tr,
                                                          op0=ALU.mult, op1=ALU.add),
                         lambda: dve.scalar_tensor_tensor(out=tr, in0=whole[:, :], scalar=-TWO_PI_3, in1=tr,
                                                          op0=ALU.mult, op1=ALU.add),
                         lambda: dve.tensor_scalar(tr, tr, TWO_PI * quarter, PI_BELOW, ALU.add, ALU.min)]
                for s in steps:
                    s().then_inc(turned, 1)
                    n += 1
                    dve.wait_ge(turned, n)
                dve.tensor_scalar(tr, tr, -PI_BELOW, None, ALU.max).then_inc(reduced, 1)
            dve.wait_ge(scaled_done, 2)


def project1(nc, c, t):
    a = Alloc(nc, "p1")
    with a.stack:
        x, ctx_in, xl = (a.sb(n, [P, TILES, D]) for n in ("x", "ctx", "xl"))
        xT, cT = (a.sb(n, [P, DC, TOK]) for n in ("xT", "cT"))
        wq, wk, wv = (a.sb(n, [P, DC, D]) for n in ("wq", "wk", "wv"))
        bq, bq4, bk = (a.sb(n, [P, DC]) for n in ("bq", "bq4", "bk"))
        bv = a.sb("bv", [P, D])
        stats, mv, rstd = a.sb("stats", [P, TILES, 6]), a.sb("mv", [P, TILES, 2]), a.sb("rstd", [P, 3, TILES])
        full = a.sb("full", [P, 4, S])
        high, low = a.sb("high", [P, 4, S], F32R), a.sb("low", [P, 4, S], F32R)
        vout = a.sb("vout", [P, 4, 2, D])
        tb = [a.ps(f"tb{i}") for i in range(4)]
        qb = [a.ps(f"qb{i}") for i in range(2)]
        vb = [a.ps(f"vb{i}") for i in range(2)]
        x_in = [a.sem(f"x_in{b}") for b in range(B)]
        c_in = [a.sem(f"c_in{b}") for b in range(B)]
        w_in, stat_done, norm_step, xl_ready = a.sem("w_in"), a.sem("stat_done"), a.sem("norm_step"), a.sem("xl_ready")
        sq_done, c_turned, x_turned, c_copied, x_copied = (a.sem(n) for n in (
            "sq_done", "c_turned", "x_turned", "c_copied", "x_copied"))
        qk_mul, qk_full, split, v_mul, v_full = (a.sem(n) for n in ("qk_mul", "qk_full", "split", "v_mul", "v_full"))
        high_done = a.sem("high_done")
        bq_scaled = a.sem("bq_scaled")
        stack_out = [a.sem(f"stack_out{i}") for i in range(4)]
        v_out = [a.sem(f"v_out{i}") for i in range(4)]
        block = a.stack.enter_context(nc.Block())
        SCALE = D1 ** -0.5

        @block.sync
        def _(sp):
            xv = t["x"].rearrange("b (s p) d -> b p s d", p=P)
            cv = t["ctx_1024"].rearrange("b (s p) d -> b p s d", p=P)
            for b in range(B):
                sp.dma_start(ctx_in[:, SB * b:SB * b + SB, :], cv[b]).then_inc(c_in[b], 16)
                sp.dma_start(x[:, SB * b:SB * b + SB, :], xv[b]).then_inc(x_in[b], 16)
            for u in range(4 * B):
                b, is_q, m = u // 4, u % 4 >= 2, u % 2
                sp.wait_ge(split, u + 1)
                dst = (t["qs1"] if is_q else t["ks1"])[b * H + 8 * m:b * H + 8 * m + 8]
                parts = [(high, 0), (low, D1), (high, 2 * D1)] if is_q else [(high, 0), (high, D1), (low, 2 * D1)]
                for src, row in parts:
                    sp.dma_start(dst[:, row:row + D1, :], src[:, u % 4, :].bitcast(F32)).then_inc(stack_out[u % 4], 16)
                if not is_q:
                    n = 2 * b + m
                    sp.wait_ge(v_full, 2 * (n + 1))
                    for j in range(2):
                        tile = 2 * n + j
                        sp.dma_start(t["vs1"][SB * b:SB * b + SB, P * (tile % SB):P * (tile % SB) + P, :]
                                     .rearrange("g p d -> p g d"),
                                     vout[:, n % 4, j, :].rearrange("p (g d) -> p g d", g=4)).then_inc(v_out[n % 4], 16)
            for i in range(4):
                sp.wait_ge(stack_out[i], 16 * 3 * B)
                sp.wait_ge(v_out[i], 16 * 2 * 2 * B // 4)

        @block.scalar
        def _(act):
            for dst, name in ((wk, "L0_xattn_wk"), (wv, "L0_xattn_wv"), (wq, "L0_xattn_wq")):
                act.dma_start(dst[:, :, :], t[name].rearrange("(k p) n -> p k n", p=P)).then_inc(w_in, 16)
            for dst, name in ((bq, "L0_xattn_bq"), (bk, "L0_xattn_bk")):
                act.dma_start(dst[:, :], t[name]).then_inc(w_in, 16)
            act.dma_start(bv[:, :], t["L0_xattn_bv"].to_broadcast([P, D])).then_inc(w_in, 16)
            act.wait_ge(w_in, 16 * 6)
            act.activation(bq4[:, :], bq[:, :], ACT.Copy, scale=SCALE).then_inc(bq_scaled, 1)

            def turned_ctx(b):
                for k in range(DC):
                    n = DC * b + k
                    act.wait_ge(c_turned, n + 1)
                    act.activation(cT[:, k, S * b:S * b + S], tb[n % 2][:, :], ACT.Copy).then_inc(c_copied, 1)

            def unit(u):
                is_q, m = u % 4 >= 2, u % 2
                act.wait_ge(qk_mul, u + 1)
                if u >= 4:
                    act.wait_ge(split, u - 3)
                if u == 2:
                    act.wait_ge(bq_scaled, 1)
                act.activation(full[:, u % 4, :], qb[u % 2][:, :], ACT.Identity,
                               bias=(bq4 if is_q else bk)[:, m:m + 1], scale=SCALE if is_q else 1.0).then_inc(qk_full, 1)

            turned_ctx(0)
            for b in range(B):
                act.wait_ge(norm_step, 2 * b + 1)
                act.activation(rstd[:, 1, SB * b:SB * b + SB], rstd[:, 0, SB * b:SB * b + SB], ACT.Sqrt).then_inc(sq_done, 1)
            for b in range(B):
                unit(4 * b)
                unit(4 * b + 1)
                if b + 1 < B:
                    turned_ctx(b + 1)
                unit(4 * b + 2)
                unit(4 * b + 3)

        @block.tensor
        def _(pe):
            def turn(src, banks, b, copied, turned):
                for k in range(DC):
                    n = DC * b + k
                    if n >= 2:
                        pe.wait_ge(copied, n - 1)
                    for s in range(SB):
                        mm = pe.transpose(banks[n % 2][:, P * s:P * s + P], src[:, SB * b + s, P * k:P * k + P],
                                          c.ident[:, :])
                    mm.then_inc(turned, 1)

            def unit(u, w, src):
                b, m = u // 4, u % 2
                if u >= 2:
                    pe.wait_ge(qk_full, u - 1)
                for k in range(DC):
                    mm = pe.matmul(qb[u % 2][:, :], w[:, k, P * m:P * m + P], src[:, k, S * b:S * b + S],
                                   start=(k == 0), stop=(k == DC - 1))
                mm.then_inc(qk_mul, 1)

            def values(n):
                if n >= 2:
                    pe.wait_ge(v_full, 2 * (n - 1))
                for j in range(2):
                    tile = 2 * n + j
                    for k in range(DC):
                        mm = pe.matmul(vb[n % 2][:, D * j:D * j + D], cT[:, k, P * tile:P * tile + P], wv[:, k, :],
                                       start=(k == 0), stop=(k == DC - 1))
                mm.then_inc(v_mul, 1)

            pe.wait_ge(c_in[0], 16)
            turn(ctx_in, tb[0:2], 0, c_copied, c_turned)
            for b in range(B):
                pe.wait_ge(c_copied, DC * (b + 1))
                if b == 0:
                    pe.wait_ge(w_in, 16 * 6)
                unit(4 * b, wk, cT)
                unit(4 * b + 1, wk, cT)
                values(2 * b)
                values(2 * b + 1)
                if b + 1 < B:
                    pe.wait_ge(c_in[b + 1], 16)
                    turn(ctx_in, tb[0:2], b + 1, c_copied, c_turned)
                pe.wait_ge(xl_ready, SB * (b + 1))
                turn(xl, tb[2:4], b, x_copied, x_turned)
                pe.wait_ge(x_copied, DC * (b + 1))
                unit(4 * b + 2, wq, xT)
                unit(4 * b + 3, wq, xT)

        @block.vector
        def _(dve):
            for b in range(B):
                dve.wait_ge(x_in[b], 16)
                for i in range(SB * b, SB * b + SB):
                    dve.bn_stats(stats[:, i, :], x[:, i, :]).then_inc(stat_done, 1)
                    dve.wait_ge(stat_done, 2 * i + 1)
                    dve.bn_aggr(mv[:, i, :], stats[:, i, :]).then_inc(stat_done, 1)
                tiles = slice(SB * b, SB * b + SB)
                dve.wait_ge(stat_done, 2 * SB * (b + 1))
                dve.tensor_scalar(rstd[:, 0, tiles], mv[:, tiles, 1], EPS, None, ALU.add).then_inc(norm_step, 1)
                dve.wait_ge(sq_done, b + 1)
                dve.reciprocal(rstd[:, 2, tiles], rstd[:, 1, tiles]).then_inc(norm_step, 1)
                dve.wait_ge(norm_step, 2 * b + 2)
                for i in range(SB * b, SB * b + SB):
                    dve.tensor_scalar(xl[:, i, :], x[:, i, :], mv[:, i, 0:1], rstd[:, 2, i:i + 1],
                                      ALU.subtract, ALU.mult).then_inc(xl_ready, 1)

            def parts(u):
                dve.wait_ge(qk_full, u + 1)
                if u >= 4:
                    dve.wait_ge(stack_out[u % 4], 16 * 3 * (u // 4))
                dve.tensor_copy(high[:, u % 4, :], full[:, u % 4, :]).then_inc(high_done, 1)
                dve.wait_ge(high_done, u + 1)
                dve.tensor_sub(low[:, u % 4, :], full[:, u % 4, :], high[:, u % 4, :].bitcast(F32)).then_inc(split, 1)

            for b in range(B):
                for n in (2 * b, 2 * b + 1):
                    dve.wait_ge(v_mul, n + 1)
                    if n == 0:
                        dve.wait_ge(w_in, 16 * 6)
                    if n >= 4:
                        dve.wait_ge(v_out[n % 4], 32 * (n // 4))
                    for j in range(2):
                        dve.tensor_add(vout[:, n % 4, j, :], vb[n % 2][:, D * j:D * j + D], bv[:, :]).then_inc(v_full, 1)
                parts(4 * b)
                parts(4 * b + 1)
                for k in range(DC):
                    n = DC * b + k
                    dve.wait_ge(x_turned, n + 1)
                    dve.tensor_copy(xT[:, k, S * b:S * b + S], tb[2 + n % 2][:, :]).then_inc(x_copied, 1)
                parts(4 * b + 2)
                parts(4 * b + 3)



def attention(nc, c, t, two):
    a = Alloc(nc, "a2" if two else "a1")
    stacks_q, stacks_k, values_d, out_d, sums_d = (
        t["qs2" if two else "qs1"], t["ks2" if two else "ks1"], t["vs2" if two else "vs1"], t["o2" if two else "o1"],
        t["s2"])
    HEADS = B * H
    PASSES = HEADS // 8
    PEELED = 2
    NLOAD = 2
    NV = 1 if two else SB
    KR = 64
    KS = D2 if two else SP1
    SLOTS = 4 if two else 8
    OUTS = 2 if two else 1
    with a.stack:
        raw = a.sb("raw", [P, 4, S]) if two else None
        qa = a.sb("qa", [P, SLOTS, S], F32R) if two else None
        ka = a.sb("ka", [P, SLOTS, S], F32R) if two else None
        qm = a.sb("qm", [KR + 1, SLOTS, S], F32R)
        km = a.sb("km", [KR + 1, SLOTS, S], F32R)
        vals = a.sb("vals", [P, 2, SB, 4, D2 if two else 32])
        probs = a.sb("probs", [P, 8, PCOLS])
        junk = a.sb("junk", [P, SB, S], BF16)
        mx = a.sb("mx", [P, 2, SB])
        mxr = a.sb("mxr", [P, 2, SB], F32R)
        ones = a.sb("ones", [P, 32]) if two else None
        part = a.sb("part", [P, 8, S - P]) if two else None
        osb = a.sb("osb", [P, 2, S])
        ssb = a.sb("ssb", [P, 2, S]) if two else None
        sc = [a.ps("sc0"), a.ps("sc1")]
        sc.append(sc[0] if two else a.ps("sc2"))
        mrow = a.ps("mrow")
        st = a.ps("st", 1536)
        ob = a.ps("ob")
        sums = a.ps("sums") if two else None

        loaded = [a.sem(f"loaded{i}") for i in range(8)]
        v_loaded = [a.sem(f"v_loaded{i}") for i in range(2)]
        stored = [a.sem(f"stored{i}") for i in range(2)]
        s_stored = [a.sem(f"s_stored{i}") for i in range(2)]
        masked, summed, split_dve, split_act = (a.sem(n) for n in ("masked", "summed", "split_dve", "split_act"))
        set_up, scored, reduced, maxed, turned, row_set, st_done, exp_done = (a.sem(n) for n in (
            "set_up", "scored", "reduced", "maxed", "turned", "row_set", "st_done", "exp_done"))
        pv_done, o_copied, s_copied = (a.sem(n) for n in ("pv_done", "o_copied", "s_copied"))
        block = a.stack.enter_context(nc.Block())
        NSET = 2 if two else 4

        def ge(eng, sem, it, per_pass, const):
            if not isinstance(it, int):
                assert PEELED * per_pass + const > 0
                eng.wait_ge(sem, per_pass * it + const)
            elif per_pass * it + const > 0:
                eng.wait_ge(sem, per_pass * it + const)

        def steps(eng, step, last, end=PASSES):
            for s in range(8 * PEELED):
                step(s // 8, s % 8)
            with eng.Fori(PEELED, end) as it:
                for r in range(8):
                    step(it, r)
            for s in range(8 * end, last + 1):
                step(s // 8, s % 8)

        def there(it, r):
            return not isinstance(it, int) or 0 <= 8 * it + r < HEADS

        @block.sync
        def _(sp):
            def load_stacks(it, j):
                for r in range(4 * j, 4 * j + 4):
                    if two:
                        ge(sp, split_dve, it, 32, 4 * (r - 3))
                        sp.nop(nofuse=True)
                        ge(sp, split_act, it, 16, 2 * (r - 3))
                        sp.nop(nofuse=True)
                        sp.dma_start(raw[0:D2, r % 4, :], stacks_q[8 * it + r]).then_inc(loaded[r], 16)
                        sp.dma_start(raw[D2:P, r % 4, :], stacks_k[8 * it + r]).then_inc(loaded[r], 16)
                    else:
                        ge(sp, st_done, it, 24, 3 * (r - 8) + 3)
                        sp.dma_start(qm[0:SP1, r, :].bitcast(F32), stacks_q[8 * it + r]).then_inc(loaded[r], 16)
                        sp.dma_start(km[0:SP1, r, :].bitcast(F32), stacks_k[8 * it + r]).then_inc(loaded[r], 16)

            def load_values(it, j):
                ge(sp, pv_done, it, 8, 4 * j - 4)
                src = values_d[2 * it + j].rearrange("(kb p) d -> p kb d", p=P)
                if two:
                    sp.dma_start(vals[:, j % 2, :, :, :].rearrange("p kb h d -> p kb (h d)"), src).then_inc(v_loaded[j % 2], 16)
                else:
                    for kb in range(SB):
                        sp.dma_start(vals[:, j % 2, kb, :, 0:D1], src[:, kb, :].rearrange("p (h d) -> p h d", h=4))\
                          .then_inc(v_loaded[j % 2], 16)

            def load_experts(first, n):
                for k in range(DC):
                    sp.dma_start(c.w1[:, bass.ds(first, n), FF * k:FF * k + FF],
                                 t["L0_ffn_re_w1"][bass.ds(first, n), P * k:P * k + P, :].rearrange("e p n -> p e n"))\
                      .then_inc(c.w1_in, 16)

            def store_quad(it, j):
                for n in range(OUTS * j, OUTS * j + OUTS):
                    ge(sp, o_copied, it, 2 * OUTS, n + 1)
                    sp.dma_start(out_d[2 * OUTS * it + n], osb[:, n % 2, :]).then_inc(stored[n % 2], 16)
                if two:
                    ge(sp, s_copied, it, 2, j + 1)
                    sp.dma_start(sums_d[2 * it + j], ssb[0:P:32, j % 2, :]).then_inc(s_stored[j % 2], 16)

            sp.wait_ge(set_up, NSET)
            for n in range(2 * PEELED):
                load_stacks(n // 2, n % 2)
                if n >= 3:
                    store_quad(0, n - 3)
                if n:
                    load_values((n - 1) // 2, (n - 1) % 2)
            if two:
                load_experts(0, E - 4 * (PASSES - PEELED))
                sp.dma_start(c.w1[:, :, DC * FF:], t["L0_ffn_re_b1"]).then_inc(c.w1_in, 16)
            with sp.Fori(PEELED, PASSES) as it:
                for j in range(2):
                    load_stacks(it, j)
                    store_quad(it, j - 3)
                    load_values(it, j - 1)
                    if two:
                        load_experts(4 * it + (E - 4 * PASSES) + 2 * j, 2)
            load_values(PASSES - 1, 1)
            for n in range(2 * PASSES - 3, 2 * PASSES):
                store_quad(n // 2, n % 2)
            for sl in range(2):
                sp.wait_ge(stored[sl], 16 * PASSES * OUTS)
                if two:
                    sp.wait_ge(s_stored[sl], 16 * PASSES)

        @block.gpsimd
        def _(pool):
            pool.memset(km[KR:KR + 1, :, :].bitcast(F32), 1.0).then_inc(set_up, 1)
            pool.wait_ge(set_up, 1)
            if two:
                pool.memset(ones[:, :], 1.0).then_inc(set_up, 1)
            else:
                pool.memset(km[32:KR, :, :].bitcast(F32), 0.0).then_inc(set_up, 1)
                pool.wait_ge(set_up, 2)
                pool.memset(qm[32:KR, :, :].bitcast(F32), 0.0).then_inc(set_up, 1)
                pool.wait_ge(set_up, 3)
                pool.memset(vals[:, :, :, :, :], 1.0).then_inc(set_up, 1)

            pool.wait_ge(set_up, NSET)

            def select(cols):
                pool.nop(nofuse=True)
                return pool.affine_select(out=cols, in_=cols, compare_op=ALU.is_ge, fill=0.0, base=0,
                                          pattern=[[0, cols.shape[1]], [1, P]], channel_multiplier=-1)

            def step(it, r):
                if there(it, r - 2):
                    h = r - 2
                    for n, (lo, hi) in enumerate(((0, P), (S, S + P), (KCOL[3], KCOL[2] + P))):
                        ge(pool, exp_done, it, 24, 3 * h + n + 1)
                        select(probs[:, h % 8, lo:hi].rearrange("p (b n) -> p b n", n=P)).then_inc(masked, 1)
                    if two:
                        ge(pool, masked, it, 24, 3 * h + 3)
                        acc = part[:, h % 8, :]
                        pool.tensor_tensor(acc, probs[:, h % 8, P:S], probs[:, h % 8, KCOL[1]:KCOL[1] + KLEN[1]], ALU.add)\
                            .then_inc(summed, 1)
                        for n, kb in enumerate((2, 3)):
                            ge(pool, summed, it, 24, 3 * h + n + 1)
                            rest = part[:, h % 8, P * (kb - 1):S - P]
                            pool.tensor_tensor(rest, rest, probs[:, h % 8, KCOL[kb]:KCOL[kb] + KLEN[kb]], ALU.add)\
                                .then_inc(summed, 1)

            steps(pool, step, HEADS + 1)

        @block.tensor
        def _(pe):
            def score(out, sl, qb, n):
                q, k = slice(P * qb, P * qb + P), slice(0, n)
                if two:
                    pe.matmul(out, qa[:, sl, q], ka[:, sl, k], start=True, stop=False)
                    return pe.matmul(out, qm[0:D2, sl, q], km[0:D2, sl, k], start=False, stop=True)
                return pe.matmul(out, qm[0:KR, sl, q], km[0:KR, sl, k], start=True, stop=True)

            def shifted(sl, kb, half):
                out = st[:, KCOL[kb]:KCOL[kb] + KLEN[kb]]
                k, q = slice(P * kb, P * kb + P), slice(P * kb, S)
                if two and half == 0:
                    pe.matmul(out, ka[:, sl, k], qa[:, sl, q], start=True, stop=False)
                if half == 1:
                    return pe.matmul(out, km[:, sl, k], qm[:, sl, q], start=not two, stop=True)

            def values(n, j, it, kb):
                for hh in range(2 if two else 4):
                    hq = 2 * (j // 2) + hh if two else hh
                    M = D2 if two else 32
                    mm = pe.matmul(ob[M * hh:M * hh + M, P * kb:S], vals[:, n % 2, kb, hq, :],
                                   probs[:, (4 * n + hq) % 8, KCOL[kb]:KCOL[kb] + KLEN[kb]],
                                   start=(kb == 0), stop=(kb == (2 if two else 3)), tile_position=(0, M * hh))
                return mm

            def step(it, r):
                new, old, mid, late = there(it, r), there(it, r - 2), there(it, r - 1), there(it, r - 6)
                h, sl, osl = r - 2, r % SLOTS, (r - 2) % SLOTS
                if new:
                    if two:
                        ge(pe, split_dve, it, 32, 4 * r + 4)
                        ge(pe, split_act, it, 16, 2 * r + 2)
                    else:
                        pe.wait_ge(loaded[r], 16 * NLOAD * (it + 1))
                    ge(pe, reduced, it, 24, 3 * r - (1 if two else 2))
                    score(sc[0][:, :], sl, 3, S).then_inc(scored, 1)
                if old:
                    ge(pe, row_set, it, 8, r - 1)
                    ge(pe, exp_done, it, 24, 3 * (h - 1) + 1)
                    shifted(osl, 0, 0)
                    shifted(osl, 0, 1).then_inc(st_done, 1)
                    ge(pe, exp_done, it, 24, 3 * (h - 1) + 2)
                    shifted(osl, 1, 0)
                    shifted(osl, 1, 1)
                    shifted(osl, 3, 0)
                if late:
                    n, j = (r - 6) // 4, (r - 6) % 4
                    if j == 0:
                        pe.wait_ge(v_loaded[n % 2], 16 * NV * (it + n // 2 + 1))
                    if two:
                        ge(pe, masked, it, 24, 3 * (4 * n + 2 * (j // 2) + 2))
                        if j % 2 == 0:
                            ge(pe, o_copied, it, 4, 2 * n + j // 2)
                        kbs = ((0, 3), (1, 2))[j % 2]
                    else:
                        ge(pe, masked, it, 24, 3 * (4 * n + 4) - (0 if j else 2))
                        if j == 0:
                            ge(pe, o_copied, it, 2, n)
                        kbs = (j,)
                if not two and old:
                    shifted(osl, 3, 1).then_inc(st_done, 1)
                if mid:
                    ge(pe, maxed, it, 8, r)
                    ge(pe, row_set, it, 8, r - 1)
                    for qb in range(SB):
                        mm = pe.matmul(mrow[0:1, P * qb:P * qb + P], mxr[:, (r - 1) % 2, qb:qb + 1], c.ident_r[:, :],
                                       start=True, stop=True)
                    mm.then_inc(turned, 1)
                if late:
                    mm = values(n, j, it, kbs[0])
                if two and old:
                    shifted(osl, 3, 1).then_inc(st_done, 1)
                if late:
                    if two:
                        mm = values(n, j, it, kbs[1])
                        if j == 3:
                            ge(pe, summed, it, 24, 3 * (4 * n + 4))
                            ge(pe, s_copied, it, 2, n)
                            for hq in range(4):
                                pe.matmul(sums[32 * hq:32 * hq + 32, 0:P], ones[:, :], probs[:, (4 * n + hq) % 8, 0:P],
                                          start=True, stop=True, tile_position=(0, 32 * hq))
                            for hq in range(4):
                                mm = pe.matmul(sums[32 * hq:32 * hq + 32, P:S], ones[:, :], part[:, (4 * n + hq) % 8, :],
                                               start=True, stop=True, tile_position=(0, 32 * hq))
                    mm.then_inc(pv_done, 1)
                if new:
                    ge(pe, reduced, it, 24, 3 * r + (1 if two else -1))
                    score(sc[2][:, 0:2 * P], sl, 1, 2 * P).then_inc(scored, 1)
                    ge(pe, reduced, it, 24, 3 * r)
                    score(sc[1][:, 0:3 * P], sl, 2, 3 * P)
                    score(sc[1][:, 3 * P:S], sl, 0, P).then_inc(scored, 1)
                if old:
                    ge(pe, exp_done, it, 24, 3 * h)
                    shifted(osl, 2, 0)
                    shifted(osl, 2, 1).then_inc(st_done, 1)

            pe.wait_ge(set_up, NSET)
            steps(pe, step, HEADS + 5)

        @block.scalar
        def _(act):
            def split(it, r):
                sl = r % SLOTS
                act.wait_ge(loaded[r % 8], 16 * NLOAD * (it + r // 8 + 1))
                ge(act, st_done, it, 24, 3 * (r - 4) + 3)
                act.activation(ka[0:D2, sl, :], raw[D2:P, r % 4, :], ACT.Copy).then_inc(split_act, 1)
                act.activation(qm[0:D2, sl, :], raw[0:D2, r % 4, :], ACT.Copy).then_inc(split_act, 1)

            def step(it, r):
                def exps(u):
                    h = r - 2
                    ge(act, st_done, it, 24, 3 * h + u + 1)
                    lo, hi = S * u, min(S * u + S, PCOLS)
                    act.activation(probs[:, h % 8, lo:hi], st[:, lo:hi], ACT.Exp).then_inc(exp_done, 1)

                if two and there(it, r + 1):
                    split(it, r + 1)
                if there(it, r - 2):
                    ge(act, pv_done, it, 8, 4 * ((r - 10) // 4) + 4)
                    exps(0)
                if there(it, r - 1):
                    h = r - 1
                    ge(act, turned, it, 8, h + 1)
                    act.activation(qm[KR:KR + 1, h % SLOTS, :], mrow[0:1, :], ACT.Copy).then_inc(row_set, 1)
                if there(it, r - 2):
                    exps(1)
                    exps(2)
                p = r - 6
                if p % (4 // OUTS) == 4 // OUTS - 1 and there(it, p):
                    n = p // (4 // OUTS)
                    ge(act, pv_done, it, 8, p + 1)
                    ge(act, stored[n % 2], it, 16 * OUTS, 16 * (n // 2))
                    act.activation(osb[:, n % 2, :], ob[:, :], ACT.Copy).then_inc(o_copied, 1)
                    if two and n % 2 == 1:
                        n = n // 2
                        ge(act, s_stored[n % 2], it, 16, 16 * (n // 2))
                        act.activation(ssb[:, n % 2, :], sums[:, :], ACT.Copy).then_inc(s_copied, 1)

            if two:
                split(0, 0)
            else:
                for i, n in enumerate(("L0_ffn_q_w", "L0_ffn_k_w", "L0_ffn_v_w")):
                    act.dma_start(c.wqkv[:, i, :, :], t[n].rearrange("(k p) n -> p k n", p=P)).then_inc(c.wqkv_in, 16)
            steps(act, step, HEADS + 5, PASSES - 1 if two else PASSES)

        @block.vector
        def _(dve):
            def largest(it, r, src, qb):
                n = P * qb + P
                dve.nop(nofuse=True)
                return dve.tensor_tensor_reduce(
                    out=junk[:, qb, 0:n], in0=src, in1=c.mask_qk[:, S - n:S], scale=1.0, scalar=-3e38,
                    op0=ALU.add, op1=ALU.max, accum_out=mx[:, r % 2, qb:qb + 1])

            def split(it, r):
                sl = r % SLOTS
                q, k = raw[0:D2, r % 4, :], raw[D2:P, r % 4, :]
                dve.wait_ge(loaded[r % 8], 16 * NLOAD * (it + r // 8 + 1))
                ge(dve, st_done, it, 24, 3 * (r - 4) + 3)
                dve.tensor_copy(qa[0:D2, sl, :], q).then_inc(split_dve, 1)
                dve.tensor_copy(ka[D2:P, sl, :], k).then_inc(split_dve, 1)
                ge(dve, split_dve, it, 32, 4 * r + 1)
                dve.tensor_sub(qa[D2:P, sl, :], q, qa[0:D2, sl, :].bitcast(F32)).then_inc(split_dve, 1)
                ge(dve, split_dve, it, 32, 4 * r + 2)
                dve.tensor_sub(km[0:D2, sl, :], k, ka[D2:P, sl, :].bitcast(F32)).then_inc(split_dve, 1)

            def step(it, r):
                if there(it, r):
                    ge(dve, scored, it, 24, 3 * r + 1)
                    largest(it, r, sc[0][:, :], 3).then_inc(reduced, 1)
                if two and there(it, r + 1):
                    split(it, r + 1)
                if there(it, r):
                    ge(dve, scored, it, 24, 3 * r + 2)
                    largest(it, r, sc[2][:, 0:2 * P], 1).then_inc(reduced, 1)
                    ge(dve, scored, it, 24, 3 * r + 3)
                    largest(it, r, sc[1][:, 0:3 * P], 2)
                    largest(it, r, sc[1][:, 3 * P:S], 0).then_inc(reduced, 1)
                    ge(dve, reduced, it, 24, 3 * r + 3)
                    ge(dve, turned, it, 8, r - 1)
                    dve.tensor_copy(mxr[:, r % 2, :], mx[:, r % 2, :]).then_inc(maxed, 1)

            if two:
                split(0, 0)
            steps(dve, step, HEADS - 1, PASSES - 1 if two else PASSES)

class Tally:

    def __init__(self, sem):
        self.sem, self.n = sem, 0

    def add(self, instruction, by=1):
        self.n += by
        instruction.then_inc(self.sem, by)
        return self.n


def inverse_root(dve, r, cols, tick, rooted, n):
    v, root, inv, out = (r[:, i, cols] for i in range(4))
    dve.wait_ge(rooted, n)
    k = tick.add(dve.reciprocal(inv, root))
    dve.wait_ge(tick.sem, k)
    k = tick.add(dve.tensor_mul(out, inv, inv))
    dve.wait_ge(tick.sem, k)
    k = tick.add(dve.tensor_mul(out, out, v))
    dve.wait_ge(tick.sem, k)
    k = tick.add(dve.tensor_scalar(out, out, -0.5, 1.5, ALU.mult, ALU.add))
    dve.wait_ge(tick.sem, k)
    k = tick.add(dve.tensor_mul(out, out, inv))
    dve.wait_ge(tick.sem, k)


def project2(nc, c, t):
    a = Alloc(nc, "p2")
    with a.stack:
        sraw, srec = a.sb("sraw", [QUADS * 4, S]), a.sb("srec", [QUADS * 4, S])
        oT, rT = a.sb("oT", [P, 2, DC, S]), a.sb("rT", [P, 2, DC, S])
        wo = a.sb("wo", [P, DC, D])
        bo, g1 = a.sb("bo", [P, D]), a.sb("g1", [P, D])
        x = a.sb("x", [P, 2, SB, D])
        x1, xn = a.sb("x1", [P, 2, SB, D]), a.sb("xn", [P, 2, SB, D])
        sq = a.sb("sq", [P, D])
        stats, mv = a.sb("stats", [P, TILES, 6]), a.sb("mv", [P, TILES, 2])
        r1, r2 = a.sb("r1", [P, 4, TILES]), a.sb("r2", [P, 4, TILES])
        ssum = a.sb("ssum", [P, TILES])
        shift = a.sb("shift", [P, TILES])
        xh, xlo = a.sb("xh", [P, DC, 2, S], F32R), a.sb("xlo", [P, DC, 2, S], F32R)
        wh = [a.sb(f"wh{i}", [P, DC, W2], F32R) for i in range(3)]
        wl = [a.sb(f"wl{i}", [P, DC, W2], F32R) for i in range(3)]
        bqk = a.sb("bqk", [P, 2, W2 // P])
        bv = a.sb("bv", [1, W2])
        bvp, ones = a.sb("bvp", [33, W2], F32R), a.sb("ones", [33, P], F32R)
        prod = a.sb("prod", [P, 2, 4, S])
        ROT = 4
        rot = a.sb("rot", [P, ROT, 2, S])
        vout = a.sb("vout", [P, 2, W2])
        op = [a.ps("op0"), a.ps("op1")]
        tp = [a.ps("tp0"), a.ps("tp1")]
        ub = [a.ps(f"ub{i}") for i in range(4)]

        s_in, r_out, small_in = (a.sem(n) for n in ("s_in", "r_out", "small_in"))
        o_in = [a.sem(f"o_in{i}") for i in range(B)]
        x_in = [a.sem(f"x_in{i}") for i in range(B)]
        srec_done, o_scaled, xb_done = (a.sem(n) for n in ("srec_done", "o_scaled", "xb_done"))
        projected, x1_done, xn_done, root_asked, rooted, squared = (a.sem(n) for n in (
            "projected", "x1_done", "xn_done", "root_asked", "rooted", "squared"))
        t_done, h_copied, parts_done, split_h, split_l = (a.sem(n) for n in (
            "t_done", "h_copied", "parts_done", "split_h", "split_l"))
        unit_done, prods, rotated = (a.sem(n) for n in ("unit_done", "prods", "rotated"))
        xf_done = a.sem("xf_done")
        bias_set, shifted = a.sem("bias_set"), a.sem("shifted")
        v_mul, v_full, tick_s = a.sem("v_mul"), a.sem("v_full"), a.sem("tick")
        u_out = [a.sem(f"u_out{i}") for i in range(ROT)]
        v_out = [a.sem(f"v_out{i}") for i in range(2)]
        r_st = [a.sem(f"resid_out{i}") for i in range(2)]
        block = a.stack.enter_context(nc.Block())
        UNITS = 8

        def flat(x):
            return x.rearrange("p i d -> p (i d)")

        @block.sync
        def _(sp):
            sp.dma_start(sraw[:, :], t["o1"][:, :, D1, :].rearrange("q h n -> (q h) n")).then_inc(s_in, 16)
            def load(b):
                if b >= 2:
                    sp.wait_ge(projected, SB * (b - 1))
                    sp.wait_ge(x1_done, SB * (b - 1))
                sp.dma_start(x[:, b % 2, :, :], t["x"][b].rearrange("(s p) d -> p s d", p=P)).then_inc(x_in[b], 16)
                for m in range(DC):
                    q = SB * b + 2 * m
                    sp.dma_start(oT[:, b % 2, m, :], t["o1"][q:q + 2, :, 0:D1, :].rearrange("q h d n -> (q h) d n")).then_inc(o_in[b], 16)
                    if b == 0 and m == 0:
                        sp.wait_ge(srec_done, 1)
                        sp.dma_start(t["r1"].rearrange("q h n -> (q h) n"), srec[:, :]).then_inc(r_out, 16)
                        sp.wait_ge(r_out, 16)
                    for j in range(2):
                        for hh in range(4):
                            p0 = 64 * j + D1 * hh
                            sp.dma_start(rT[p0:p0 + D1, b % 2, m, :], t["r1"][q + j, hh:hh + 1, :].to_broadcast([D1, S]))\
                              .then_inc(o_in[b], 16)

            def store(b):
                sp.wait_ge(xn_done, SB * (b + 1))
                for src, name in ((x1, "x1"), (xn, "xn")):
                    sp.dma_start(t[name][SB * b:SB * b + SB].rearrange("s p d -> p s d"), src[:, b % 2, :, :])\
                      .then_inc(r_st[b % 2], 16)

            load(0)
            load(1)
            store(0)
            for b in range(B):
                if b + 2 < B:
                    load(b + 2)
                for u in range(UNITS * b, UNITS * b + UNITS):
                    g, is_k = u % UNITS // 2, u % 2
                    dst = t["ks2" if is_k else "qs2"][b * H + 4 * g:b * H + 4 * g + 4]
                    for half in range(2):
                        sp.wait_ge(rotated, 2 * u + half + 1)
                        sp.dma_start(dst[:, 32 * half:32 * half + 32, :], rot[:, u % ROT, half, :]).then_inc(u_out[u % ROT], 16)
                    if u % 2 == 0:
                        continue
                    i = u // 2
                    sp.wait_ge(v_full, 2 * (i + 1))
                    sp.dma_start(t["vs2"][SB * b:SB * b + SB, P * (i % SB):P * (i % SB) + P, :].rearrange("g p d -> p g d"),
                                 vout[:, i % 2, :].rearrange("p (g d) -> p g d", g=4)).then_inc(v_out[i % 2], 16)
                if b + 1 < B:
                    store(b + 1)
            for i in range(2):
                sp.wait_ge(r_st[i], 16 * 2 * B // 2)
                sp.wait_ge(v_out[i], 16 * TILES // 2)
            for i in range(ROT):
                sp.wait_ge(u_out[i], 16 * 2 * UNITS * B // ROT)

        @block.scalar
        def _(act):
            def high_weight(i):
                act.activation(wh[i][:, :, :], c.wqkv[:, i, :, :], ACT.Copy).then_inc(split_h, 1)

            def aside(b, n):
                cols = slice(SB * b, SB * b + SB)
                if n == 3:
                    act.wait_ge(root_asked, 2 * b + 1)
                    act.activation(r1[:, 1, cols], r1[:, 0, cols], ACT.Sqrt).then_inc(rooted, 1)
                if n == 4:
                    act.wait_ge(shifted, b + 1)
                    if b >= 2:
                        act.wait_ge(r_st[b % 2], 32 * (b // 2))
                    for i in range(SB):
                        m = SB * b + i
                        act.activation(xn[:, b % 2, i, :], x1[:, b % 2, i, :], ACT.Identity, bias=shift[:, m:m + 1],
                                       scale=r1[:, 3, m:m + 1]).then_inc(xf_done, 1)
                    for i in range(SB):
                        m = SB * b + i
                        act.wait_ge(xf_done, m + 1)
                        if m:
                            act.wait_ge(squared, m)
                        act.activation(sq[:, :], xn[:, b % 2, i, :], ACT.Square, accum_out=ssum[:, m:m + 1]).then_inc(squared, 1)
                if n == 5:
                    act.wait_ge(root_asked, 2 * b + 2)
                    act.activation(r2[:, 1, cols], r2[:, 0, cols], ACT.Sqrt).then_inc(rooted, 1)

            def parts(b):
                for k in range(DC):
                    act.wait_ge(t_done, DC * b + k + 1)
                    act.activation(xh[:, k, b % 2, :], tp[k][:, :], ACT.Copy).then_inc(h_copied, 1)

            def value_half(n):
                i, half = n // 2, n % 2
                act.wait_ge(v_mul, n + 1)
                if i >= 2 and not half:
                    act.wait_ge(v_out[i % 2], 16 * (i // 2))
                act.activation(vout[:, i % 2, S * half:S * half + S], tp[half][:, :], ACT.Copy).then_inc(v_full, 1)

            act.dma_start(wo[:, :, :], t["L0_xattn_wo"].rearrange("(k p) n -> p k n", p=P)).then_inc(small_in, 16)
            act.dma_start(bo[:, :], t["L0_xattn_bo"].to_broadcast([P, D])).then_inc(small_in, 16)
            act.dma_start(g1[:, :], t["L0_ffn_gamma1"].to_broadcast([P, D])).then_inc(small_in, 16)
            act.dma_start(bqk[:, 0, :], t["L0_ffn_q_b"]).then_inc(small_in, 16)
            act.dma_start(bqk[:, 1, :], t["L0_ffn_k_b"]).then_inc(small_in, 16)
            act.dma_start(bv[:, :], t["L0_ffn_v_b"]).then_inc(small_in, 16)
            act.wait_ge(c.wqkv_in, 16 * 3)
            for i in range(3):
                high_weight(i)
            for n in range(3, 6):
                aside(0, n)
            parts(0)
            for b in range(B):
                for n in range(UNITS):
                    value_half(UNITS * b + n)
                    if b + 1 < B:
                        aside(b + 1, n)
                if b + 1 < B:
                    parts(b + 1)

        @block.tensor
        def _(pe):
            def outputs(b):
                pe.wait_ge(small_in, 16 * 6)
                for i in range(SB):
                    n = SB * b + i
                    bank = op[i // 2]
                    for m in range(DC):
                        pe.wait_ge(o_scaled, DC * b + m + 1)
                        if n >= SB and i % 2 == 0 and m == 0:
                            pe.wait_ge(x1_done, n - 2)
                        mm = pe.matmul(bank[:, D * (i % 2):D * (i % 2) + D], oT[:, b % 2, m, P * i:P * i + P],
                                       wo[:, m, :], start=(m == 0), stop=(m == DC - 1))
                    mm.then_inc(projected, 1)

            def turn(b):
                pe.wait_ge(xn_done, SB * (b + 1))
                if b:
                    pe.wait_ge(v_full, 2 * SB * b)
                for k in range(DC):
                    for i in range(SB):
                        mm = pe.transpose(tp[k][:, P * i:P * i + P], xn[:, b % 2, i, P * k:P * k + P], c.ident[:, :])
                    mm.then_inc(t_done, 1)

            def unit(u):
                b, g, i = u // UNITS, u % UNITS // 2, u % 2
                if u < 2:
                    pe.wait_ge(split_l, i + 1)
                if u >= 2:
                    pe.wait_ge(prods, 4 * (u - 1))
                for half in range(2):
                    cols = slice(2 * P * g + P * half, 2 * P * g + P * half + P)
                    bank = ub[2 * (u % 2) + half]
                    n = 0
                    for k in range(DC):
                        for wt, xt in ((wh[i], xh), (wh[i], xlo), (wl[i], xh)):
                            mm = pe.matmul(bank[:, :], wt[:, k, cols], xt[:, k, b % 2, :], start=(n == 0), stop=(n == 5))
                            n += 1
                mm.then_inc(unit_done, 1)

            def value_half(n):
                i, half = n // 2, n % 2
                b, cols = i // SB, slice(S * half, S * half + S)
                toks = slice(P * (i % SB), P * (i % SB) + P)
                if n == 0:
                    pe.wait_ge(split_l, 3)
                    pe.wait_ge(bias_set, 4)
                if n % UNITS >= 2:
                    pe.wait_ge(v_full, n - 1)
                pe.matmul(tp[half][:, :], ones[:, :], bvp[:, cols], start=True, stop=False)
                for k in range(DC):
                    for xt, wt in ((xh, wh[2]), (xh, wl[2]), (xlo, wh[2])):
                        mm = pe.matmul(tp[half][:, :], xt[:, k, b % 2, toks], wt[:, k, cols], start=False,
                                       stop=(k == DC - 1 and wt is wh[2] and xt is xlo))
                mm.then_inc(v_mul, 1)

            outputs(0)
            turn(0)
            for b in range(B):
                pe.wait_ge(parts_done, DC * (b + 1))
                for n in range(UNITS):
                    unit(UNITS * b + n)
                    value_half(UNITS * b + n)
                    if n == 1 and b + 1 < B:
                        outputs(b + 1)
                if b + 1 < B:
                    turn(b + 1)

        @block.gpsimd
        def _(pool):
            def aside(b, n):
                if n == 0:
                    pool.wait_ge(o_in[b], 16 * 9 * DC)
                    for m in range(DC):
                        pool.tensor_tensor(oT[:, b % 2, m, :], oT[:, b % 2, m, :], rT[:, b % 2, m, :], ALU.mult).then_inc(o_scaled, 1)
                if n == 1:
                    pool.wait_ge(x_in[b], 16)
                    if b == 0:
                        pool.wait_ge(small_in, 16 * 6)
                    for i in range(SB):
                        pool.tensor_tensor(x[:, b % 2, i, :], x[:, b % 2, i, :], bo[:, :], ALU.add).then_inc(xb_done, 1)

            def unit(u):
                if u >= ROT:
                    pool.wait_ge(u_out[u % ROT], 32 * (u // ROT))
                for half, op in ((0, ALU.subtract), (1, ALU.add)):
                    pool.wait_ge(prods, 4 * u + 2 * half + 2)
                    pool.tensor_tensor(rot[:, u % ROT, half, :], prod[:, u % 2, 2 * half, :], prod[:, u % 2, 2 * half + 1, :], op)\
                        .then_inc(rotated, 1)

            pool.memset(ones[:, :].bitcast(F32), 1.0).then_inc(bias_set, 1)
            pool.wait_ge(bias_set, 1)
            pool.memset(bvp[:, :].bitcast(F32), 0.0).then_inc(bias_set, 1)
            for n in range(2):
                aside(0, n)
            for b in range(B):
                for n in range(UNITS):
                    unit(UNITS * b + n)
                    if b + 1 < B:
                        aside(b + 1, n)

        @block.vector
        def _(dve):
            tick = Tally(tick_s)

            dve.wait_ge(s_in, 16)
            dve.reciprocal(srec[:, :], sraw[:, :]).then_inc(srec_done, 1)

            def low_weight(i):
                dve.wait_ge(split_h, i + 1)
                dve.tensor_sub(wl[i][:, :, :], c.wqkv[:, i, :, :], wh[i][:, :, :].bitcast(F32)).then_inc(split_l, 1)

            def aside(b, n):
                cols = slice(SB * b, SB * b + SB)
                if n in (2, 3):
                    if n == 2 and b >= 2:
                        dve.wait_ge(r_st[b % 2], 32 * (b // 2))
                    dve.wait_ge(projected, SB * b + 2 * (n - 2) + 2)
                    m = SB * b + 2 * (n - 2)
                    dve.wait_ge(xb_done, m + 2)
                    dve.tensor_add(flat(x1[:, b % 2, 2 * (n - 2):2 * (n - 2) + 2, :]), op[n - 2][:, :],
                                   flat(x[:, b % 2, 2 * (n - 2):2 * (n - 2) + 2, :])).then_inc(x1_done, 2)
                    dve.wait_ge(x1_done, m + 2)
                    for i in range(m, m + 2):
                        k = tick.add(dve.bn_stats(stats[:, i, :], x1[:, b % 2, i % SB, :]))
                    dve.wait_ge(tick_s, k)
                    for i in range(m, m + 2):
                        k = tick.add(dve.bn_aggr(mv[:, i, :], stats[:, i, :]))
                    dve.wait_ge(tick_s, k)
                if n == 3:
                    dve.tensor_scalar(r1[:, 0, cols], mv[:, cols, 1], EPS, None, ALU.add).then_inc(root_asked, 1)
                if n == 4:
                    dve.wait_ge(root_asked, 2 * b + 1)
                    inverse_root(dve, r1, cols, tick, rooted, 2 * b + 1)
                    dve.scalar_tensor_tensor(out=shift[:, cols], in0=mv[:, cols, 0], scalar=-1.0, in1=r1[:, 3, cols],
                                             op0=ALU.mult, op1=ALU.mult).then_inc(shifted, 1)
                if n == 5:
                    dve.wait_ge(squared, SB * (b + 1))
                    dve.tensor_scalar(r2[:, 0, cols], ssum[:, cols], 1.0 / D, EPS, ALU.mult, ALU.add).then_inc(root_asked, 1)
                if n == 6:
                    dve.wait_ge(root_asked, 2 * b + 2)
                    inverse_root(dve, r2, cols, tick, rooted, 2 * b + 2)
                    for i in range(SB):
                        m = SB * b + i
                        dve.scalar_tensor_tensor(out=xn[:, b % 2, i, :], in0=xn[:, b % 2, i, :], scalar=r2[:, 3, m:m + 1],
                                                 in1=g1[:, :], op0=ALU.mult, op1=ALU.mult).then_inc(xn_done, 1)

            def parts(b):
                for k in range(DC):
                    dve.wait_ge(h_copied, DC * b + k + 1)
                    dve.tensor_sub(xlo[:, k, b % 2, :], tp[k][:, :], xh[:, k, b % 2, :].bitcast(F32)).then_inc(parts_done, 1)

            def unit(u):
                g, is_k = u % UNITS // 2, u % 2
                dve.wait_ge(unit_done, u + 1)
                cos, sin = (c.cos, c.sin) if is_k else (c.cos_q, c.sin_q)
                for n, (half, table) in enumerate(((0, cos), (1, sin), (0, sin), (1, cos))):
                    if u >= 2:
                        dve.wait_ge(rotated, 2 * (u - 2) + n // 2 + 1)
                    dve.scalar_tensor_tensor(out=prod[:, u % 2, n, :], in0=ub[2 * (u % 2) + half][:, :],
                                             scalar=bqk[:, is_k, 2 * g + half:2 * g + half + 1], in1=table[:, :],
                                             op0=ALU.add, op1=ALU.mult).then_inc(prods, 1)

            dve.wait_ge(c.wqkv_in, 16 * 3)
            for i in range(2):
                low_weight(i)
            dve.wait_ge(small_in, 16 * 6)
            dve.wait_ge(bias_set, 2)
            dve.tensor_copy(bvp[0:1, :], bv[:, :]).then_inc(bias_set, 1)
            dve.wait_ge(bias_set, 3)
            dve.tensor_sub(bvp[32:33, :], bv[:, :], bvp[0:1, :].bitcast(F32)).then_inc(bias_set, 1)
            for n in range(2, 7):
                aside(0, n)
            low_weight(2)
            parts(0)
            for b in range(B):
                for n in range(UNITS):
                    unit(UNITS * b + n)
                    if b + 1 < B:
                        aside(b + 1, n)
                if b + 1 < B:
                    parts(b + 1)



def mix(nc, c, t):
    a = Alloc(nc, "mx")
    with a.stack:
        CH = W2 // P
        RING = 4
        sraw, srec = a.sb("sraw", [B * H, S]), a.sb("srec", [B * H, S])
        oT, rT = a.sb("oT", [P, RING, S]), a.sb("rT", [P, RING, S])
        ow = a.sb("ow", [P, CH, D])
        ob, g2, sb2 = (a.sb(n, [P, D]) for n in ("ob", "g2", "sb2"))
        rb, sb1 = a.sb("rb", [P, E]), a.sb("sb1", [P, FF // P])
        rw = a.sb("rw", [P, DC, E])
        sw1, sw2 = a.sb("sw1", [P, DC, FF]), a.sb("sw2", [P, FF // P, D])
        ao, an = a.sb("ao", [P, 2, SB, D]), a.sb("an", [P, 2, SB, D])
        sq = a.sb("sq", [P, D])
        ssum, r2 = a.sb("ssum", [P, TILES]), a.sb("r2", [P, 4, TILES])
        anT = a.sb("anT", [P, DC, S])
        hid = a.sb("hid", [P, FF // P, S])
        op, tp, hp, yp = ([a.ps(f"{n}{i}") for i in range(2)] for n in ("op", "tp", "hp", "yp"))
        s_in, srec_done, r_out, small_in = (a.sem(n) for n in ("s_in", "srec_done", "r_out", "small_in"))
        x1_in = [a.sem(f"x1_in{i}") for i in range(B)]
        o_in = [a.sem(f"o_in{i}") for i in range(RING)]
        xn_in = [a.sem(f"xn_in{i}") for i in range(2)]
        an_out = [a.sem(f"an_out{i}") for i in range(2)]
        o_scaled, chunk_done, xb_done, ao_done, squared, root_asked, rooted, an_done = (a.sem(n) for n in (
            "o_scaled", "chunk_done", "xb_done", "ao_done", "squared", "root_asked", "rooted", "an_done"))
        t_done, t_copied, l_mul, l_done, h_mul, h_done, y_mul, y_done, base_step, tick_s = (a.sem(n) for n in (
            "t_done", "t_copied", "l_mul", "l_done", "h_mul", "h_done", "y_mul", "y_done", "base_step", "tick"))
        block = a.stack.enter_context(nc.Block())
        NSMALL = 9
        MID = CH // 2

        def flat(x):
            return x.rearrange("p i d -> p (i d)")

        @block.sync
        def _(sp):
            sp.dma_start(sraw[:, :], t["s2"].rearrange("q h n -> (q h) n")).then_inc(s_in, 16)

            def batch(b):
                for g in range(CH * b, CH * b + CH):
                    if g == CH * b + MID:
                        if b >= 2:
                            sp.wait_ge(base_step, 3 * (b - 1))
                        sp.dma_start(ao[:, b % 2, :, :], t["xn"][SB * b:SB * b + SB].rearrange("s p d -> p s d"))\
                          .then_inc(xn_in[b % 2], 16)
                    if g >= RING:
                        sp.wait_ge(chunk_done, g - RING + 1)
                    sp.dma_start(oT[:, g % RING, :], t["o2"][g]).then_inc(o_in[g % RING], 16)
                    if g == 0:
                        sp.wait_ge(srec_done, 1)
                        sp.dma_start(t["r2"].rearrange("q h n -> (q h) n"), srec[:, :]).then_inc(r_out, 16)
                        sp.wait_ge(r_out, 16)
                    for h in range(2):
                        sp.dma_start(rT[D2 * h:D2 * h + D2, g % RING, :],
                                     t["r2"][g // 2, 2 * (g % 2) + h:2 * (g % 2) + h + 1, :].to_broadcast([D2, S]))\
                          .then_inc(o_in[g % RING], 16)

            batch(0)
            for b in range(B):
                if b + 1 < B:
                    batch(b + 1)
                sp.wait_ge(an_done, SB * (b + 1))
                sp.dma_start(t["an"][P * SB * b:P * SB * (b + 1), :].rearrange("(s p) d -> p s d", p=P), an[:, b % 2, :, :])\
                  .then_inc(an_out[b % 2], 16)
            for i in range(2):
                sp.wait_ge(an_out[i], 16 * B // 2)

        @block.scalar
        def _(act):
            for dst, name, pat in ((ow, "L0_ffn_o_w", "(k p) n -> p k n"), (rw, "L0_ffn_router_w", "(k p) n -> p k n"),
                                   (sw1, "L0_ffn_sh_w1", "(k p) n -> p k n"), (sw2, "L0_ffn_sh_w2", "(k p) n -> p k n")):
                act.dma_start(dst[:, :, :], t[name].rearrange(pat, p=P)).then_inc(small_in, 16)
            for dst, name in ((ob, "L0_ffn_o_b"), (g2, "L0_ffn_gamma2"), (sb2, "L0_ffn_sh_b2"), (rb, "L0_ffn_router_b")):
                act.dma_start(dst[:, :], t[name].to_broadcast([P, dst.shape[1]])).then_inc(small_in, 16)
            act.dma_start(sb1[:, :], t["L0_ffn_sh_b1"]).then_inc(small_in, 16)

            def loads(b):
                act.dma_start(c.base[:, SB * b:SB * b + SB, :], t["x1"][SB * b:SB * b + SB].rearrange("s p d -> p s d"))\
                   .then_inc(x1_in[b], 16)
                lo, hi = 8 * b, min(8 * b + 8, E)
                for m in range(FF // P):
                    act.dma_start(c.w2[:, lo:hi, m, :], t["L0_ffn_re_w2"][lo:hi, P * m:P * m + P, :].rearrange("e p n -> p e n"))\
                       .then_inc(c.w2_in, 16)

            def pre(b):
                for i in range(SB):
                    n = SB * b + i
                    act.wait_ge(ao_done, 2 * b + i // 2 + 1)
                    if n:
                        act.wait_ge(squared, n)
                    act.activation(sq[:, :], ao[:, b % 2, i, :], ACT.Square, accum_out=ssum[:, n:n + 1]).then_inc(squared, 1)
                act.wait_ge(root_asked, b + 1)
                cols = slice(SB * b, SB * b + SB)
                act.activation(r2[:, 1, cols], r2[:, 0, cols], ACT.Sqrt).then_inc(rooted, 1)

            def post(b):
                for k in range(DC):
                    act.wait_ge(t_done, DC * b + k + 1)
                    if b:
                        act.wait_ge(h_mul, 2 * b)
                    act.activation(anT[:, k, :], tp[k][:, :], ACT.Copy).then_inc(t_copied, 1)
                for m in range(FF // P):
                    act.wait_ge(h_mul, 2 * b + m + 1)
                    if b:
                        act.wait_ge(y_mul, 2 * b)
                    act.activation(hid[:, m, :], hp[m][:, :], ACT.Gelu, bias=sb1[:, m:m + 1]).then_inc(h_done, 1)

            pre(0)
            for b in range(B):
                loads(b)
                post(b)
                if b + 1 < B:
                    pre(b + 1)

        @block.tensor
        def _(pe):
            def outputs(b):
                if b:
                    pe.wait_ge(ao_done, 2 * b)
                for m in range(CH):
                    g = CH * b + m
                    pe.wait_ge(o_scaled, g + 1)
                    for i in range(SB):
                        mm = pe.matmul(op[i // 2][:, D * (i % 2):D * (i % 2) + D], oT[:, g % RING, P * i:P * i + P],
                                       ow[:, m, :], start=(m == 0 and i % 2 == 0), stop=(m == CH - 1 and i % 2 == 1))
                    mm.then_inc(chunk_done, 1)

            pe.wait_ge(small_in, 16 * NSMALL)
            outputs(0)
            for b in range(B):
                if b + 1 < B:
                    outputs(b + 1)
                pe.wait_ge(an_done, SB * (b + 1))
                if b:
                    pe.wait_ge(l_done, b)
                for k in range(DC):
                    for i in range(SB):
                        mm = pe.transpose(tp[k][:, P * i:P * i + P], an[:, b % 2, i, P * k:P * k + P], c.ident[:, :])
                    mm.then_inc(t_done, 1)
                pe.wait_ge(t_copied, DC * (b + 1))
                for i in range(SB):
                    for k in range(DC):
                        mm = pe.matmul(tp[0][:, 32 * i:32 * i + E], anT[:, k, P * i:P * i + P], rw[:, k, :],
                                       start=(k == 0), stop=(k == DC - 1))
                mm.then_inc(l_mul, 1)
                for m in range(FF // P):
                    if b:
                        pe.wait_ge(h_done, 2 * (b - 1) + m + 1)
                    for k in range(DC):
                        mm = pe.matmul(hp[m][:, :], sw1[:, k, P * m:P * m + P], anT[:, k, :],
                                       start=(k == 0), stop=(k == DC - 1))
                    mm.then_inc(h_mul, 1)
                pe.wait_ge(h_done, 2 * (b + 1))
                for j in range(2):
                    if b:
                        pe.wait_ge(y_done, 2 * (b - 1) + j + 1)
                    for i in (2 * j, 2 * j + 1):
                        for m in range(FF // P):
                            mm = pe.matmul(yp[j][:, D * (i % 2):D * (i % 2) + D], hid[:, m, P * i:P * i + P], sw2[:, m, :],
                                           start=(m == 0), stop=(m == FF // P - 1))
                    mm.then_inc(y_mul, 1)

        @block.gpsimd
        def _(pool):
            def bias(b):
                pool.wait_ge(xn_in[b % 2], 16 * (b // 2 + 1))
                for j in range(SB):
                    pool.tensor_tensor(ao[:, b % 2, j, :], ao[:, b % 2, j, :], ob[:, :], ALU.add).then_inc(xb_done, 1)

            def scale(b):
                for g in range(CH * b, CH * b + CH):
                    if g == CH * b + MID:
                        bias(b)
                    pool.wait_ge(o_in[g % RING], 48 * (g // RING + 1))
                    pool.tensor_tensor(oT[:, g % RING, :], oT[:, g % RING, :], rT[:, g % RING, :], ALU.mult).then_inc(o_scaled, 1)

            pool.wait_ge(small_in, 16 * NSMALL)
            for b in range(B):
                scale(b)

        @block.vector
        def _(dve):
            tick = Tally(tick_s)
            dve.wait_ge(s_in, 16)
            dve.reciprocal(srec[:, :], sraw[:, :]).then_inc(srec_done, 1)
            dve.wait_ge(small_in, 16 * NSMALL)

            def outputs(b):
                dve.wait_ge(chunk_done, CH * (b + 1))
                dve.wait_ge(xb_done, SB * (b + 1))
                for j in range(2):
                    tiles = flat(ao[:, b % 2, 2 * j:2 * j + 2, :])
                    dve.tensor_add(tiles, tiles, op[j][:, :]).then_inc(ao_done, 1)

            def norm(b):
                cols = slice(SB * b, SB * b + SB)
                dve.wait_ge(squared, SB * (b + 1))
                dve.tensor_scalar(r2[:, 0, cols], ssum[:, cols], 1.0 / D, EPS, ALU.mult, ALU.add).then_inc(root_asked, 1)
                dve.wait_ge(root_asked, b + 1)
                inverse_root(dve, r2, cols, tick, rooted, b + 1)
                if b >= 2:
                    dve.wait_ge(an_out[b % 2], 16 * (b // 2))
                    dve.wait_ge(base_step, 3 * (b - 1))
                for i in range(SB):
                    n = SB * b + i
                    dve.scalar_tensor_tensor(out=an[:, b % 2, i, :], in0=ao[:, b % 2, i, :], scalar=r2[:, 3, n:n + 1],
                                             in1=g2[:, :], op0=ALU.mult, op1=ALU.mult).then_inc(an_done, 1)

            def base(b):
                tiles = c.base[:, SB * b:SB * b + SB, :]
                dve.wait_ge(x1_in[b], 16)
                dve.tensor_tensor(tiles, tiles, sb2[:, :].rearrange("p (o d) -> p o d", o=1).to_broadcast([P, SB, D]), ALU.add)\
                   .then_inc(base_step, 1)
                dve.wait_ge(base_step, 3 * b + 1)
                dve.tensor_add(flat(tiles), flat(tiles), flat(ao[:, b % 2, :, :])).then_inc(base_step, 1)
                dve.wait_ge(base_step, 3 * b + 2)
                dve.tensor_add(flat(tiles), flat(tiles), flat(an[:, b % 2, :, :])).then_inc(base_step, 1)

            outputs(0)
            norm(0)
            for b in range(B):
                if b + 1 < B:
                    outputs(b + 1)
                base(b)
                dve.wait_ge(l_mul, b + 1)
                dve.tensor_tensor(c.logits[:, SB * b:SB * b + SB, :],
                                  tp[0][:, 0:32 * SB].rearrange("p (i e) -> p i e", e=32)[:, :, 0:E],
                                  rb[:, :].rearrange("p (o e) -> p o e", o=1).to_broadcast([P, SB, E]), ALU.add).then_inc(l_done, 1)
                dve.wait_ge(base_step, 3 * (b + 1))
                for j in range(2):
                    tiles = flat(c.base[:, SB * b + 2 * j:SB * b + 2 * j + 2, :])
                    dve.wait_ge(y_mul, 2 * b + j + 1)
                    dve.tensor_add(tiles, tiles, yp[j][:, :]).then_inc(y_done, 1)
                if b + 1 < B:
                    norm(b + 1)



def route(nc, c, t):
    a = Alloc(nc, "rt")
    with a.stack:
        IX = NT + 2
        lg, ex, pos = (a.sb(n, [P, TILES, E]) for n in ("lg", "ex", "pos"))
        mx, tot, inv = (a.sb(n, [P, TILES]) for n in ("mx", "tot", "inv"))
        idx = a.sb("idx", [P, TILES, 8], U32)
        idxf = a.sb("idxf", [P, TILES, TOPK])
        oh, picked = a.sb("oh", [P, TOPK, TILES, E]), a.sb("picked", [P, TOPK, TILES, E])
        member = a.sb("member", [P, TILES, E], BF16)
        gate = a.sb("gate", [P, TILES, E])
        gateT = a.sb("gateT", [E, TOK])
        b2 = a.sb("b2", [E, D])
        counts = a.sb("counts", [P, E])
        over = a.sb("over", [P, E, TILES])
        nt, ct, start = (a.sb(n, [P, E]) for n in ("nt", "ct", "start"))
        tri = a.sb("tri", [P, E, E])
        spread = a.sb("spread", [P, E, E])
        slotf, rowf, tilef = (a.sb(n, [P, TOPK, TILES]) for n in ("slotf", "rowf", "tilef"))
        sloti, rowi, tilei = (a.sb(n, [P, TOPK, TILES], I32) for n in ("sloti", "rowi", "tilei"))
        e_no, j_no, t_no, row_no, p_no = (a.sb(n, s, I32) for n, s in (
            ("e_no", [P, E]), ("j_no", [P, TILES]), ("t_no", [P, TILES]), ("row_no", [P, P]), ("p_no", [P, 1])))
        e_nof, j_nof, t_nof, row_nof, p_nof = (a.sb(n + "f", s) for n, s in (
            ("e_no", [P, E]), ("j_no", [P, TILES]), ("t_no", [P, TILES]), ("row_no", [P, P]), ("p_no", [P, 1])))
        upper, ones = a.sb("upper", [P, P], BF16), a.sb("ones", [P, P], BF16)
        hot_row, hot_tile = a.sb("hot_row", [P, 4, P], F32R), a.sb("hot_tile", [P, 4, NT], F32R)
        of_tile, cmp = a.sb("of_tile", [P, 1]), a.sb("cmp", [P, E])
        rank_b, count_b, ids_b, row_b = (a.ps(n) for n in ("rank", "count", "ids", "row"))
        gt_b = [a.ps("gt0"), a.ps("gt1")]
        bb = [a.ps("bb0"), a.ps("bb1")]
        set_up, numbers, exped, tick_s, member_done, ranked, hot_r, hot_t, placed, b2_in = (a.sem(n) for n in (
            "set_up", "numbers", "exped", "tick", "member_done", "ranked", "hot_r", "hot_t", "placed", "b2_in"))
        l_ready, tile_of, rowed, gate_ready, g_turned, g_copied, b_mul, b_added = (a.sem(n) for n in (
            "l_ready", "tile_of", "rowed", "gate_ready", "g_turned", "g_copied", "b_mul", "b_added"))
        slots_known = a.sem("slots_known")
        block = a.stack.enter_context(nc.Block())
        STEPS = TOPK * TILES

        def over_tiles(x, n=TILES):
            return x.rearrange("p (o e) -> p o e", o=1).to_broadcast([P, n, E])

        def over_experts(x):
            return x.rearrange("p (i o) -> p i o", o=1).to_broadcast([P, TILES, E])

        @block.sync
        def _(sp):
            sp.dma_start(b2[:, :], t["L0_ffn_re_b2"]).then_inc(b2_in, 16)

        @block.gpsimd
        def _(pool):
            pool.iota(e_no[:, :], pattern=[[1, E]], base=0, channel_multiplier=0).then_inc(set_up, 1)
            pool.iota(j_no[:, :], pattern=[[P, TILES]], base=0, channel_multiplier=0).then_inc(set_up, 1)
            pool.iota(t_no[:, :], pattern=[[P, TILES]], base=0, channel_multiplier=1).then_inc(set_up, 1)
            pool.iota(row_no[:, :], pattern=[[1, P]], base=0, channel_multiplier=0).then_inc(set_up, 1)
            pool.iota(p_no[:, :], pattern=[[0, 1]], base=0, channel_multiplier=1).then_inc(set_up, 1)
            for m in (upper[:, :], tri[:, :, :], ones[:, :]):
                pool.wait_ge(set_up, 5)
                pool.memset(m, 1.0).then_inc(set_up, 1)
            pool.wait_ge(set_up, 8)
            pool.affine_select(out=upper[:, :], in_=upper[:, :], compare_op=ALU.is_gt, fill=0.0, base=0,
                               pattern=[[1, P]], channel_multiplier=-1).then_inc(set_up, 1)
            pool.affine_select(out=tri[:, :, :], in_=tri[:, :, :], compare_op=ALU.is_ge, fill=0.0, base=0,
                               pattern=[[1, E], [-1, E]], channel_multiplier=0).then_inc(set_up, 1)
            pool.wait_ge(placed, 1)
            pool.wait_ge(numbers, 5)
            for n in range(STEPS):
                k, i = n // TILES, n % TILES
                if n >= 4:
                    pool.wait_ge(ranked, n - 1)
                pool.tensor_scalar(hot_tile[:, n % 4, :], row_nof[:, 0:NT], tilef[:, k, i:i + 1], t_nof[:, i:i + 1],
                                   ALU.is_equal, ALU.mult).then_inc(hot_t, 1)

        @block.scalar
        def _(act):
            act.wait_ge(l_ready, 1)
            act.activation(ex[:, :, :], lg[:, :, :], ACT.Exp).then_inc(exped, 1)
            for b in range(B):
                act.wait_ge(g_turned, b + 1)
                act.activation(gateT[:, S * b:S * b + S], gt_b[b % 2][0:E, :], ACT.Copy).then_inc(g_copied, 1)

        @block.tensor
        def _(pe):
            pe.wait_ge(set_up, 10)
            pe.wait_ge(member_done, 1)
            pe.matmul(rank_b[:, 0:TILES * E], upper[:, :], member[:, :, :], start=True, stop=False)
            for i in range(TILES - 1):
                mm = pe.matmul(rank_b[:, E * (i + 1):E * TILES], ones[:, :], over_tiles(member[:, i, :], TILES - 1 - i),
                               start=False, stop=(i == TILES - 2))
            for i in range(TILES):
                mm = pe.matmul(count_b[:, 0:E], ones[:, :], member[:, i, :], start=(i == 0), stop=(i == TILES - 1))
            mm.then_inc(ranked, 1)
            pe.wait_ge(gate_ready, 1)
            for b in range(B):
                if b >= 2:
                    pe.wait_ge(g_copied, b - 1)
                for i in range(SB):
                    mm = pe.transpose(gt_b[b % 2][0:E, P * i:P * i + P], gate[:, SB * b + i, :], c.ident[:, :])
                mm.then_inc(g_turned, 1)
            pe.wait_ge(tile_of, 1)
            pe.matmul(row_b[0:1, 0:P], of_tile[:, :], c.ident[:, :], start=True, stop=True).then_inc(rowed, 1)
            for n in range(STEPS):
                pe.wait_ge(hot_r, n + 1)
                pe.wait_ge(hot_t, n + 1)
                pe.matmul(ids_b[:, 0:NT], hot_row[:, n % 4, :], hot_tile[:, n % 4, :], start=(n == 0),
                          stop=(n == STEPS - 1)).then_inc(ranked, 1)
            pe.wait_ge(b2_in, 16)
            for j in range(TILES // 2):
                pe.wait_ge(g_copied, j // 2 + 1)
                if j >= 2:
                    pe.wait_ge(b_added, j - 1)
                for i in (2 * j, 2 * j + 1):
                    mm = pe.matmul(bb[j % 2][:, D * (i % 2):D * (i % 2) + D], gateT[:, P * i:P * i + P], b2[:, :],
                                   start=True, stop=True)
                mm.then_inc(b_mul, 1)

        @block.vector
        def _(dve):
            tick = Tally(tick_s)

            def then(instruction):
                dve.wait_ge(tick_s, tick.add(instruction))

            then(dve.tensor_reduce(mx[:, :], c.logits[:, :, :], AX.X, ALU.max))
            dve.tensor_tensor(lg[:, :, :], c.logits[:, :, :], over_experts(mx[:, :]), ALU.subtract).then_inc(l_ready, 1)
            dve.wait_ge(set_up, 10)
            for dst, src in ((e_nof, e_no), (j_nof, j_no), (t_nof, t_no), (row_nof, row_no), (p_nof, p_no)):
                dve.tensor_copy(dst[:, :], src[:, :]).then_inc(numbers, 1)
            dve.wait_ge(exped, 1)
            then(dve.tensor_reduce(tot[:, :], ex[:, :, :], AX.X, ALU.add))
            then(dve.reciprocal(inv[:, :], tot[:, :]))
            then(dve.tensor_tensor(ex[:, :, :], ex[:, :, :], over_experts(inv[:, :]), ALU.mult))
            for i in range(TILES):
                k = tick.add(dve.max(c.gates[:, i, :], ex[:, i, :]))
            dve.wait_ge(tick_s, k)
            for i in range(TILES):
                k = tick.add(dve.max_index(idx[:, i, :], c.gates[:, i, :], ex[:, i, :]))
            dve.wait_ge(tick_s, k)
            then(dve.tensor_copy(idxf[:, :, :], idx[:, :, 0:TOPK]))
            dve.wait_ge(numbers, 5)
            for k in range(TOPK):
                n = tick.add(dve.tensor_tensor(oh[:, k, :, :], over_tiles(e_nof[:, :]), over_experts(idxf[:, :, k]), ALU.is_equal))
            dve.wait_ge(tick_s, n)
            then(dve.tensor_add(member[:, :, :], oh[:, 0, :, :], oh[:, 1, :, :]))
            dve.tensor_add(member[:, :, :], member[:, :, :], oh[:, 2, :, :]).then_inc(member_done, 1)
            for k in range(TOPK):
                n = tick.add(dve.tensor_tensor(picked[:, k, :, :], oh[:, k, :, :], over_experts(c.gates[:, :, k]), ALU.mult))
            dve.wait_ge(tick_s, n)
            then(dve.tensor_add(gate[:, :, :], picked[:, 0, :, :], picked[:, 1, :, :]))
            then(dve.tensor_add(gate[:, :, :], gate[:, :, :], picked[:, 2, :, :]))
            dve.nop(nofuse=True).then_inc(gate_ready, 1)
            dve.wait_ge(ranked, 1)
            then(dve.tensor_copy(counts[:, :], count_b[:, 0:E]))
            then(dve.tensor_tensor(over[:, :, :], counts[:, :].rearrange("p (e o) -> p e o", o=1).to_broadcast([P, E, TILES]),
                                   j_nof[:, :].rearrange("p (o j) -> p o j", o=1).to_broadcast([P, E, TILES]), ALU.is_gt))
            then(dve.tensor_reduce(nt[:, :], over[:, :, :], AX.X, ALU.add))
            then(dve.tensor_tensor(spread[:, :, :], tri[:, :, :], over_tiles(nt[:, :], E), ALU.mult))
            then(dve.tensor_reduce(ct[:, :], spread[:, :, :], AX.X, ALU.add))
            then(dve.tensor_scalar(cmp[:, :], ct[:, :], p_nof[:, 0:1], None, ALU.is_le))
            then(dve.tensor_reduce(of_tile[:, :], cmp[:, :], AX.X, ALU.add))
            dve.tensor_scalar(of_tile[:, :], of_tile[:, :], float(E - 1), None, ALU.min).then_inc(tile_of, 1)
            then(dve.tensor_sub(start[:, :], ct[:, :], nt[:, :]))
            then(dve.tensor_scalar(start[:, :], start[:, :], float(P), None, ALU.mult))
            then(dve.tensor_tensor(pos[:, :, :], rank_b[:, 0:TILES * E].rearrange("p (i e) -> p i e", e=E),
                                   over_tiles(start[:, :]), ALU.add))
            for k in range(TOPK):
                n = tick.add(dve.tensor_tensor(picked[:, k, :, :], oh[:, k, :, :], pos[:, :, :], ALU.mult))
            dve.wait_ge(tick_s, n)
            then(dve.tensor_reduce(slotf[:, :, :], picked[:, :, :, :], AX.X, ALU.add))
            then(dve.tensor_copy(sloti[:, :, :], slotf[:, :, :]))
            k = tick.add(dve.tensor_scalar(rowi[:, :, :], sloti[:, :, :], P - 1, None, ALU.bitwise_and))
            then(dve.tensor_scalar(tilei[:, :, :], sloti[:, :, :], 7, None, ALU.logical_shift_right))
            k = tick.add(dve.tensor_copy(rowf[:, :, :], rowi[:, :, :]))
            then(dve.tensor_copy(tilef[:, :, :], tilei[:, :, :]))
            then(dve.scalar_tensor_tensor(out=slotf[:, :, :], in0=rowf[:, :, :], scalar=float(NT), in1=tilef[:, :, :],
                                          op0=ALU.mult, op1=ALU.add))
            dve.tensor_copy(c.slots[:, :, :], slotf[:, :, :]).then_inc(placed, 1)
            dve.wait_ge(placed, 1)
            for n in range(STEPS):
                k, i = n // TILES, n % TILES
                if n >= 4:
                    dve.wait_ge(ranked, n - 2)
                dve.tensor_scalar(hot_row[:, n % 4, :], row_nof[:, :], rowf[:, k, i:i + 1], None, ALU.is_equal).then_inc(hot_r, 1)
            dve.wait_ge(rowed, 1)
            dve.tensor_copy(c.experts[:, :], row_b[0:1, 0:P]).then_inc(slots_known, 1)
            dve.wait_ge(ranked, STEPS + 1)
            dve.tensor_copy(c.ids[:, :], ids_b[:, 0:NT]).then_inc(slots_known, 1)
            for j in range(TILES // 2):
                dve.wait_ge(b_mul, j + 1)
                tiles = c.base[:, 2 * j:2 * j + 2, :].rearrange("p i d -> p (i d)")
                dve.tensor_add(tiles, tiles, bb[j % 2][:, :]).then_inc(b_added, 1)
            dve.wait_ge(b_added, TILES // 2)


def experts(nc, c, t):
    a = Alloc(nc, "ex")
    with a.stack:
        MC = FF // P
        PASSES = NT // 4
        PEELED = 2
        idc = a.sb("idc", [P, 4], I32)
        xg = a.sb("xg", [P, 4, D])
        w1 = a.sb("w1", [P, 2, DC * FF + MC])
        xT, hid = a.sb("xT", [P, 2, DC, P]), a.sb("hid", [P, 2, MC, P])
        y = a.sb("y", [P, 4, D])
        tb, hb, yb = ([a.ps(f"{n}{i}") for i in range(2)] for n in ("tb", "hb", "yb"))
        gathered = [a.sem(f"gathered{i}") for i in range(4)]
        stored = [a.sem(f"stored{i}") for i in range(4)]
        id_set, turned, x_copied, w_copied, h_mul, h_done, y_mul, y_copied = (a.sem(n) for n in (
            "id_set", "turned", "x_copied", "w_copied", "h_mul", "h_done", "y_mul", "y_copied"))
        block = a.stack.enter_context(nc.Block())

        def ge(eng, sem, it, per_pass, const):
            if not isinstance(it, int):
                assert PEELED * per_pass + const > 0
                eng.wait_ge(sem, per_pass * it + const)
            elif per_pass * it + const > 0:
                eng.wait_ge(sem, per_pass * it + const)

        def steps(eng, step, last):
            for s in range(4 * PEELED):
                step(s // 4, s % 4)
            with eng.Fori(PEELED, PASSES) as it:
                for r in range(4):
                    step(it, r)
            for r in range(last + 1 - 4 * PASSES):
                step(PASSES, r)

        def there(it, r):
            return not isinstance(it, int) or 0 <= 4 * it + r < NT

        ye = t["ye"].rearrange("(p n) d -> n p d", n=NT)

        @block.gpsimd
        def _(pool):
            def step(it, r):
                sl = r % 4
                ge(pool, turned, it, 4, r - 3)
                pool.tensor_copy(idc[:, sl:sl + 1], c.ids[:, bass.ds(4 * it + r, 1)]).then_inc(id_set, 1)
                ge(pool, id_set, it, 4, r + 1)
                pool.nop(nofuse=True)
                pool.indirect_dma_start(out=xg[:, sl, :], out_offset=None, in_=t["an"],
                                        in_offset=bass.IndirectOffsetOnAxis(ap=idc[:, sl:sl + 1], axis=0)).then_inc(gathered[sl], 16)

            steps(pool, step, NT - 1)

        @block.sync
        def _(sp):
            def step(it, r):
                ge(sp, y_copied, it, 4, r + 1)
                sp.dma_start(ye[4 * it + r], y[:, r % 4, :]).then_inc(stored[r % 4], 16)

            steps(sp, step, NT - 1)
            for i in range(4):
                sp.wait_ge(stored[i], 16 * ((NT - 1 - i) // 4 + 1))

        @block.tensor
        def _(pe):
            def step(it, r):
                if there(it, r):
                    sl = r % 4
                    ge(pe, gathered[sl], it, 16, 16)
                    ge(pe, x_copied, it, 4, r - 1)
                    for k in range(DC):
                        mm = pe.transpose(tb[r % 2][:, P * k:P * k + P], xg[:, sl, P * k:P * k + P], c.ident[:, :])
                    mm.then_inc(turned, 1)
                if there(it, r - 1):
                    n = r - 1
                    ge(pe, x_copied, it, 4, n + 1)
                    ge(pe, w_copied, it, 4, n + 1)
                    ge(pe, h_done, it, 4, n - 1)
                    for m in range(MC):
                        for k in range(DC):
                            mm = pe.matmul(hb[n % 2][:, P * m:P * m + P], w1[:, n % 2, FF * k + P * m:FF * k + P * m + P],
                                           xT[:, n % 2, k, :], start=(k == 0), stop=(k == DC - 1))
                    mm.then_inc(h_mul, 1)
                if there(it, r - 2):
                    n = r - 2
                    e = pe.value_load(c.experts[0:1, bass.ds(4 * it + n, 1)], min_val=0, max_val=E - 1)
                    ge(pe, h_done, it, 4, n + 1)
                    ge(pe, y_copied, it, 4, n - 1)
                    for m in range(MC):
                        mm = pe.matmul(yb[n % 2][:, 0:D], hid[:, n % 2, m, :], c.w2[:, bass.ds(e, 1), m, :],
                                       start=(m == 0), stop=(m == MC - 1))
                    mm.then_inc(y_mul, 1)

            pe.wait_ge(c.w2_in, 16 * MC * B)
            steps(pe, step, NT + 1)

        @block.scalar
        def _(act):
            def step(it, r):
                if there(it, r - 1):
                    n = r - 1
                    ge(act, h_mul, it, 4, n + 1)
                    ge(act, y_mul, it, 4, n - 1)
                    for m in range(MC):
                        mm = act.activation(hid[:, n % 2, m, :], hb[n % 2][:, P * m:P * m + P], ACT.Gelu,
                                            bias=w1[:, n % 2, DC * FF + m:DC * FF + m + 1])
                    mm.then_inc(h_done, 1)
                if there(it, r - 2):
                    n = r - 2
                    ge(act, y_mul, it, 4, n + 1)
                    ge(act, stored[n % 4], it, 16, 16 * (n // 4))
                    act.activation(y[:, n % 4, :], yb[n % 2][:, 0:D], ACT.Copy).then_inc(y_copied, 1)

            steps(act, step, NT + 1)

        @block.vector
        def _(dve):
            def step(it, r):
                e = dve.value_load(c.experts[0:1, bass.ds(4 * it + r, 1)], min_val=0, max_val=E - 1)
                ge(dve, h_done, it, 4, r - 1)
                dve.tensor_copy(w1[:, r % 2, :], c.w1[:, bass.ds(e, 1), :].rearrange("p o n -> p (o n)")).then_inc(w_copied, 1)
                ge(dve, turned, it, 4, r + 1)
                dve.tensor_copy(xT[:, r % 2, :, :].rearrange("p k n -> p (k n)"), tb[r % 2][:, 0:DC * P]).then_inc(x_copied, 1)

            dve.wait_ge(c.w1_in, 16 * c.w1_loads)
            steps(dve, step, NT - 1)


def combine(nc, c, t, out):
    a = Alloc(nc, "cb")
    with a.stack:
        RING = 4
        y = a.sb("y", [P, RING, TOPK, D])
        gathered = [a.sem(f"gathered{i}") for i in range(RING)]
        summed, out_s = a.sem("summed"), a.sem("out")
        block = a.stack.enter_context(nc.Block())

        @block.gpsimd
        def _(pool):
            for i in range(TILES):
                if i >= RING:
                    pool.wait_ge(summed, TOPK * (i - RING + 1))
                for k in range(TOPK):
                    pool.indirect_dma_start(out=y[:, i % RING, k, :], out_offset=None, in_=t["ye"],
                                            in_offset=bass.IndirectOffsetOnAxis(ap=c.slots[:, k, i:i + 1], axis=0))\
                        .then_inc(gathered[i % RING], 16)

        @block.vector
        def _(dve):
            for i in range(TILES):
                dve.wait_ge(gathered[i % RING], 16 * TOPK * (i // RING + 1))
                for k in range(TOPK):
                    if k:
                        dve.wait_ge(summed, TOPK * i + k)
                    dve.scalar_tensor_tensor(out=c.base[:, i, :], in0=y[:, i % RING, k, :], scalar=c.gates[:, i, k:k + 1],
                                             in1=c.base[:, i, :], op0=ALU.mult, op1=ALU.add).then_inc(summed, 1)

        @block.sync
        def _(sp):
            for i in range(TILES):
                sp.wait_ge(summed, TOPK * (i + 1))
                sp.dma_start(out[i // SB, P * (i % SB):P * (i % SB) + P, :], c.base[:, i, :]).then_inc(out_s, 16)
            sp.wait_ge(out_s, 16 * TILES)





NAMES = ["x", "ctx_1024", "L0_xattn_wq", "L0_xattn_bq", "L0_xattn_wk", "L0_xattn_bk", "L0_xattn_wv",
         "L0_xattn_bv", "L0_xattn_wo", "L0_xattn_bo", "L0_ffn_theta", "L0_ffn_gamma1", "L0_ffn_gamma2",
         "L0_ffn_q_w", "L0_ffn_q_b", "L0_ffn_k_w", "L0_ffn_k_b", "L0_ffn_v_w", "L0_ffn_v_b", "L0_ffn_o_w",
         "L0_ffn_o_b", "L0_ffn_router_w", "L0_ffn_router_b", "L0_ffn_sh_w1", "L0_ffn_sh_b1", "L0_ffn_sh_w2",
         "L0_ffn_sh_b2", "L0_ffn_re_w1", "L0_ffn_re_b1", "L0_ffn_re_w2", "L0_ffn_re_b2"]


def program(nc, t, out):
    def scratch(name, shape, dt=F32):
        t[name] = nc.dram_tensor(name, shape, dt).ap()

    scratch("qs1", (B * H, SP1, S))
    scratch("ks1", (B * H, SP1, S))
    scratch("vs1", (QUADS, S, 4 * D1))
    scratch("o1", (QUADS, 4, 32, S))
    scratch("qs2", (B * H, D2, S))
    scratch("ks2", (B * H, D2, S))
    scratch("vs2", (QUADS, S, 4 * D2))
    scratch("o2", (B * H // 2, 2 * D2, S))
    scratch("s2", (QUADS, 4, S))
    scratch("r2", (QUADS, 4, S))
    scratch("an", (TOK, D))
    scratch("ye", (P * NT, D))
    scratch("r1", (QUADS, 4, S))
    scratch("x1", (TILES, P, D))
    scratch("xn", (TILES, P, D))
    c = Alloc(nc, "keep")
    c.keep = c
    with c.stack:
        c.w1_loads = 2 * (1 + 2 * (B * H // 8 - 2)) + 1
        c.w1_in, c.w2_in, c.wqkv_in = c.sem("w1_in"), c.sem("w2_in"), c.sem("wqkv_in")
        make_identities(nc, c)
        rope = Alloc(nc, "rope")
        with rope.stack:
            make_tables(nc, c, rope, t)
            project1(nc, c, t)
            c.wqkv = rope.sb("wqkv", [P, 3, DC, W2])
            attention(nc, c, t, False)
            project2(nc, c, t)
        c.w1 = c.sb("w1", [P, E, DC * FF + FF // P])
        attention(nc, c, t, True)
        c.w2 = c.sb("w2", [P, E, FF // P, D])
        c.base = c.sb("base", [P, TILES, D])
        c.logits = c.sb("logits", [P, TILES, E])
        mix(nc, c, t)
        c.gates = c.sb("gates", [P, TILES, 8])
        c.slots = c.sb("slots", [P, TOPK, TILES], I32)
        c.ids = c.sb("ids", [P, NT], I32)
        c.experts = c.sb("experts", [1, P], I32)
        route(nc, c, t)
        experts(nc, c, t)
        combine(nc, c, t, out)


def kernel(**inputs):
    import concourse.bacc as bacc
    from concourse.bass_utils import run_bass_kernel_spmd

    x = {n: np.asarray(inputs[n]) for n in NAMES}
    for n in ("L0_xattn_bq", "L0_xattn_bk"):
        x[n] = x[n].reshape(DC, P).T
    for n in ("L0_ffn_q_w", "L0_ffn_k_w", "L0_ffn_q_b", "L0_ffn_k_b"):
        w = x[n].reshape(-1, 4, 4, D2 // 2, 2)
        x[n] = np.moveaxis(w, 4, 2).reshape(x[n].shape)
    for n in ("L0_ffn_q_b", "L0_ffn_k_b"):
        x[n] = x[n].reshape(W2 // P, P).T
    x["L0_ffn_sh_b1"] = x["L0_ffn_sh_b1"].reshape(FF // P, P).T
    x["L0_ffn_re_b1"] = np.moveaxis(x["L0_ffn_re_b1"].reshape(E, FF // P, P), 2, 0)
    x["L0_ffn_theta"] = x["L0_ffn_theta"].reshape(-1, 1)
    x = {n: v.reshape(1, -1) if v.ndim == 1 else v for n, v in x.items()}
    nc = bacc.Bacc("TRN2", target_bir_lowering=False, num_devices=1)
    arrays, t = {}, {}
    for n in NAMES:
        arrays[f"in_{n}"] = v = np.ascontiguousarray(x[n])
        t[n] = nc.dram_tensor(f"in_{n}", v.shape, mybir.dt.from_np(v.dtype), kind="ExternalInput").ap()
    out = nc.dram_tensor("out", (B, S, D), F32, kind="ExternalOutput").ap()
    program(nc, t, out)
    r = run_bass_kernel_spmd(nc, [arrays], core_ids=[0])
    return r.results[0]["out"]
```

```python
from contextlib import ExitStack

import numpy as np

import concourse.bass as bass
from concourse import mybir
from concourse.alu_op_type import AluOpType as ALU

F32 = mybir.dt.float32
F32R = mybir.dt.float32r
BF16 = mybir.dt.bfloat16
I32 = mybir.dt.int32
U32 = mybir.dt.uint32
ACT = mybir.ActivationFunctionType
AX = mybir.AxisListType

P = 128
B, S, D = 4, 512, 256
TOK = B * S
TILES = TOK // P
SB = S // P
DC = D // P
H = 16
D1 = D // H
D2 = 64
W2 = H * D2
QUADS = B * H // 4
E = 31
TOPK = 3
FF = 256
NT = (TOK * TOPK + E * (P - 1)) // P
EARLY = 3
EPS = 1e-5
MASKED = -1e30
TWO_PI = 2 * np.pi
TWO_PI_1 = 6.28125
TWO_PI_2 = float(np.round((TWO_PI - TWO_PI_1) * 2 ** 20) / 2 ** 20)
TWO_PI_3 = TWO_PI - TWO_PI_1 - TWO_PI_2
PI_BELOW = 3.1415925
ROUNDER = 1.5 * 2 ** 23
SP1 = 3 * D1
KCOL = [0, 512, 1024, 896]
KLEN = [S - P * kb for kb in range(SB)]
PCOLS = sum(KLEN)


class Alloc:

    def __init__(self, nc, tag):
        self.nc, self.tag, self.stack, self.sems = nc, tag, ExitStack(), []
        self.stack.callback(self.clear)

    def clear(self):
        if self.sems:
            self.nc.clear_and_free_semaphores(self.sems)
            self.nc.all_engine_barrier()

    def sb(self, name, shape, dt=F32):
        return self.stack.enter_context(self.nc.sbuf_tensor(f"{self.tag}_{name}", shape, dt))

    def ps(self, name, cols=512):
        return self.stack.enter_context(self.nc.psum_tensor(f"{self.tag}_{name}", [P, cols], F32))

    def sem(self, name):
        self.sems.append(self.nc.alloc_semaphore(f"{self.tag}_{name}"))
        return self.sems[-1]


def make_identities(nc, c):
    a = Alloc(nc, "const")
    c.ident = c.sb("ident", [P, P])
    c.ident_r = c.sb("ident_r", [P, P], F32R)
    c.mask_qk = c.sb("mask_qk", [P, S])
    with a.stack:
        filled, shaped, turned = a.sem("filled"), a.sem("shaped"), a.sem("turned")
        block = a.stack.enter_context(nc.Block())

        @block.gpsimd
        def _(pool):
            pool.memset(c.ident[:, :], 0.0).then_inc(filled, 1)
            pool.memset(c.mask_qk[:, :], 0.0).then_inc(filled, 1)
            pool.wait_ge(filled, 2)
            pool.affine_select(out=c.ident[:, :], in_=c.ident[:, :], compare_op=ALU.not_equal, fill=1.0, base=0,
                               pattern=[[-1, P]], channel_multiplier=1).then_inc(shaped, 1)
            pool.affine_select(out=c.mask_qk[:, S - P:S], in_=c.mask_qk[:, S - P:S], compare_op=ALU.is_ge,
                               fill=MASKED, base=0, pattern=[[-1, P]], channel_multiplier=1).then_inc(shaped, 1)

        @block.vector
        def _(dve):
            dve.wait_ge(shaped, 1)
            dve.tensor_scalar(c.ident_r[:, :], c.ident[:, :], -1.0, None, ALU.mult).then_inc(turned, 1)
            dve.wait_ge(turned, 1)
            dve.wait_ge(shaped, 2)


def project1(nc, c, t):
    a = Alloc(nc, "p1")
    with a.stack:
        x, ctx_in, xl = (a.sb(n, [P, TILES, D]) for n in ("x", "ctx", "xl"))
        xT, cT = (a.sb(n, [P, DC, TOK]) for n in ("xT", "cT"))
        wq, wk, wv = (a.sb(n, [P, DC, D]) for n in ("wq", "wk", "wv"))
        bq, bq4, bk = (a.sb(n, [P, DC]) for n in ("bq", "bq4", "bk"))
        bv = a.sb("bv", [P, D])
        stats, mv, rstd = a.sb("stats", [P, TILES, 6]), a.sb("mv", [P, TILES, 2]), a.sb("rstd", [P, 3, TILES])
        full = a.sb("full", [P, 4, S])
        high, low = a.sb("high", [P, 4, S], F32R), a.sb("low", [P, 4, S], F32R)
        vout = a.sb("vout", [P, 4, 2, D])
        tb = [a.ps(f"tb{i}") for i in range(4)]
        qb = [a.ps(f"qb{i}") for i in range(2)]
        vb = [a.ps(f"vb{i}") for i in range(2)]
        x_in = [a.sem(f"x_in{b}") for b in range(B)]
        c_in = [a.sem(f"c_in{b}") for b in range(B)]
        w_in, stat_done, norm_step, xl_ready = a.sem("w_in"), a.sem("stat_done"), a.sem("norm_step"), a.sem("xl_ready")
        sq_done, c_turned, x_turned, c_copied, x_copied = (a.sem(n) for n in (
            "sq_done", "c_turned", "x_turned", "c_copied", "x_copied"))
        qk_mul, qk_full, split, v_mul, v_full = (a.sem(n) for n in ("qk_mul", "qk_full", "split", "v_mul", "v_full"))
        high_done = a.sem("high_done")
        bq_scaled = a.sem("bq_scaled")
        stack_out = [a.sem(f"stack_out{i}") for i in range(4)]
        v_out = [a.sem(f"v_out{i}") for i in range(4)]
        counted, turned, theta_in, reduced, sine = (a.sem(n) for n in ("counted", "turned", "theta_in", "reduced", "sine"))
        theta, angle, whole, turn = a.sb("theta", [P, 1]), a.sb("angle", [P, S]), a.sb("whole", [P, S]), a.sb("turn", [P, 2, S])
        count = a.sb("count", [P, S], I32)
        block = a.stack.enter_context(nc.Block())
        SCALE = D1 ** -0.5

        @block.gpsimd
        def _(pool):
            pool.iota(count[:, :], pattern=[[1, S]], base=0, channel_multiplier=0).then_inc(counted, 1)

        @block.sync
        def _(sp):
            xv = t["x"].rearrange("b (s p) d -> b p s d", p=P)
            cv = t["ctx_1024"].rearrange("b (s p) d -> b p s d", p=P)
            for b in range(B):
                sp.dma_start(ctx_in[:, SB * b:SB * b + SB, :], cv[b]).then_inc(c_in[b], 16)
                sp.dma_start(x[:, SB * b:SB * b + SB, :], xv[b]).then_inc(x_in[b], 16)
                if b == 0:
                    for h in range(4):
                        sp.dma_start(theta[32 * h:32 * h + 32, :], t["L0_ffn_theta"]).then_inc(theta_in, 16)
                    sp.wait_ge(w_in, 16 * 6)
            for u in range(4 * B):
                b, is_q, m = u // 4, u % 4 >= 2, u % 2
                sp.wait_ge(split, u + 1)
                dst = (t["qs1"] if is_q else t["ks1"])[b * H + 8 * m:b * H + 8 * m + 8]
                parts = [(high, 0), (low, D1), (high, 2 * D1)] if is_q else [(high, 0), (high, D1), (low, 2 * D1)]
                for src, row in parts:
                    sp.dma_start(dst[:, row:row + D1, :], src[:, u % 4, :].bitcast(F32)).then_inc(stack_out[u % 4], 16)
                if not is_q:
                    n = 2 * b + m
                    sp.wait_ge(v_full, 2 * (n + 1))
                    for j in range(2):
                        tile = 2 * n + j
                        sp.dma_start(t["vs1"][SB * b:SB * b + SB, P * (tile % SB):P * (tile % SB) + P, :]
                                     .rearrange("g p d -> p g d"),
                                     vout[:, n % 4, j, :].rearrange("p (g d) -> p g d", g=4)).then_inc(v_out[n % 4], 16)
            for i in range(4):
                sp.wait_ge(stack_out[i], 16 * 3 * B)
                sp.wait_ge(v_out[i], 16 * 2 * 2 * B // 4)

        @block.scalar
        def _(act):
            for dst, name in ((wk, "L0_xattn_wk"), (wv, "L0_xattn_wv"), (wq, "L0_xattn_wq")):
                act.dma_start(dst[:, :, :], t[name].rearrange("(k p) n -> p k n", p=P)).then_inc(w_in, 16)
            for dst, name in ((bq, "L0_xattn_bq"), (bk, "L0_xattn_bk")):
                act.dma_start(dst[:, :], t[name]).then_inc(w_in, 16)
            act.dma_start(bv[:, :], t["L0_xattn_bv"].to_broadcast([P, D])).then_inc(w_in, 16)
            act.wait_ge(w_in, 16 * 6)
            act.activation(bq4[:, :], bq[:, :], ACT.Copy, scale=SCALE).then_inc(bq_scaled, 1)

            def turned_ctx(b):
                for k in range(DC):
                    n = DC * b + k
                    act.wait_ge(c_turned, n + 1)
                    act.activation(cT[:, k, S * b:S * b + S], tb[n % 2][:, :], ACT.Copy).then_inc(c_copied, 1)

            def unit(u):
                is_q, m = u % 4 >= 2, u % 2
                act.wait_ge(qk_mul, u + 1)
                if u >= 4:
                    act.wait_ge(split, u - 3)
                if u == 2:
                    act.wait_ge(bq_scaled, 1)
                act.activation(full[:, u % 4, :], qb[u % 2][:, :], ACT.Identity,
                               bias=(bq4 if is_q else bk)[:, m:m + 1], scale=SCALE if is_q else 1.0).then_inc(qk_full, 1)

            def root(b):
                act.wait_ge(norm_step, 2 * b + 1)
                act.activation(rstd[:, 1, SB * b:SB * b + SB], rstd[:, 0, SB * b:SB * b + SB], ACT.Sqrt).then_inc(sq_done, 1)

            turned_ctx(0)
            root(0)
            for b in range(B):
                unit(4 * b)
                unit(4 * b + 1)
                if b + 1 < B:
                    turned_ctx(b + 1)
                    root(b + 1)
                unit(4 * b + 2)
                unit(4 * b + 3)
            for n, table in enumerate((c.sin, c.cos)):
                act.wait_ge(reduced, n + 1)
                act.activation(table[:, :], turn[:, n, :], ACT.Sin).then_inc(sine, 1)
            act.wait_ge(sine, 2)
            for table, scaled in ((c.sin, c.sin_q), (c.cos, c.cos_q)):
                act.activation(scaled[:, :], table[:, :], ACT.Copy, scale=D2 ** -0.5)

        @block.tensor
        def _(pe):
            def turn(src, banks, b, copied, turned):
                for k in range(DC):
                    n = DC * b + k
                    if n >= 2:
                        pe.wait_ge(copied, n - 1)
                    for s in range(SB):
                        mm = pe.transpose(banks[n % 2][:, P * s:P * s + P], src[:, SB * b + s, P * k:P * k + P],
                                          c.ident[:, :])
                    mm.then_inc(turned, 1)

            def unit(u, w, src):
                b, m = u // 4, u % 2
                if u >= 2:
                    pe.wait_ge(qk_full, u - 1)
                for k in range(DC):
                    mm = pe.matmul(qb[u % 2][:, :], w[:, k, P * m:P * m + P], src[:, k, S * b:S * b + S],
                                   start=(k == 0), stop=(k == DC - 1))
                mm.then_inc(qk_mul, 1)

            def values(n):
                if n >= 2:
                    pe.wait_ge(v_full, 2 * (n - 1))
                for j in range(2):
                    tile = 2 * n + j
                    for k in range(DC):
                        mm = pe.matmul(vb[n % 2][:, D * j:D * j + D], cT[:, k, P * tile:P * tile + P], wv[:, k, :],
                                       start=(k == 0), stop=(k == DC - 1))
                mm.then_inc(v_mul, 1)

            pe.wait_ge(c_in[0], 16)
            turn(ctx_in, tb[0:2], 0, c_copied, c_turned)
            for b in range(B):
                pe.wait_ge(c_copied, DC * (b + 1))
                if b == 0:
                    pe.wait_ge(w_in, 16 * 6)
                unit(4 * b, wk, cT)
                unit(4 * b + 1, wk, cT)
                values(2 * b)
                values(2 * b + 1)
                if b + 1 < B:
                    pe.wait_ge(c_in[b + 1], 16)
                    turn(ctx_in, tb[0:2], b + 1, c_copied, c_turned)
                pe.wait_ge(xl_ready, SB * (b + 1))
                turn(xl, tb[2:4], b, x_copied, x_turned)
                pe.wait_ge(x_copied, DC * (b + 1))
                unit(4 * b + 2, wq, xT)
                unit(4 * b + 3, wq, xT)

        @block.vector
        def _(dve):
            def angles():
                dve.wait_ge(counted, 1)
                dve.tensor_copy(angle[:, :], count[:, :]).then_inc(turned, 1)
                dve.wait_ge(theta_in, 64)
                dve.wait_ge(turned, 1)
                dve.tensor_scalar(angle[:, :], angle[:, :], theta[:, 0:1], None, ALU.mult).then_inc(turned, 1)
                dve.wait_ge(turned, 2)
                n = 2
                for i, quarter in enumerate((0.0, 0.25)):
                    tr = turn[:, i, :]
                    steps = [lambda: dve.tensor_scalar(whole[:, :], angle[:, :], 1.0 / TWO_PI, quarter, ALU.mult, ALU.add),
                             lambda: dve.tensor_scalar(whole[:, :], whole[:, :], ROUNDER, None, ALU.add),
                             lambda: dve.tensor_scalar(whole[:, :], whole[:, :], -ROUNDER, None, ALU.add),
                             lambda: dve.scalar_tensor_tensor(out=tr, in0=whole[:, :], scalar=-TWO_PI_1, in1=angle[:, :],
                                                              op0=ALU.mult, op1=ALU.add),
                             lambda: dve.scalar_tensor_tensor(out=tr, in0=whole[:, :], scalar=-TWO_PI_2, in1=tr,
                                                              op0=ALU.mult, op1=ALU.add),
                             lambda: dve.scalar_tensor_tensor(out=tr, in0=whole[:, :], scalar=-TWO_PI_3, in1=tr,
                                                              op0=ALU.mult, op1=ALU.add),
                             lambda: dve.tensor_scalar(tr, tr, TWO_PI * quarter, PI_BELOW, ALU.add, ALU.min)]
                    for s in steps:
                        s().then_inc(turned, 1)
                        n += 1
                        dve.wait_ge(turned, n)
                    dve.tensor_scalar(tr, tr, -PI_BELOW, None, ALU.max).then_inc(reduced, 1)

            def norm(b):
                dve.wait_ge(x_in[b], 16)
                for i in range(SB * b, SB * b + SB):
                    dve.bn_stats(stats[:, i, :], x[:, i, :]).then_inc(stat_done, 1)
                    dve.wait_ge(stat_done, 2 * i + 1)
                    dve.bn_aggr(mv[:, i, :], stats[:, i, :]).then_inc(stat_done, 1)
                tiles = slice(SB * b, SB * b + SB)
                dve.wait_ge(stat_done, 2 * SB * (b + 1))
                dve.tensor_scalar(rstd[:, 0, tiles], mv[:, tiles, 1], EPS, None, ALU.add).then_inc(norm_step, 1)
                dve.wait_ge(sq_done, b + 1)
                dve.reciprocal(rstd[:, 2, tiles], rstd[:, 1, tiles]).then_inc(norm_step, 1)
                dve.wait_ge(norm_step, 2 * b + 2)
                for i in range(SB * b, SB * b + SB):
                    dve.tensor_scalar(xl[:, i, :], x[:, i, :], mv[:, i, 0:1], rstd[:, 2, i:i + 1],
                                      ALU.subtract, ALU.mult).then_inc(xl_ready, 1)

            def parts(u):
                dve.wait_ge(qk_full, u + 1)
                if u >= 4:
                    dve.wait_ge(stack_out[u % 4], 16 * 3 * (u // 4))
                dve.tensor_copy(high[:, u % 4, :], full[:, u % 4, :]).then_inc(high_done, 1)
                dve.wait_ge(high_done, u + 1)
                dve.tensor_sub(low[:, u % 4, :], full[:, u % 4, :], high[:, u % 4, :].bitcast(F32)).then_inc(split, 1)

            angles()
            norm(0)
            for b in range(B):
                for n in (2 * b, 2 * b + 1):
                    dve.wait_ge(v_mul, n + 1)
                    if n == 0:
                        dve.wait_ge(w_in, 16 * 6)
                    if n >= 4:
                        dve.wait_ge(v_out[n % 4], 32 * (n // 4))
                    for j in range(2):
                        dve.tensor_add(vout[:, n % 4, j, :], vb[n % 2][:, D * j:D * j + D], bv[:, :]).then_inc(v_full, 1)
                parts(4 * b)
                parts(4 * b + 1)
                for k in range(DC):
                    n = DC * b + k
                    dve.wait_ge(x_turned, n + 1)
                    dve.tensor_copy(xT[:, k, S * b:S * b + S], tb[2 + n % 2][:, :]).then_inc(x_copied, 1)
                if b + 1 < B:
                    norm(b + 1)
                parts(4 * b + 2)
                parts(4 * b + 3)



def attention(nc, c, t, two):
    a = Alloc(nc, "a2" if two else "a1")
    stacks_q, stacks_k, values_d, out_d, sums_d = (
        t["qs2" if two else "qs1"], t["ks2" if two else "ks1"], t["vs2" if two else "vs1"], t["o2" if two else "o1"],
        t["s2"])
    HEADS = B * H
    PASSES = HEADS // 8
    PEELED = 2
    NLOAD = 2
    NV = 1 if two else SB
    KR = 64
    KS = D2 if two else SP1
    SLOTS = 4 if two else 8
    OUTS = 2 if two else 1
    with a.stack:
        raw = a.sb("raw", [P, 4, S]) if two else None
        qa = a.sb("qa", [P, SLOTS, S], F32R) if two else None
        ka = a.sb("ka", [P, SLOTS, S], F32R) if two else None
        qm = a.sb("qm", [KR + 1, SLOTS, S], F32R)
        km = a.sb("km", [KR + 1, SLOTS, S], F32R)
        vals = a.sb("vals", [P, 2, SB, 4, D2 if two else 32])
        probs = a.sb("probs", [P, 8, PCOLS])
        junk = a.sb("junk", [P, SB, S], BF16)
        mx = a.sb("mx", [P, 2, SB])
        mxr = a.sb("mxr", [P, 2, SB], F32R)
        ones = a.sb("ones", [P, 32]) if two else None
        part = a.sb("part", [P, 8, S - P]) if two else None
        osb = a.sb("osb", [P, 2, S])
        ssb = a.sb("ssb", [P, 2, S]) if two else None
        sc = [a.ps("sc0"), a.ps("sc1")]
        sc.append(sc[0] if two else a.ps("sc2"))
        mrow = a.ps("mrow")
        st = a.ps("st", 1536)
        ob = a.ps("ob")
        sums = a.ps("sums") if two else None

        loaded = [a.sem(f"loaded{i}") for i in range(8)]
        v_loaded = [a.sem(f"v_loaded{i}") for i in range(2)]
        stored = [a.sem(f"stored{i}") for i in range(2)]
        s_stored = [a.sem(f"s_stored{i}") for i in range(2)]
        rows_set, masked, summed, split_dve, split_act = (a.sem(n) for n in ("rows_set", "masked", "summed", "split_dve", "split_act"))
        set_up, scored, reduced, maxed, turned, row_set, st_done, exp_done = (a.sem(n) for n in (
            "set_up", "scored", "reduced", "maxed", "turned", "row_set", "st_done", "exp_done"))
        pv_done, o_copied, s_copied = (a.sem(n) for n in ("pv_done", "o_copied", "s_copied"))
        first_in, inverted = a.sem("first_in"), a.sem("inverted")
        rec = a.sb("rec", [P, EARLY * S * H // P]) if two else None
        block = a.stack.enter_context(nc.Block())

        def ge(eng, sem, it, per_pass, const):
            if not isinstance(it, int):
                assert PEELED * per_pass + const > 0
                eng.wait_ge(sem, per_pass * it + const)
            elif per_pass * it + const > 0:
                eng.wait_ge(sem, per_pass * it + const)

        def steps(eng, step, last, end=PASSES):
            for s in range(8 * PEELED):
                step(s // 8, s % 8)
            with eng.Fori(PEELED, end) as it:
                for r in range(8):
                    step(it, r)
            for s in range(8 * end, last + 1):
                step(s // 8, s % 8)

        def there(it, r):
            return not isinstance(it, int) or 0 <= 8 * it + r < HEADS

        @block.sync
        def _(sp):
            def load_stacks(it, j):
                for r in range(4 * j, 4 * j + 4):
                    if two:
                        ge(sp, split_dve, it, 32, 4 * (r - 3))
                        sp.nop(nofuse=True)
                        ge(sp, split_act, it, 16, 2 * (r - 3))
                        sp.nop(nofuse=True)
                        sp.dma_start(raw[0:D2, r % 4, :], stacks_q[8 * it + r]).then_inc(loaded[r], 16)
                        sp.dma_start(raw[D2:P, r % 4, :], stacks_k[8 * it + r]).then_inc(loaded[r], 16)
                    else:
                        ge(sp, st_done, it, 24, 3 * (r - 8) + 3)
                        sp.dma_start(qm[0:SP1, r, :].bitcast(F32), stacks_q[8 * it + r]).then_inc(loaded[r], 16)
                        sp.dma_start(km[0:SP1, r, :].bitcast(F32), stacks_k[8 * it + r]).then_inc(loaded[r], 16)

            def load_values(it, j):
                ge(sp, pv_done, it, 8, 4 * j - 4)
                src = values_d[2 * it + j].rearrange("(kb p) d -> p kb d", p=P)
                if two:
                    sp.dma_start(vals[:, j % 2, :, :, :].rearrange("p kb h d -> p kb (h d)"), src).then_inc(v_loaded[j % 2], 16)
                else:
                    for kb in range(SB):
                        sp.dma_start(vals[:, j % 2, kb, :, 0:D1], src[:, kb, :].rearrange("p (h d) -> p h d", h=4))\
                          .then_inc(v_loaded[j % 2], 16)

            def load_experts(first, n):
                for k in range(DC):
                    sp.dma_start(c.w1[:, bass.ds(first, n), FF * k:FF * k + FF],
                                 t["L0_ffn_re_w1"][bass.ds(first, n), P * k:P * k + P, :].rearrange("e p n -> p e n"))\
                      .then_inc(c.w1_in, 16)

            def store_quad(it, j):
                for n in range(OUTS * j, OUTS * j + OUTS):
                    ge(sp, o_copied, it, 2 * OUTS, n + 1)
                    sp.dma_start(out_d[2 * OUTS * it + n], osb[:, n % 2, :]).then_inc(stored[n % 2], 16)
                if two:
                    ge(sp, s_copied, it, 2, j + 1)
                    sp.dma_start(sums_d[2 * it + j], ssb[0:P:32, j % 2, :]).then_inc(s_stored[j % 2], 16)

            def next_stage():
                if two:
                    for sl in range(2):
                        sp.wait_ge(s_stored[sl], 16 * EARLY * SB // 2)
                    sums = sums_d[0:EARLY * SB].rearrange("q h n -> (q h n)").rearrange("(p n) -> p n", p=P)
                    sp.dma_start(rec[:, :], sums).then_inc(first_in, 16)
                    sp.dma_start(c.ow[:, :, :], t["L0_ffn_o_w"].rearrange("(k p) n -> p k n", p=P)).then_inc(c.ow_in, 16)
                    return
                for sl in range(2):
                    sp.wait_ge(stored[sl], 16 * SB // 2)
                for m in range(DC):
                    heads = out_d[2 * m:2 * m + 2].rearrange("q h d n -> (q h) d n")
                    sp.dma_start(c.rT[:, 0, m, :], heads[:, D1:D1 + 1, :].to_broadcast([8, D1, S])).then_inc(first_in, 16)
                    sp.dma_start(c.oT[:, 0, m, :], heads[:, 0:D1, :]).then_inc(first_in, 16)
                sp.dma_start(c.wo[:, :, :], t["L0_xattn_wo"].rearrange("(k p) n -> p k n", p=P)).then_inc(c.small_in, 16)
                sp.dma_start(c.bo[:, :], t["L0_xattn_bo"].to_broadcast([P, D])).then_inc(c.small_in, 16)
                sp.dma_start(c.g1[:, :], t["L0_ffn_gamma1"].to_broadcast([P, D])).then_inc(c.small_in, 16)
                sp.dma_start(c.bqk[:, 0, :], t["L0_ffn_q_b"]).then_inc(c.small_in, 16)
                sp.dma_start(c.bqk[:, 1, :], t["L0_ffn_k_b"]).then_inc(c.small_in, 16)
                sp.dma_start(c.bv[:, :], t["L0_ffn_v_b"]).then_inc(c.small_in, 16)
                sp.dma_start(c.x[:, 0, :, :], t["x"][0].rearrange("(s p) d -> p s d", p=P)).then_inc(c.small_in, 16)

            sp.wait_ge(set_up, 1 if two else 2)
            sp.wait_ge(rows_set, 1 if two else 2)
            for n in range(2 * PEELED):
                load_stacks(n // 2, n % 2)
                if n >= 3:
                    store_quad(0, n - 3)
                if n:
                    load_values((n - 1) // 2, (n - 1) % 2)
            if two:
                load_experts(0, E - 4 * (PASSES - PEELED))
                sp.dma_start(c.w1[:, :, DC * FF:], t["L0_ffn_re_b1"]).then_inc(c.w1_in, 16)
            with sp.Fori(PEELED, PASSES) as it:
                for j in range(2):
                    load_stacks(it, j)
                    store_quad(it, j - 3)
                    load_values(it, j - 1)
                    if two:
                        load_experts(4 * it + (E - 4 * PASSES) + 2 * j, 2)
            load_values(PASSES - 1, 1)
            next_stage()
            for n in range(2 * PASSES - 3, 2 * PASSES):
                if two and n == 2 * PASSES - 1:
                    sp.wait_ge(inverted, 1)
                    sp.dma_start(t["r2"][0:EARLY * SB].rearrange("q h n -> (q h n)").rearrange("(p n) -> p n", p=P), rec[:, :])\
                      .then_inc(c.r2_out, 16)
                store_quad(n // 2, n % 2)
            for sl in range(2):
                sp.wait_ge(stored[sl], 16 * PASSES * OUTS)
                if two:
                    sp.wait_ge(s_stored[sl], 16 * PASSES)

        @block.gpsimd
        def _(pool):
            if two:
                pool.memset(ones[:, :], 1.0).then_inc(set_up, 1)
            else:
                pool.memset(qm[32:KR, :, :].bitcast(F32), 0.0).then_inc(set_up, 1)
                pool.wait_ge(set_up, 1)
                pool.memset(vals[:, :, :, :, :], 1.0).then_inc(set_up, 1)

            pool.wait_ge(set_up, 1 if two else 2)

            def select(cols):
                pool.nop(nofuse=True)
                return pool.affine_select(out=cols, in_=cols, compare_op=ALU.is_ge, fill=0.0, base=0,
                                          pattern=[[0, cols.shape[1]], [1, P]], channel_multiplier=-1)

            def step(it, r):
                if there(it, r - 2):
                    h = r - 2
                    for n, (lo, hi) in enumerate(((0, P), (S, S + P), (KCOL[3], KCOL[2] + P))):
                        ge(pool, exp_done, it, 24, 3 * h + n + 1)
                        select(probs[:, h % 8, lo:hi].rearrange("p (b n) -> p b n", n=P)).then_inc(masked, 1)
                    if two:
                        ge(pool, masked, it, 24, 3 * h + 3)
                        acc = part[:, h % 8, :]
                        pool.tensor_tensor(acc, probs[:, h % 8, P:S], probs[:, h % 8, KCOL[1]:KCOL[1] + KLEN[1]], ALU.add)\
                            .then_inc(summed, 1)
                        for n, kb in enumerate((2, 3)):
                            ge(pool, summed, it, 24, 3 * h + n + 1)
                            rest = part[:, h % 8, P * (kb - 1):S - P]
                            pool.tensor_tensor(rest, rest, probs[:, h % 8, KCOL[kb]:KCOL[kb] + KLEN[kb]], ALU.add)\
                                .then_inc(summed, 1)

            steps(pool, step, HEADS + 1)
            if not two:
                for m in range(DC):
                    pool.wait_ge(inverted, m + 1)
                    pool.tensor_tensor(c.oT[:, 0, m, :], c.oT[:, 0, m, :], c.rT[:, 0, m, :], ALU.mult).then_inc(c.o_scaled, 1)

        @block.tensor
        def _(pe):
            def score(out, sl, qb, n):
                q, k = slice(P * qb, P * qb + P), slice(0, n)
                if two:
                    pe.matmul(out, qa[:, sl, q], ka[:, sl, k], start=True, stop=False)
                    return pe.matmul(out, qm[0:D2, sl, q], km[0:D2, sl, k], start=False, stop=True)
                return pe.matmul(out, qm[0:KR, sl, q], km[0:KR, sl, k], start=True, stop=True)

            def shifted(sl, kb, half):
                out = st[:, KCOL[kb]:KCOL[kb] + KLEN[kb]]
                k, q = slice(P * kb, P * kb + P), slice(P * kb, S)
                if two and half == 0:
                    pe.matmul(out, ka[:, sl, k], qa[:, sl, q], start=True, stop=False)
                if half == 1:
                    return pe.matmul(out, km[:, sl, k], qm[:, sl, q], start=not two, stop=True)

            def values(n, j, it, kb):
                for hh in range(2 if two else 4):
                    hq = 2 * (j // 2) + hh if two else hh
                    M = D2 if two else 32
                    mm = pe.matmul(ob[M * hh:M * hh + M, P * kb:S], vals[:, n % 2, kb, hq, :],
                                   probs[:, (4 * n + hq) % 8, KCOL[kb]:KCOL[kb] + KLEN[kb]],
                                   start=(kb == 0), stop=(kb == (2 if two else 3)), tile_position=(0, M * hh))
                return mm

            def step(it, r):
                new, old, mid, late = there(it, r), there(it, r - 2), there(it, r - 1), there(it, r - 6)
                h, sl, osl = r - 2, r % SLOTS, (r - 2) % SLOTS
                if new:
                    if two:
                        ge(pe, split_dve, it, 32, 4 * r + 4)
                        ge(pe, split_act, it, 16, 2 * r + 2)
                    else:
                        pe.wait_ge(loaded[r], 16 * NLOAD * (it + 1))
                    ge(pe, reduced, it, 24, 3 * r - (1 if two else 2))
                    score(sc[0][:, :], sl, 3, S).then_inc(scored, 1)
                    if not two:
                        ge(pe, reduced, it, 24, 3 * r - 1)
                        score(sc[2][:, 0:2 * P], sl, 1, 2 * P).then_inc(scored, 1)
                if old:
                    ge(pe, row_set, it, 8, r - 1)
                    ge(pe, exp_done, it, 24, 3 * (h - 1) + 1)
                    shifted(osl, 0, 0)
                    shifted(osl, 0, 1).then_inc(st_done, 1)
                    ge(pe, exp_done, it, 24, 3 * (h - 1) + 2)
                    shifted(osl, 1, 0)
                    shifted(osl, 1, 1)
                    shifted(osl, 3, 0)
                if late:
                    n, j = (r - 6) // 4, (r - 6) % 4
                    if j == 0:
                        pe.wait_ge(v_loaded[n % 2], 16 * NV * (it + n // 2 + 1))
                    if two:
                        ge(pe, masked, it, 24, 3 * (4 * n + 2 * (j // 2) + 2))
                        if j % 2 == 0:
                            ge(pe, o_copied, it, 4, 2 * n + j // 2)
                        kbs = ((0, 3), (1, 2))[j % 2]
                    else:
                        ge(pe, masked, it, 24, 3 * (4 * n + 4) - (0 if j else 2))
                        if j == 0:
                            ge(pe, o_copied, it, 2, n)
                        kbs = (j,)
                if not two and old:
                    shifted(osl, 3, 1).then_inc(st_done, 1)
                if late:
                    mm = values(n, j, it, kbs[0])
                if two and old:
                    shifted(osl, 3, 1).then_inc(st_done, 1)
                if late:
                    if two:
                        mm = values(n, j, it, kbs[1])
                        if j == 3:
                            ge(pe, summed, it, 24, 3 * (4 * n + 4))
                            ge(pe, s_copied, it, 2, n)
                            for hq in range(4):
                                pe.matmul(sums[32 * hq:32 * hq + 32, 0:P], ones[:, :], probs[:, (4 * n + hq) % 8, 0:P],
                                          start=True, stop=True, tile_position=(0, 32 * hq))
                            for hq in range(4):
                                mm = pe.matmul(sums[32 * hq:32 * hq + 32, P:S], ones[:, :], part[:, (4 * n + hq) % 8, :],
                                               start=True, stop=True, tile_position=(0, 32 * hq))
                    mm.then_inc(pv_done, 1)
                if mid:
                    ge(pe, maxed, it, 8, r)
                    ge(pe, row_set, it, 8, r - 1)
                    for qb in range(SB):
                        mm = pe.matmul(mrow[0:1, P * qb:P * qb + P], mxr[:, (r - 1) % 2, qb:qb + 1], c.ident_r[:, :],
                                       start=True, stop=True)
                    mm.then_inc(turned, 1)
                if new:
                    if two:
                        ge(pe, reduced, it, 24, 3 * r + 1)
                        score(sc[2][:, 0:2 * P], sl, 1, 2 * P).then_inc(scored, 1)
                    ge(pe, reduced, it, 24, 3 * r)
                    score(sc[1][:, 0:3 * P], sl, 2, 3 * P)
                    score(sc[1][:, 3 * P:S], sl, 0, P).then_inc(scored, 1)
                if old:
                    ge(pe, exp_done, it, 24, 3 * h)
                    shifted(osl, 2, 0)
                    shifted(osl, 2, 1).then_inc(st_done, 1)

            pe.wait_ge(set_up, 1 if two else 2)
            pe.wait_ge(rows_set, 1 if two else 2)
            steps(pe, step, HEADS + 5)

        @block.scalar
        def _(act):
            def split(it, r):
                sl = r % SLOTS
                act.wait_ge(loaded[r % 8], 16 * NLOAD * (it + r // 8 + 1))
                ge(act, st_done, it, 24, 3 * (r - 4) + 3)
                act.activation(ka[0:D2, sl, :], raw[D2:P, r % 4, :], ACT.Copy).then_inc(split_act, 1)
                act.activation(qm[0:D2, sl, :], raw[0:D2, r % 4, :], ACT.Copy).then_inc(split_act, 1)

            def step(it, r):
                def exps(u):
                    h = r - 2
                    ge(act, st_done, it, 24, 3 * h + u + 1)
                    lo, hi = S * u, min(S * u + S, PCOLS)
                    act.activation(probs[:, h % 8, lo:hi], st[:, lo:hi], ACT.Exp).then_inc(exp_done, 1)

                if two and there(it, r + 1):
                    split(it, r + 1)
                if there(it, r - 2):
                    ge(act, pv_done, it, 8, 4 * ((r - 10) // 4) + 4)
                    exps(0)
                if there(it, r - 2):
                    exps(1)
                if there(it, r - 1):
                    h = r - 1
                    ge(act, turned, it, 8, h + 1)
                    act.activation(qm[KR:KR + 1, h % SLOTS, :], mrow[0:1, :], ACT.Copy).then_inc(row_set, 1)
                if there(it, r - 2):
                    exps(2)
                if not two and isinstance(it, int) and it == 1 and r < 3:
                    n = ("L0_ffn_q_w", "L0_ffn_k_w", "L0_ffn_v_w")[r]
                    act.dma_start(c.wqkv[:, r, :, :], t[n].rearrange("(k p) n -> p k n", p=P)).then_inc(c.wqkv_in, 16)
                p = r - 6
                if p % (4 // OUTS) == 4 // OUTS - 1 and there(it, p):
                    n = p // (4 // OUTS)
                    ge(act, pv_done, it, 8, p + 1)
                    ge(act, stored[n % 2], it, 16 * OUTS, 16 * (n // 2))
                    act.activation(osb[:, n % 2, :], ob[:, :], ACT.Copy).then_inc(o_copied, 1)
                    if two and n % 2 == 1:
                        n = n // 2
                        ge(act, s_stored[n % 2], it, 16, 16 * (n // 2))
                        act.activation(ssb[:, n % 2, :], sums[:, :], ACT.Copy).then_inc(s_copied, 1)

            if two:
                split(0, 0)
            steps(act, step, HEADS + 5, PASSES - 1 if two else PASSES)

        @block.vector
        def _(dve):
            def largest(it, r, src, qb):
                n = P * qb + P
                dve.nop(nofuse=True)
                return dve.tensor_tensor_reduce(
                    out=junk[:, qb, 0:n], in0=src, in1=c.mask_qk[:, S - n:S], scale=1.0, scalar=-3e38,
                    op0=ALU.add, op1=ALU.max, accum_out=mx[:, r % 2, qb:qb + 1])

            def split(it, r):
                sl = r % SLOTS
                q, k = raw[0:D2, r % 4, :], raw[D2:P, r % 4, :]
                dve.wait_ge(loaded[r % 8], 16 * NLOAD * (it + r // 8 + 1))
                ge(dve, st_done, it, 24, 3 * (r - 4) + 3)
                dve.tensor_copy(qa[0:D2, sl, :], q).then_inc(split_dve, 1)
                dve.tensor_copy(ka[D2:P, sl, :], k).then_inc(split_dve, 1)
                ge(dve, split_dve, it, 32, 4 * r + 1)
                dve.tensor_sub(qa[D2:P, sl, :], q, qa[0:D2, sl, :].bitcast(F32)).then_inc(split_dve, 1)
                ge(dve, split_dve, it, 32, 4 * r + 2)
                dve.tensor_sub(km[0:D2, sl, :], k, ka[D2:P, sl, :].bitcast(F32)).then_inc(split_dve, 1)

            def step(it, r):
                if there(it, r):
                    ge(dve, scored, it, 24, 3 * r + 1)
                    largest(it, r, sc[0][:, :], 3).then_inc(reduced, 1)
                if two and there(it, r + 1):
                    split(it, r + 1)
                if there(it, r):
                    ge(dve, scored, it, 24, 3 * r + 2)
                    largest(it, r, sc[2][:, 0:2 * P], 1).then_inc(reduced, 1)
                    ge(dve, scored, it, 24, 3 * r + 3)
                    largest(it, r, sc[1][:, 0:3 * P], 2)
                    largest(it, r, sc[1][:, 3 * P:S], 0).then_inc(reduced, 1)
                    ge(dve, reduced, it, 24, 3 * r + 3)
                    ge(dve, turned, it, 8, r - 1)
                    dve.tensor_copy(mxr[:, r % 2, :], mx[:, r % 2, :]).then_inc(maxed, 1)

            dve.memset(km[KR:KR + 1, :, :].bitcast(F32), 1.0).then_inc(rows_set, 1)
            if not two:
                dve.memset(km[32:KR, :, :].bitcast(F32), 0.0).then_inc(rows_set, 1)
            if two:
                split(0, 0)
            steps(dve, step, HEADS - 1, PASSES - 1 if two else PASSES)
            dve.wait_ge(first_in, 16 if two else 32 * DC)
            if two:
                dve.reciprocal(rec[:, :], rec[:, :]).then_inc(inverted, 1)
            else:
                for m in range(DC):
                    dve.reciprocal(c.rT[:, 0, m, :], c.rT[:, 0, m, :]).then_inc(inverted, 1)

class Tally:

    def __init__(self, sem):
        self.sem, self.n = sem, 0

    def add(self, instruction, by=1):
        self.n += by
        instruction.then_inc(self.sem, by)
        return self.n


def inverse_root(dve, r, cols, tick, rooted, n):
    v, root, inv, out = (r[:, i, cols] for i in range(4))
    dve.wait_ge(rooted, n)
    k = tick.add(dve.reciprocal(inv, root))
    dve.wait_ge(tick.sem, k)
    k = tick.add(dve.tensor_mul(out, inv, inv))
    dve.wait_ge(tick.sem, k)
    k = tick.add(dve.tensor_mul(out, out, v))
    dve.wait_ge(tick.sem, k)
    k = tick.add(dve.tensor_scalar(out, out, -0.5, 1.5, ALU.mult, ALU.add))
    dve.wait_ge(tick.sem, k)
    k = tick.add(dve.tensor_mul(out, out, inv))
    dve.wait_ge(tick.sem, k)


def project2(nc, c, t):
    a = Alloc(nc, "p2")
    with a.stack:
        oT, rT, x, wo, bo, g1, bqk, bv = c.oT, c.rT, c.x, c.wo, c.bo, c.g1, c.bqk, c.bv
        srec = a.sb("srec", [(B - 1) * H, S])
        x1, xn = a.sb("x1", [P, 2, SB, D]), a.sb("xn", [P, 2, SB, D])
        sq = a.sb("sq", [P, D])
        stats, mv = a.sb("stats", [P, TILES, 6]), a.sb("mv", [P, TILES, 2])
        r1, r2 = a.sb("r1", [P, 4, TILES]), a.sb("r2", [P, 4, TILES])
        ssum = a.sb("ssum", [P, TILES])
        shift = a.sb("shift", [P, TILES])
        xh, xlo = a.sb("xh", [P, DC, 2, S], F32R), a.sb("xlo", [P, DC, 2, S], F32R)
        wh = [a.sb(f"wh{i}", [P, DC, W2], F32R) for i in range(3)]
        wl = [a.sb(f"wl{i}", [P, DC, W2], F32R) for i in range(3)]
        bvp, ones = a.sb("bvp", [33, W2], F32R), a.sb("ones", [33, P], F32R)
        prod = a.sb("prod", [P, 2, 4, S])
        ROT = 4
        rot = a.sb("rot", [P, ROT, 2, S])
        vout = a.sb("vout", [P, 2, W2])
        op = [a.ps("op0"), a.ps("op1")]
        vb = [a.ps("vb0"), a.ps("vb1")]
        ub = [a.ps(f"ub{i}") for i in range(4)]

        s_in, r_out, small_in = a.sem("s_in"), a.sem("r_out"), c.small_in
        o_in = [a.sem(f"o_in{i}") for i in range(B)]
        x_in = [a.sem(f"x_in{i}") for i in range(B)]
        srec_done, xb_done = a.sem("srec_done"), a.sem("xb_done")
        projected, x1_done, xn_done, root_asked, rooted, squared = (a.sem(n) for n in (
            "projected", "x1_done", "xn_done", "root_asked", "rooted", "squared"))
        t_done, h_copied, parts_done, split_h, split_l = (a.sem(n) for n in (
            "t_done", "h_copied", "parts_done", "split_h", "split_l"))
        unit_done, prods, rotated = (a.sem(n) for n in ("unit_done", "prods", "rotated"))
        xf_done = a.sem("xf_done")
        bias_set, shifted = a.sem("bias_set"), a.sem("shifted")
        v_mul, v_full, tick_s = a.sem("v_mul"), a.sem("v_full"), a.sem("tick")
        u_out = [a.sem(f"u_out{i}") for i in range(ROT)]
        v_out = [a.sem(f"v_out{i}") for i in range(2)]
        r_st = [a.sem(f"resid_out{i}") for i in range(2)]
        block = a.stack.enter_context(nc.Block())
        UNITS = 8

        def flat(x):
            return x.rearrange("p i d -> p (i d)")

        @block.sync
        def _(sp):
            sp.dma_start(srec[:, :], t["o1"][SB:, :, D1, :].rearrange("q h n -> (q h) n")).then_inc(s_in, 16)

            def load(b):
                if b >= 2:
                    sp.wait_ge(projected, SB * (b - 1))
                    sp.wait_ge(x1_done, SB * (b - 1))
                sp.dma_start(x[:, b % 2, :, :], t["x"][b].rearrange("(s p) d -> p s d", p=P)).then_inc(x_in[b], 16)
                for m in range(DC):
                    q = SB * b + 2 * m
                    sp.dma_start(oT[:, b % 2, m, :], t["o1"][q:q + 2, :, 0:D1, :].rearrange("q h d n -> (q h) d n")).then_inc(o_in[b], 16)
                    if b == 1 and m == 0:
                        sp.wait_ge(srec_done, 1)
                        sp.dma_start(t["r1"][SB:].rearrange("q h n -> (q h) n"), srec[:, :]).then_inc(r_out, 16)
                        sp.wait_ge(r_out, 16)
                    heads = t["r1"][q:q + 2].rearrange("q h (o n) -> (q h) o n", o=1)
                    sp.dma_start(rT[:, b % 2, m, :], heads.to_broadcast([8, D1, S])).then_inc(o_in[b], 16)

            def store(b):
                sp.wait_ge(xn_done, SB * (b + 1))
                for src, name in ((x1, "x1"), (xn, "xn")):
                    sp.dma_start(t[name][SB * b:SB * b + SB].rearrange("s p d -> p s d"), src[:, b % 2, :, :])\
                      .then_inc(r_st[b % 2], 16)

            load(1)
            store(0)
            for b in range(B):
                if b + 2 < B:
                    load(b + 2)
                for u in range(UNITS * b, UNITS * b + UNITS):
                    g, is_k = u % UNITS // 2, u % 2
                    dst = t["ks2" if is_k else "qs2"][b * H + 4 * g:b * H + 4 * g + 4]
                    for half in range(2):
                        sp.wait_ge(rotated, 2 * u + half + 1)
                        sp.dma_start(dst[:, 32 * half:32 * half + 32, :], rot[:, u % ROT, half, :]).then_inc(u_out[u % ROT], 16)
                    if u % 2 == 0:
                        continue
                    i = u // 2
                    sp.wait_ge(v_full, 2 * (i + 1))
                    sp.dma_start(t["vs2"][SB * b:SB * b + SB, P * (i % SB):P * (i % SB) + P, :].rearrange("g p d -> p g d"),
                                 vout[:, i % 2, :].rearrange("p (g d) -> p g d", g=4)).then_inc(v_out[i % 2], 16)
                if b + 1 < B:
                    store(b + 1)
            for i in range(2):
                sp.wait_ge(r_st[i], 16 * 2 * B // 2)
                sp.wait_ge(v_out[i], 16 * TILES // 2)
            for i in range(ROT):
                sp.wait_ge(u_out[i], 16 * 2 * UNITS * B // ROT)

        @block.scalar
        def _(act):
            def high_weight(i):
                act.activation(wh[i][:, :, :], c.wqkv[:, i, :, :], ACT.Copy).then_inc(split_h, 1)

            def aside(b, n):
                cols = slice(SB * b, SB * b + SB)
                if n == 3:
                    act.wait_ge(root_asked, 2 * b + 1)
                    act.activation(r1[:, 1, cols], r1[:, 0, cols], ACT.Sqrt).then_inc(rooted, 1)
                if n == 4:
                    act.wait_ge(shifted, b + 1)
                    if b >= 2:
                        act.wait_ge(r_st[b % 2], 32 * (b // 2))
                    for i in range(SB):
                        m = SB * b + i
                        act.activation(xn[:, b % 2, i, :], x1[:, b % 2, i, :], ACT.Identity, bias=shift[:, m:m + 1],
                                       scale=r1[:, 3, m:m + 1]).then_inc(xf_done, 1)
                    for i in range(SB):
                        m = SB * b + i
                        act.wait_ge(xf_done, m + 1)
                        if m:
                            act.wait_ge(squared, m)
                        act.activation(sq[:, :], xn[:, b % 2, i, :], ACT.Square, accum_out=ssum[:, m:m + 1]).then_inc(squared, 1)
                if n == 5:
                    act.wait_ge(root_asked, 2 * b + 2)
                    act.activation(r2[:, 1, cols], r2[:, 0, cols], ACT.Sqrt).then_inc(rooted, 1)

            def parts(b):
                for k in range(DC):
                    act.wait_ge(t_done, DC * b + k + 1)
                    act.activation(xh[:, k, b % 2, :], op[k][:, :], ACT.Copy).then_inc(h_copied, 1)

            def value_half(n):
                i, half = n // 2, n % 2
                act.wait_ge(v_mul, n + 1)
                if i >= 2 and not half:
                    act.wait_ge(v_out[i % 2], 16 * (i // 2))
                act.activation(vout[:, i % 2, S * half:S * half + S], vb[half][:, :], ACT.Copy).then_inc(v_full, 1)

            act.wait_ge(c.wqkv_in, 16 * 3)
            for i in range(3):
                high_weight(i)
            for n in range(3, 6):
                aside(0, n)
            parts(0)
            for b in range(B):
                for n in range(UNITS):
                    if n == UNITS - 1 and b + 1 < B:
                        parts(b + 1)
                    value_half(UNITS * b + n)
                    if b + 1 < B:
                        aside(b + 1, n)

        @block.tensor
        def _(pe):
            def outputs(b):
                pe.wait_ge(small_in, 16 * 7)
                for i in range(SB):
                    n = SB * b + i
                    bank = op[i // 2]
                    for m in range(DC):
                        pe.wait_ge(c.o_scaled, DC * b + m + 1)
                        if n >= SB and i % 2 == 0 and m == 0:
                            pe.wait_ge(x1_done, n - 2)
                        mm = pe.matmul(bank[:, D * (i % 2):D * (i % 2) + D], oT[:, b % 2, m, P * i:P * i + P],
                                       wo[:, m, :], start=(m == 0), stop=(m == DC - 1))
                    mm.then_inc(projected, 1)

            def turn(b):
                pe.wait_ge(xn_done, SB * (b + 1))
                for k in range(DC):
                    for i in range(SB):
                        mm = pe.transpose(op[k][:, P * i:P * i + P], xn[:, b % 2, i, P * k:P * k + P], c.ident[:, :])
                    mm.then_inc(t_done, 1)

            def unit(u):
                b, g, i = u // UNITS, u % UNITS // 2, u % 2
                if u < 2:
                    pe.wait_ge(split_l, i + 1)
                if u >= 2:
                    pe.wait_ge(prods, 4 * (u - 1))
                for half in range(2):
                    cols = slice(2 * P * g + P * half, 2 * P * g + P * half + P)
                    bank = ub[2 * (u % 2) + half]
                    n = 0
                    for k in range(DC):
                        for wt, xt in ((wh[i], xh), (wh[i], xlo), (wl[i], xh)):
                            mm = pe.matmul(bank[:, :], wt[:, k, cols], xt[:, k, b % 2, :], start=(n == 0), stop=(n == 5))
                            n += 1
                mm.then_inc(unit_done, 1)

            def value_half(n):
                i, half = n // 2, n % 2
                b, cols = i // SB, slice(S * half, S * half + S)
                toks = slice(P * (i % SB), P * (i % SB) + P)
                if n == 0:
                    pe.wait_ge(split_l, 3)
                    pe.wait_ge(bias_set, 4)
                if n >= 2:
                    pe.wait_ge(v_full, n - 1)
                pe.matmul(vb[half][:, :], ones[:, :], bvp[:, cols], start=True, stop=False)
                for k in range(DC):
                    for xt, wt in ((xh, wh[2]), (xh, wl[2]), (xlo, wh[2])):
                        mm = pe.matmul(vb[half][:, :], xt[:, k, b % 2, toks], wt[:, k, cols], start=False,
                                       stop=(k == DC - 1 and wt is wh[2] and xt is xlo))
                mm.then_inc(v_mul, 1)

            outputs(0)
            turn(0)
            for b in range(B):
                pe.wait_ge(parts_done, DC * (b + 1))
                for n in range(UNITS):
                    unit(UNITS * b + n)
                    if n == UNITS - 1 and b + 1 < B:
                        turn(b + 1)
                    value_half(UNITS * b + n)
                    if n == 1 and b + 1 < B:
                        outputs(b + 1)

        @block.gpsimd
        def _(pool):
            def aside(b, n):
                if n == 0:
                    pool.wait_ge(o_in[b], 16 * 2 * DC)
                    for m in range(DC):
                        pool.tensor_tensor(oT[:, b % 2, m, :], oT[:, b % 2, m, :], rT[:, b % 2, m, :], ALU.mult).then_inc(c.o_scaled, 1)
                if n == 1:
                    if b:
                        pool.wait_ge(x_in[b], 16)
                    else:
                        pool.wait_ge(small_in, 16 * 7)
                    for i in range(SB):
                        pool.tensor_tensor(x[:, b % 2, i, :], x[:, b % 2, i, :], bo[:, :], ALU.add).then_inc(xb_done, 1)

            def unit(u):
                if u >= ROT:
                    pool.wait_ge(u_out[u % ROT], 32 * (u // ROT))
                for half, op in ((0, ALU.subtract), (1, ALU.add)):
                    pool.wait_ge(prods, 4 * u + 2 * half + 2)
                    pool.tensor_tensor(rot[:, u % ROT, half, :], prod[:, u % 2, 2 * half, :], prod[:, u % 2, 2 * half + 1, :], op)\
                        .then_inc(rotated, 1)

            def low_weight(i):
                pool.wait_ge(split_h, i + 1)
                pool.tensor_tensor(wl[i][:, :, :], c.wqkv[:, i, :, :], wh[i][:, :, :].bitcast(F32), ALU.subtract).then_inc(split_l, 1)

            pool.memset(ones[:, :].bitcast(F32), 1.0).then_inc(bias_set, 1)
            pool.wait_ge(bias_set, 1)
            pool.memset(bvp[:, :].bitcast(F32), 0.0).then_inc(bias_set, 1)
            aside(0, 1)
            for i in range(3):
                low_weight(i)
            for b in range(B):
                for n in range(UNITS):
                    unit(UNITS * b + n)
                    if b + 1 < B:
                        aside(b + 1, n)

        @block.vector
        def _(dve):
            tick = Tally(tick_s)

            def aside(b, n):
                cols = slice(SB * b, SB * b + SB)
                if n in (2, 3):
                    if n == 2 and b >= 2:
                        dve.wait_ge(r_st[b % 2], 32 * (b // 2))
                    dve.wait_ge(projected, SB * b + 2 * (n - 2) + 2)
                    m = SB * b + 2 * (n - 2)
                    dve.wait_ge(xb_done, m + 2)
                    dve.tensor_add(flat(x1[:, b % 2, 2 * (n - 2):2 * (n - 2) + 2, :]), op[n - 2][:, :],
                                   flat(x[:, b % 2, 2 * (n - 2):2 * (n - 2) + 2, :])).then_inc(x1_done, 2)
                    dve.wait_ge(x1_done, m + 2)
                    for i in range(m, m + 2):
                        k = tick.add(dve.bn_stats(stats[:, i, :], x1[:, b % 2, i % SB, :]))
                    dve.wait_ge(tick_s, k)
                    for i in range(m, m + 2):
                        k = tick.add(dve.bn_aggr(mv[:, i, :], stats[:, i, :]))
                    dve.wait_ge(tick_s, k)
                if n == 3:
                    dve.tensor_scalar(r1[:, 0, cols], mv[:, cols, 1], EPS, None, ALU.add).then_inc(root_asked, 1)
                if n == 4:
                    dve.wait_ge(root_asked, 2 * b + 1)
                    inverse_root(dve, r1, cols, tick, rooted, 2 * b + 1)
                    dve.scalar_tensor_tensor(out=shift[:, cols], in0=mv[:, cols, 0], scalar=-1.0, in1=r1[:, 3, cols],
                                             op0=ALU.mult, op1=ALU.mult).then_inc(shifted, 1)
                if n == 5:
                    dve.wait_ge(squared, SB * (b + 1))
                    dve.tensor_scalar(r2[:, 0, cols], ssum[:, cols], 1.0 / D, EPS, ALU.mult, ALU.add).then_inc(root_asked, 1)
                if n == 6:
                    dve.wait_ge(root_asked, 2 * b + 2)
                    inverse_root(dve, r2, cols, tick, rooted, 2 * b + 2)
                    for i in range(SB):
                        m = SB * b + i
                        dve.scalar_tensor_tensor(out=xn[:, b % 2, i, :], in0=xn[:, b % 2, i, :], scalar=r2[:, 3, m:m + 1],
                                                 in1=g1[:, :], op0=ALU.mult, op1=ALU.mult).then_inc(xn_done, 1)

            def parts(b):
                for k in range(DC):
                    dve.wait_ge(h_copied, DC * b + k + 1)
                    dve.tensor_sub(xlo[:, k, b % 2, :], op[k][:, :], xh[:, k, b % 2, :].bitcast(F32)).then_inc(parts_done, 1)

            def unit(u):
                g, is_k = u % UNITS // 2, u % 2
                dve.wait_ge(unit_done, u + 1)
                cos, sin = (c.cos, c.sin) if is_k else (c.cos_q, c.sin_q)
                for n, (half, table) in enumerate(((0, cos), (1, sin), (0, sin), (1, cos))):
                    if u >= 2:
                        dve.wait_ge(rotated, 2 * (u - 2) + n // 2 + 1)
                    dve.scalar_tensor_tensor(out=prod[:, u % 2, n, :], in0=ub[2 * (u % 2) + half][:, :],
                                             scalar=bqk[:, is_k, 2 * g + half:2 * g + half + 1], in1=table[:, :],
                                             op0=ALU.add, op1=ALU.mult).then_inc(prods, 1)

            dve.wait_ge(small_in, 16 * 7)
            dve.wait_ge(bias_set, 2)
            dve.tensor_copy(bvp[0:1, :], bv[:, :]).then_inc(bias_set, 1)
            dve.wait_ge(bias_set, 3)
            dve.tensor_sub(bvp[32:33, :], bv[:, :], bvp[0:1, :].bitcast(F32)).then_inc(bias_set, 1)
            for n in range(2, 5):
                aside(0, n)
            dve.wait_ge(s_in, 16)
            dve.reciprocal(srec[:, :], srec[:, :]).then_inc(srec_done, 1)
            for n in range(5, 7):
                aside(0, n)
            parts(0)
            for b in range(B):
                for n in range(UNITS):
                    if n == UNITS - 1 and b + 1 < B:
                        parts(b + 1)
                    if n == 6 and b + 1 < B:
                        aside(b + 1, n)
                    unit(UNITS * b + n)
                    if n < 6 and b + 1 < B:
                        aside(b + 1, n)



def mix(nc, c, t):
    a = Alloc(nc, "mx")
    with a.stack:
        CH = W2 // P
        RING = 5
        srec = a.sb("srec", [P, (B - EARLY) * H * S // P])
        oT, rT = a.sb("oT", [P, RING, S]), a.sb("rT", [P, RING, S])
        ow = c.ow
        ob, g2, sb2 = (a.sb(n, [P, D]) for n in ("ob", "g2", "sb2"))
        rb, sb1 = a.sb("rb", [P, E]), a.sb("sb1", [P, FF // P])
        rw = a.sb("rw", [P, DC, E])
        sw1, sw2 = a.sb("sw1", [P, DC, FF]), a.sb("sw2", [P, FF // P, D])
        ao, an = a.sb("ao", [P, 2, SB, D]), a.sb("an", [P, 2, SB, D])
        ssum, r2 = a.sb("ssum", [P, TILES]), a.sb("r2", [P, 4, TILES])
        anT = a.sb("anT", [P, DC, S])
        hid = a.sb("hid", [P, FF // P, S])
        op, tp, hp, yp = ([a.ps(f"{n}{i}") for i in range(2)] for n in ("op", "tp", "hp", "yp"))
        s_in, srec_done, r_out, small_in = (a.sem(n) for n in ("s_in", "srec_done", "r_out", "small_in"))
        x1_in = [a.sem(f"x1_in{i}") for i in range(B)]
        o_in = [a.sem(f"o_in{i}") for i in range(RING)]
        xn_in = [a.sem(f"xn_in{i}") for i in range(2)]
        an_out = [a.sem(f"an_out{i}") for i in range(2)]
        o_scaled, chunk_done, xb_done, ao_done, squared, root_asked, rooted, an_done = (a.sem(n) for n in (
            "o_scaled", "chunk_done", "xb_done", "ao_done", "squared", "root_asked", "rooted", "an_done"))
        t_done, t_copied, l_mul, l_done, h_mul, h_done, y_mul, y_done, base_step, tick_s = (a.sem(n) for n in (
            "t_done", "t_copied", "l_mul", "l_done", "h_mul", "h_done", "y_mul", "y_done", "base_step", "tick"))
        block = a.stack.enter_context(nc.Block())
        NSMALL = 8
        TURN = CH - 3
        MID = CH // 2

        def flat(x):
            return x.rearrange("p i d -> p (i d)")

        @block.sync
        def _(sp):
            last = EARLY * SB

            def spread(x):
                return x[last:].rearrange("q h n -> (q h n)").rearrange("(p n) -> p n", p=P)

            sp.wait_ge(c.r2_out, 16)

            def batch(b):
                for g in range(CH * b, CH * b + CH):
                    if g == CH * b + MID:
                        if b >= 2:
                            sp.wait_ge(base_step, 3 * (b - 1))
                        sp.dma_start(ao[:, b % 2, :, :], t["xn"][SB * b:SB * b + SB].rearrange("s p d -> p s d"))\
                          .then_inc(xn_in[b % 2], 16)
                    if g >= RING:
                        sp.wait_ge(chunk_done, g - RING + 1)
                    sp.dma_start(oT[:, g % RING, :], t["o2"][g]).then_inc(o_in[g % RING], 16)
                    if g == MID - 1:
                        sp.dma_start(srec[:, :], spread(t["s2"])).then_inc(s_in, 16)
                    if g == CH:
                        sp.wait_ge(srec_done, 1)
                        sp.dma_start(spread(t["r2"]), srec[:, :]).then_inc(r_out, 16)
                    if g == CH * EARLY:
                        sp.wait_ge(r_out, 16)
                    for h in range(2):
                        sp.dma_start(rT[D2 * h:D2 * h + D2, g % RING, :],
                                     t["r2"][g // 2, 2 * (g % 2) + h:2 * (g % 2) + h + 1, :].to_broadcast([D2, S]))\
                          .then_inc(o_in[g % RING], 16)

            batch(0)
            for b in range(B):
                if b + 1 < B:
                    batch(b + 1)
                sp.wait_ge(an_done, SB * (b + 1))
                sp.dma_start(t["an"][P * SB * b:P * SB * (b + 1), :].rearrange("(s p) d -> p s d", p=P), an[:, b % 2, :, :])\
                  .then_inc(an_out[b % 2], 16)
            for i in range(2):
                sp.wait_ge(an_out[i], 16 * B // 2)

        @block.scalar
        def _(act):
            act.wait_ge(o_scaled, 2)
            for dst, name, pat in ((rw, "L0_ffn_router_w", "(k p) n -> p k n"),
                                   (sw1, "L0_ffn_sh_w1", "(k p) n -> p k n"), (sw2, "L0_ffn_sh_w2", "(k p) n -> p k n")):
                act.dma_start(dst[:, :, :], t[name].rearrange(pat, p=P)).then_inc(small_in, 16)
            for dst, name in ((ob, "L0_ffn_o_b"), (g2, "L0_ffn_gamma2"), (sb2, "L0_ffn_sh_b2"), (rb, "L0_ffn_router_b")):
                act.dma_start(dst[:, :], t[name].to_broadcast([P, dst.shape[1]])).then_inc(small_in, 16)
            act.dma_start(sb1[:, :], t["L0_ffn_sh_b1"]).then_inc(small_in, 16)

            def load_x1(b):
                act.dma_start(c.base[:, SB * b:SB * b + SB, :], t["x1"][SB * b:SB * b + SB].rearrange("s p d -> p s d"))\
                   .then_inc(x1_in[b], 16)

            def load_w2(n):
                lo, hi = 2 * n, min(2 * n + 2, E)
                for m in range(FF // P):
                    act.dma_start(c.w2[:, lo:hi, m, :], t["L0_ffn_re_w2"][lo:hi, P * m:P * m + P, :].rearrange("e p n -> p e n"))\
                       .then_inc(c.w2_in, 16)

            def pre(b):
                for i in range(SB):
                    n = SB * b + i
                    act.wait_ge(ao_done, 2 * b + i // 2 + 1)
                    if b >= 2 and i == 0:
                        act.wait_ge(an_out[b % 2], 16 * (b // 2))
                        act.wait_ge(base_step, 3 * (b - 1))
                    act.activation(an[:, b % 2, i, :], ao[:, b % 2, i, :], ACT.Square, accum_out=ssum[:, n:n + 1]).then_inc(squared, 1)
                act.wait_ge(root_asked, b + 1)
                cols = slice(SB * b, SB * b + SB)
                act.activation(r2[:, 1, cols], r2[:, 0, cols], ACT.Sqrt).then_inc(rooted, 1)

            def post(b):
                for k in range(DC):
                    act.wait_ge(t_done, DC * b + k + 1)
                    if b:
                        act.wait_ge(h_mul, 2 * b)
                    act.activation(anT[:, k, :], tp[k][:, :], ACT.Copy).then_inc(t_copied, 1)
                for m in range(FF // P):
                    act.wait_ge(h_mul, 2 * b + m + 1)
                    if b:
                        act.wait_ge(y_mul, 2 * b)
                    act.activation(hid[:, m, :], hp[m][:, :], ACT.Gelu, bias=sb1[:, m:m + 1]).then_inc(h_done, 1)

            pre(0)
            for b in range(B):
                load_x1(b)
                post(b)
                load_w2(4 * b)
                load_w2(4 * b + 1)
                load_w2(4 * b + 2)
                load_w2(4 * b + 3)
                if b + 1 < B:
                    pre(b + 1)

        @block.tensor
        def _(pe):
            def turn(b):
                pe.wait_ge(an_done, SB * (b + 1))
                if b:
                    pe.wait_ge(l_done, b)
                else:
                    pe.wait_ge(small_in, 16 * NSMALL)
                for k in range(DC):
                    for i in range(SB):
                        mm = pe.transpose(tp[k][:, P * i:P * i + P], an[:, b % 2, i, P * k:P * k + P], c.ident[:, :])
                    mm.then_inc(t_done, 1)

            def hidden(b):
                for k in range(DC):
                    pe.wait_ge(t_copied, DC * b + k + 1)
                    for m in range(FF // P):
                        if b and not k:
                            pe.wait_ge(h_done, 2 * (b - 1) + m + 1)
                        mm = pe.matmul(hp[m][:, :], sw1[:, k, P * m:P * m + P], anT[:, k, :],
                                       start=(k == 0), stop=(k == DC - 1))
                        if k == DC - 1:
                            mm.then_inc(h_mul, 1)

            def logits(b):
                for i in range(SB):
                    for k in range(DC):
                        mm = pe.matmul(tp[0][:, 32 * i:32 * i + E], anT[:, k, P * i:P * i + P], rw[:, k, :],
                                       start=(k == 0), stop=(k == DC - 1))
                mm.then_inc(l_mul, 1)

            def shared(b):
                for j in range(2):
                    if b:
                        pe.wait_ge(y_done, 2 * (b - 1) + j + 1)
                    for i in (2 * j, 2 * j + 1):
                        for m in range(FF // P):
                            pe.wait_ge(h_done, 2 * b + m + 1)
                            mm = pe.matmul(yp[j][:, D * (i % 2):D * (i % 2) + D], hid[:, m, P * i:P * i + P], sw2[:, m, :],
                                           start=(m == 0), stop=(m == FF // P - 1))
                    mm.then_inc(y_mul, 1)

            pe.wait_ge(c.ow_in, 16)
            for b in range(B + 1):
                if b and b < B:
                    pe.wait_ge(ao_done, 2 * b)
                for m in range(CH):
                    if b and m == TURN:
                        turn(b - 1)
                    if b and m == CH - 1:
                        hidden(b - 1)
                        logits(b - 1)
                    if b == B:
                        continue
                    g = CH * b + m
                    pe.wait_ge(o_scaled, g + 1)
                    for i in range(SB):
                        mm = pe.matmul(op[i // 2][:, D * (i % 2):D * (i % 2) + D], oT[:, g % RING, P * i:P * i + P],
                                       ow[:, m, :], start=(m == 0 and i % 2 == 0), stop=(m == CH - 1 and i % 2 == 1))
                    mm.then_inc(chunk_done, 1)
                if b:
                    shared(b - 1)

        @block.gpsimd
        def _(pool):
            def bias(b):
                if b == 0:
                    pool.wait_ge(small_in, 16 * NSMALL)
                pool.wait_ge(xn_in[b % 2], 16 * (b // 2 + 1))
                for j in range(SB):
                    pool.tensor_tensor(ao[:, b % 2, j, :], ao[:, b % 2, j, :], ob[:, :], ALU.add).then_inc(xb_done, 1)

            def scale(b):
                for g in range(CH * b, CH * b + CH):
                    if g == CH * b + CH - 2:
                        bias(b)
                    pool.wait_ge(o_in[g % RING], 48 * (g // RING + 1))
                    pool.tensor_tensor(oT[:, g % RING, :], oT[:, g % RING, :], rT[:, g % RING, :], ALU.mult).then_inc(o_scaled, 1)

            for b in range(B):
                scale(b)

        @block.vector
        def _(dve):
            tick = Tally(tick_s)
            dve.wait_ge(s_in, 16)
            dve.reciprocal(srec[:, :], srec[:, :]).then_inc(srec_done, 1)
            dve.wait_ge(small_in, 16 * NSMALL)

            def outputs(b):
                dve.wait_ge(chunk_done, CH * (b + 1))
                dve.wait_ge(xb_done, SB * (b + 1))
                for j in range(2):
                    tiles = flat(ao[:, b % 2, 2 * j:2 * j + 2, :])
                    dve.tensor_add(tiles, tiles, op[j][:, :]).then_inc(ao_done, 1)

            def norm(b):
                cols = slice(SB * b, SB * b + SB)
                dve.wait_ge(squared, SB * (b + 1))
                dve.tensor_scalar(r2[:, 0, cols], ssum[:, cols], 1.0 / D, EPS, ALU.mult, ALU.add).then_inc(root_asked, 1)
                dve.wait_ge(root_asked, b + 1)
                inverse_root(dve, r2, cols, tick, rooted, b + 1)
                for i in range(SB):
                    n = SB * b + i
                    dve.scalar_tensor_tensor(out=an[:, b % 2, i, :], in0=ao[:, b % 2, i, :], scalar=r2[:, 3, n:n + 1],
                                             in1=g2[:, :], op0=ALU.mult, op1=ALU.mult).then_inc(an_done, 1)

            def base(b):
                tiles = c.base[:, SB * b:SB * b + SB, :]
                dve.wait_ge(x1_in[b], 16)
                dve.tensor_tensor(tiles, tiles, sb2[:, :].rearrange("p (o d) -> p o d", o=1).to_broadcast([P, SB, D]), ALU.add)\
                   .then_inc(base_step, 1)
                dve.wait_ge(base_step, 3 * b + 1)
                dve.tensor_add(flat(tiles), flat(tiles), flat(ao[:, b % 2, :, :])).then_inc(base_step, 1)
                dve.wait_ge(base_step, 3 * b + 2)
                dve.tensor_add(flat(tiles), flat(tiles), flat(an[:, b % 2, :, :])).then_inc(base_step, 1)

            def logits(b):
                dve.wait_ge(l_mul, b + 1)
                dve.tensor_tensor(c.logits[:, SB * b:SB * b + SB, :],
                                  tp[0][:, 0:32 * SB].rearrange("p (i e) -> p i e", e=32)[:, :, 0:E],
                                  rb[:, :].rearrange("p (o e) -> p o e", o=1).to_broadcast([P, SB, E]), ALU.add).then_inc(l_done, 1)

            def shared(b):
                dve.wait_ge(base_step, 3 * (b + 1))
                for j in range(2):
                    tiles = flat(c.base[:, SB * b + 2 * j:SB * b + 2 * j + 2, :])
                    dve.wait_ge(y_mul, 2 * b + j + 1)
                    dve.tensor_add(tiles, tiles, yp[j][:, :]).then_inc(y_done, 1)

            for b in range(B + 1):
                if b:
                    base(b - 1)
                    logits(b - 1)
                if b < B:
                    outputs(b)
                    norm(b)
                if b:
                    shared(b - 1)



def route(nc, c, t):
    a = Alloc(nc, "rt")
    with a.stack:
        IX = NT + 2
        lg, ex, pos = (a.sb(n, [P, TILES, E]) for n in ("lg", "ex", "pos"))
        mx, tot, inv = (a.sb(n, [P, TILES]) for n in ("mx", "tot", "inv"))
        idx = a.sb("idx", [P, TILES, 8], U32)
        idxf = a.sb("idxf", [P, TILES, TOPK])
        oh, picked = c.oh, a.sb("picked", [P, TOPK, TILES, E])
        member = a.sb("member", [P, TILES, E], BF16)
        counts = a.sb("counts", [P, E])
        over = a.sb("over", [P, E, TILES])
        nt, ct, start = (a.sb(n, [P, E]) for n in ("nt", "ct", "start"))
        tri = a.sb("tri", [P, E, E])
        spread = a.sb("spread", [P, E, E])
        slotf, rowf, tilef = (a.sb(n, [P, TOPK, TILES]) for n in ("slotf", "rowf", "tilef"))
        sloti, rowi, tilei = (a.sb(n, [P, TOPK, TILES], I32) for n in ("sloti", "rowi", "tilei"))
        e_no, j_no, t_no, row_no, p_no = (a.sb(n, s, I32) for n, s in (
            ("e_no", [P, E]), ("j_no", [P, TILES]), ("t_no", [P, TILES]), ("row_no", [P, P]), ("p_no", [P, 1])))
        e_nof, j_nof, t_nof, row_nof, p_nof = (a.sb(n + "f", s) for n, s in (
            ("e_no", [P, E]), ("j_no", [P, TILES]), ("t_no", [P, TILES]), ("row_no", [P, P]), ("p_no", [P, 1])))
        upper, ones = a.sb("upper", [P, P], BF16), a.sb("ones", [P, P], BF16)
        hot_row, hot_tile = a.sb("hot_row", [P, 4, P], F32R), a.sb("hot_tile", [P, 4, NT], F32R)
        of_tile, cmp = a.sb("of_tile", [P, 1]), a.sb("cmp", [P, E])
        rank_b, count_b, ids_b, row_b = (a.ps(n) for n in ("rank", "count", "ids", "row"))
        set_up, numbers, exped, tick_s, member_done, ranked, hot_r, hot_t, hot_tp, placed = (a.sem(n) for n in (
            "set_up", "numbers", "exped", "tick", "member_done", "ranked", "hot_r", "hot_t", "hot_tp", "placed"))
        l_ready, tile_of, rowed = (a.sem(n) for n in ("l_ready", "tile_of", "rowed"))
        slots_known = a.sem("slots_known")
        block = a.stack.enter_context(nc.Block())
        STEPS = TOPK * TILES

        def over_tiles(x, n=TILES):
            return x.rearrange("p (o e) -> p o e", o=1).to_broadcast([P, n, E])

        def over_experts(x):
            return x.rearrange("p (i o) -> p i o", o=1).to_broadcast([P, TILES, E])

        def by_pool(n):
            return n % 3 == 2

        def make_hot_tile(eng, n):
            k, i = n // TILES, n % TILES
            return eng.tensor_scalar(hot_tile[:, n % 4, :], row_nof[:, 0:NT], tilef[:, k, i:i + 1], t_nof[:, i:i + 1],
                                     ALU.is_equal, ALU.mult)

        @block.gpsimd
        def _(pool):
            pool.iota(e_no[:, :], pattern=[[1, E]], base=0, channel_multiplier=0).then_inc(set_up, 1)
            pool.iota(j_no[:, :], pattern=[[P, TILES]], base=0, channel_multiplier=0).then_inc(set_up, 1)
            pool.iota(t_no[:, :], pattern=[[P, TILES]], base=0, channel_multiplier=1).then_inc(set_up, 1)
            pool.iota(row_no[:, :], pattern=[[1, P]], base=0, channel_multiplier=0).then_inc(set_up, 1)
            pool.iota(p_no[:, :], pattern=[[0, 1]], base=0, channel_multiplier=1).then_inc(set_up, 1)
            for m in (upper[:, :], tri[:, :, :], ones[:, :]):
                pool.wait_ge(set_up, 5)
                pool.memset(m, 1.0).then_inc(set_up, 1)
            pool.wait_ge(set_up, 8)
            pool.affine_select(out=upper[:, :], in_=upper[:, :], compare_op=ALU.is_gt, fill=0.0, base=0,
                               pattern=[[1, P]], channel_multiplier=-1).then_inc(set_up, 1)
            pool.affine_select(out=tri[:, :, :], in_=tri[:, :, :], compare_op=ALU.is_ge, fill=0.0, base=0,
                               pattern=[[1, E], [-1, E]], channel_multiplier=0).then_inc(set_up, 1)
            pool.wait_ge(placed, 1)
            pool.wait_ge(numbers, 5)
            for n in filter(by_pool, range(STEPS)):
                if n >= 4:
                    pool.wait_ge(ranked, n - 2)
                make_hot_tile(pool, n).then_inc(hot_tp, 1)

        @block.scalar
        def _(act):
            act.wait_ge(l_ready, 1)
            act.activation(ex[:, :, :], lg[:, :, :], ACT.Exp).then_inc(exped, 1)

        @block.tensor
        def _(pe):
            pe.wait_ge(set_up, 10)
            pe.wait_ge(member_done, 1)
            pe.matmul(rank_b[:, 0:TILES * E], upper[:, :], member[:, :, :], start=True, stop=False)
            for i in range(TILES - 1):
                mm = pe.matmul(rank_b[:, E * (i + 1):E * TILES], ones[:, :], over_tiles(member[:, i, :], TILES - 1 - i),
                               start=False, stop=(i == TILES - 2))
            for i in range(TILES):
                mm = pe.matmul(count_b[:, 0:E], ones[:, :], member[:, i, :], start=(i == 0), stop=(i == TILES - 1))
            mm.then_inc(ranked, 1)
            pe.wait_ge(tile_of, 1)
            pe.matmul(row_b[0:1, 0:P], of_tile[:, :], c.ident[:, :], start=True, stop=True).then_inc(rowed, 1)
            for n in range(STEPS):
                pe.wait_ge(hot_r, n + 1)
                pe.wait_ge(*((hot_tp, n // 3 + 1) if by_pool(n) else (hot_t, n + 1 - (n + 1) // 3)))
                pe.matmul(ids_b[:, 0:NT], hot_row[:, n % 4, :], hot_tile[:, n % 4, :], start=(n == 0),
                          stop=(n == STEPS - 1)).then_inc(ranked, 1)

        @block.vector
        def _(dve):
            tick = Tally(tick_s)

            def then(instruction):
                dve.wait_ge(tick_s, tick.add(instruction))

            then(dve.tensor_reduce(mx[:, :], c.logits[:, :, :], AX.X, ALU.max))
            dve.tensor_tensor(lg[:, :, :], c.logits[:, :, :], over_experts(mx[:, :]), ALU.subtract).then_inc(l_ready, 1)
            dve.wait_ge(set_up, 10)
            for dst, src in ((e_nof, e_no), (j_nof, j_no), (t_nof, t_no), (row_nof, row_no), (p_nof, p_no)):
                dve.tensor_copy(dst[:, :], src[:, :]).then_inc(numbers, 1)
            dve.wait_ge(exped, 1)
            then(dve.tensor_reduce(tot[:, :], ex[:, :, :], AX.X, ALU.add))
            then(dve.reciprocal(inv[:, :], tot[:, :]))
            then(dve.tensor_tensor(ex[:, :, :], ex[:, :, :], over_experts(inv[:, :]), ALU.mult))
            for i in range(TILES):
                k = tick.add(dve.max(c.gates[:, i, :], ex[:, i, :]))
            dve.wait_ge(tick_s, k)
            for i in range(TILES):
                k = tick.add(dve.max_index(idx[:, i, :], c.gates[:, i, :], ex[:, i, :]))
            dve.wait_ge(tick_s, k)
            then(dve.tensor_copy(idxf[:, :, :], idx[:, :, 0:TOPK]))
            dve.wait_ge(numbers, 5)
            for k in range(TOPK):
                n = tick.add(dve.tensor_tensor(oh[:, k, :, :], over_tiles(e_nof[:, :]), over_experts(idxf[:, :, k]), ALU.is_equal))
            dve.wait_ge(tick_s, n)
            then(dve.tensor_add(member[:, :, :], oh[:, 0, :, :], oh[:, 1, :, :]))
            dve.tensor_add(member[:, :, :], member[:, :, :], oh[:, 2, :, :]).then_inc(member_done, 1)
            dve.wait_ge(ranked, 1)
            then(dve.tensor_copy(counts[:, :], count_b[:, 0:E]))
            then(dve.tensor_tensor(over[:, :, :], counts[:, :].rearrange("p (e o) -> p e o", o=1).to_broadcast([P, E, TILES]),
                                   j_nof[:, :].rearrange("p (o j) -> p o j", o=1).to_broadcast([P, E, TILES]), ALU.is_gt))
            then(dve.tensor_reduce(nt[:, :], over[:, :, :], AX.X, ALU.add))
            then(dve.tensor_tensor(spread[:, :, :], tri[:, :, :], over_tiles(nt[:, :], E), ALU.mult))
            then(dve.tensor_reduce(ct[:, :], spread[:, :, :], AX.X, ALU.add))
            then(dve.tensor_scalar(cmp[:, :], ct[:, :], p_nof[:, 0:1], None, ALU.is_le))
            then(dve.tensor_reduce(of_tile[:, :], cmp[:, :], AX.X, ALU.add))
            dve.tensor_scalar(of_tile[:, :], of_tile[:, :], float(E - 1), None, ALU.min).then_inc(tile_of, 1)
            then(dve.tensor_sub(start[:, :], ct[:, :], nt[:, :]))
            then(dve.tensor_scalar(start[:, :], start[:, :], float(P), None, ALU.mult))
            then(dve.tensor_tensor(pos[:, :, :], rank_b[:, 0:TILES * E].rearrange("p (i e) -> p i e", e=E),
                                   over_tiles(start[:, :]), ALU.add))
            for k in range(TOPK):
                n = tick.add(dve.tensor_tensor(picked[:, k, :, :], oh[:, k, :, :], pos[:, :, :], ALU.mult))
            dve.wait_ge(tick_s, n)
            then(dve.tensor_reduce(slotf[:, :, :], picked[:, :, :, :], AX.X, ALU.add))
            then(dve.tensor_copy(sloti[:, :, :], slotf[:, :, :]))
            k = tick.add(dve.tensor_scalar(rowi[:, :, :], sloti[:, :, :], P - 1, None, ALU.bitwise_and))
            then(dve.tensor_scalar(tilei[:, :, :], sloti[:, :, :], 7, None, ALU.logical_shift_right))
            k = tick.add(dve.tensor_copy(rowf[:, :, :], rowi[:, :, :]))
            then(dve.tensor_copy(tilef[:, :, :], tilei[:, :, :]))
            then(dve.scalar_tensor_tensor(out=slotf[:, :, :], in0=rowf[:, :, :], scalar=float(NT), in1=tilef[:, :, :],
                                          op0=ALU.mult, op1=ALU.add))
            dve.tensor_copy(c.slots[:, :, :], slotf[:, :, :]).then_inc(placed, 1)
            dve.wait_ge(placed, 1)
            for n in range(STEPS):
                k, i = n // TILES, n % TILES
                if n >= 4:
                    dve.wait_ge(ranked, n - 2)
                dve.tensor_scalar(hot_row[:, n % 4, :], row_nof[:, :], rowf[:, k, i:i + 1], None, ALU.is_equal).then_inc(hot_r, 1)
                if not by_pool(n):
                    make_hot_tile(dve, n).then_inc(hot_t, 1)
            dve.wait_ge(rowed, 1)
            dve.tensor_copy(c.experts[:, :], row_b[0:1, 0:P]).then_inc(slots_known, 1)
            dve.wait_ge(ranked, STEPS + 1)
            dve.tensor_copy(c.ids[:, :], ids_b[:, 0:NT]).then_inc(slots_known, 1)
            dve.wait_ge(slots_known, 2)


def experts(nc, c, t):
    a = Alloc(nc, "ex")
    with a.stack:
        MC = FF // P
        PASSES = NT // 4
        PEELED = 2
        idc = a.sb("idc", [P, 4], I32)
        xg = a.sb("xg", [P, 4, D])
        w1 = a.sb("w1", [P, 2, DC * FF + MC])
        xT, hid = a.sb("xT", [P, 2, DC, P]), a.sb("hid", [P, 2, MC, P])
        y = a.sb("y", [P, 4, D])
        tb, hb, yb = ([a.ps(f"{n}{i}") for i in range(2)] for n in ("tb", "hb", "yb"))
        gathered = [a.sem(f"gathered{i}") for i in range(4)]
        stored = [a.sem(f"stored{i}") for i in range(4)]
        id_set, turned, x_copied, w_copied, h_mul, h_done, y_mul, y_copied = (a.sem(n) for n in (
            "id_set", "turned", "x_copied", "w_copied", "h_mul", "h_done", "y_mul", "y_copied"))
        block = a.stack.enter_context(nc.Block())

        def ge(eng, sem, it, per_pass, const):
            if not isinstance(it, int):
                assert PEELED * per_pass + const > 0
                eng.wait_ge(sem, per_pass * it + const)
            elif per_pass * it + const > 0:
                eng.wait_ge(sem, per_pass * it + const)

        def steps(eng, step, last):
            for s in range(4 * PEELED):
                step(s // 4, s % 4)
            with eng.Fori(PEELED, PASSES) as it:
                for r in range(4):
                    step(it, r)
            for r in range(last + 1 - 4 * PASSES):
                step(PASSES, r)

        def there(it, r):
            return not isinstance(it, int) or 0 <= 4 * it + r < NT

        ye = t["ye"].rearrange("(p n) d -> n p d", n=NT)

        @block.gpsimd
        def _(pool):
            def step(it, r):
                sl = r % 4
                ge(pool, turned, it, 4, r - 3)
                pool.tensor_copy(idc[:, sl:sl + 1], c.ids[:, bass.ds(4 * it + r, 1)]).then_inc(id_set, 1)
                ge(pool, id_set, it, 4, r + 1)
                pool.nop(nofuse=True)
                pool.indirect_dma_start(out=xg[:, sl, :], out_offset=None, in_=t["an"],
                                        in_offset=bass.IndirectOffsetOnAxis(ap=idc[:, sl:sl + 1], axis=0)).then_inc(gathered[sl], 16)

            steps(pool, step, NT - 1)

        @block.sync
        def _(sp):
            def step(it, r):
                ge(sp, y_copied, it, 4, r + 1)
                sp.dma_start(ye[4 * it + r], y[:, r % 4, :]).then_inc(stored[r % 4], 16)

            steps(sp, step, NT - 1)
            for i in range(4):
                sp.wait_ge(stored[i], 16 * ((NT - 1 - i) // 4 + 1))

        @block.tensor
        def _(pe):
            def step(it, r):
                if there(it, r):
                    sl = r % 4
                    ge(pe, gathered[sl], it, 16, 16)
                    ge(pe, x_copied, it, 4, r - 1)
                    for k in range(DC):
                        mm = pe.transpose(tb[r % 2][:, P * k:P * k + P], xg[:, sl, P * k:P * k + P], c.ident[:, :])
                    mm.then_inc(turned, 1)
                if there(it, r - 1):
                    n = r - 1
                    ge(pe, x_copied, it, 4, n + 1)
                    ge(pe, w_copied, it, 4, n + 1)
                    ge(pe, h_done, it, 4, n - 1)
                    for m in range(MC):
                        for k in range(DC):
                            mm = pe.matmul(hb[n % 2][:, P * m:P * m + P], w1[:, n % 2, FF * k + P * m:FF * k + P * m + P],
                                           xT[:, n % 2, k, :], start=(k == 0), stop=(k == DC - 1))
                    mm.then_inc(h_mul, 1)
                if there(it, r - 2):
                    n = r - 2
                    e = pe.value_load(c.experts[0:1, bass.ds(4 * it + n, 1)], min_val=0, max_val=E - 1)
                    ge(pe, h_done, it, 4, n + 1)
                    ge(pe, y_copied, it, 4, n - 1)
                    for m in range(MC):
                        mm = pe.matmul(yb[n % 2][:, 0:D], hid[:, n % 2, m, :], c.w2[:, bass.ds(e, 1), m, :],
                                       start=(m == 0), stop=(m == MC - 1))
                    mm.then_inc(y_mul, 1)

            pe.wait_ge(c.w2_in, 16 * MC * ((E + 1) // 2))
            steps(pe, step, NT + 1)

        @block.scalar
        def _(act):
            def step(it, r):
                if there(it, r - 1):
                    n = r - 1
                    ge(act, h_mul, it, 4, n + 1)
                    ge(act, y_mul, it, 4, n - 1)
                    for m in range(MC):
                        mm = act.activation(hid[:, n % 2, m, :], hb[n % 2][:, P * m:P * m + P], ACT.Gelu,
                                            bias=w1[:, n % 2, DC * FF + m:DC * FF + m + 1])
                    mm.then_inc(h_done, 1)
                if there(it, r - 2):
                    n = r - 2
                    ge(act, y_mul, it, 4, n + 1)
                    ge(act, stored[n % 4], it, 16, 16 * (n // 4))
                    act.activation(y[:, n % 4, :], yb[n % 2][:, 0:D], ACT.Copy).then_inc(y_copied, 1)

            steps(act, step, NT + 1)

        @block.vector
        def _(dve):
            def step(it, r):
                e = dve.value_load(c.experts[0:1, bass.ds(4 * it + r, 1)], min_val=0, max_val=E - 1)
                ge(dve, h_done, it, 4, r - 1)
                dve.tensor_copy(w1[:, r % 2, :], c.w1[:, bass.ds(e, 1), :].rearrange("p o n -> p (o n)")).then_inc(w_copied, 1)
                ge(dve, turned, it, 4, r + 1)
                dve.tensor_copy(xT[:, r % 2, :, :].rearrange("p k n -> p (k n)"), tb[r % 2][:, 0:DC * P]).then_inc(x_copied, 1)

            dve.wait_ge(c.w1_in, 16 * c.w1_loads)
            steps(dve, step, NT - 1)


def combine(nc, c, t, out):
    a = Alloc(nc, "cb")
    with a.stack:
        RING = 4
        y = a.sb("y", [P, RING, TOPK, D])
        picked, gate = a.sb("picked", [P, TOPK, TILES, E]), a.sb("gate", [P, TILES, E])
        gateT = a.sb("gateT", [E, TOK])
        b2 = a.sb("b2", [E, D])
        gt_b, bb = ([a.ps(f"{n}{i}") for i in range(2)] for n in ("gt", "bb"))
        gathered = [a.sem(f"gathered{i}") for i in range(RING)]
        summed, out_s, b2_in, tick_s, gate_ready, g_turned, g_copied, b_mul = (a.sem(n) for n in (
            "summed", "out", "b2_in", "tick", "gate_ready", "g_turned", "g_copied", "b_mul"))
        block = a.stack.enter_context(nc.Block())
        ADDS = TOPK + 1

        @block.gpsimd
        def _(pool):
            for i in range(TILES):
                if i >= RING:
                    pool.wait_ge(summed, ADDS * (i - RING + 1))
                for k in range(TOPK):
                    pool.indirect_dma_start(out=y[:, i % RING, k, :], out_offset=None, in_=t["ye"],
                                            in_offset=bass.IndirectOffsetOnAxis(ap=c.slots[:, k, i:i + 1], axis=0))\
                        .then_inc(gathered[i % RING], 16)

        @block.tensor
        def _(pe):
            pe.wait_ge(gate_ready, 1)
            for b in range(B):
                if b >= 2:
                    pe.wait_ge(g_copied, b - 1)
                for i in range(SB):
                    mm = pe.transpose(gt_b[b % 2][0:E, P * i:P * i + P], gate[:, SB * b + i, :], c.ident[:, :])
                mm.then_inc(g_turned, 1)
            pe.wait_ge(b2_in, 16)
            for i in range(TILES):
                pe.wait_ge(g_copied, i // SB + 1)
                if i >= 2:
                    pe.wait_ge(summed, ADDS * (i - 2) + 1)
                pe.matmul(bb[i % 2][:, 0:D], gateT[:, P * i:P * i + P], b2[:, :], start=True, stop=True).then_inc(b_mul, 1)

        @block.scalar
        def _(act):
            for b in range(B):
                act.wait_ge(g_turned, b + 1)
                act.activation(gateT[:, S * b:S * b + S], gt_b[b % 2][0:E, :], ACT.Copy).then_inc(g_copied, 1)

        @block.vector
        def _(dve):
            tick = Tally(tick_s)
            for k in range(TOPK):
                gates = c.gates[:, :, k:k + 1].to_broadcast([P, TILES, E])
                n = tick.add(dve.tensor_tensor(picked[:, k, :, :], c.oh[:, k, :, :], gates, ALU.mult))
            dve.wait_ge(tick_s, n)
            dve.wait_ge(tick_s, tick.add(dve.tensor_add(gate[:, :, :], picked[:, 0, :, :], picked[:, 1, :, :])))
            dve.tensor_add(gate[:, :, :], gate[:, :, :], picked[:, 2, :, :]).then_inc(gate_ready, 1)
            for i in range(TILES):
                dve.wait_ge(b_mul, i + 1)
                dve.tensor_add(c.base[:, i, :], c.base[:, i, :], bb[i % 2][:, 0:D]).then_inc(summed, 1)
                dve.wait_ge(gathered[i % RING], 16 * TOPK * (i // RING + 1))
                for k in range(TOPK):
                    dve.wait_ge(summed, ADDS * i + k + 1)
                    dve.scalar_tensor_tensor(out=c.base[:, i, :], in0=y[:, i % RING, k, :], scalar=c.gates[:, i, k:k + 1],
                                             in1=c.base[:, i, :], op0=ALU.mult, op1=ALU.add).then_inc(summed, 1)

        @block.sync
        def _(sp):
            sp.dma_start(b2[:, :], t["L0_ffn_re_b2"]).then_inc(b2_in, 16)
            for i in range(TILES):
                sp.wait_ge(summed, ADDS * (i + 1))
                sp.dma_start(out[i // SB, P * (i % SB):P * (i % SB) + P, :], c.base[:, i, :]).then_inc(out_s, 16)
            sp.wait_ge(out_s, 16 * TILES)





NAMES = ["x", "ctx_1024", "L0_xattn_wq", "L0_xattn_bq", "L0_xattn_wk", "L0_xattn_bk", "L0_xattn_wv",
         "L0_xattn_bv", "L0_xattn_wo", "L0_xattn_bo", "L0_ffn_theta", "L0_ffn_gamma1", "L0_ffn_gamma2",
         "L0_ffn_q_w", "L0_ffn_q_b", "L0_ffn_k_w", "L0_ffn_k_b", "L0_ffn_v_w", "L0_ffn_v_b", "L0_ffn_o_w",
         "L0_ffn_o_b", "L0_ffn_router_w", "L0_ffn_router_b", "L0_ffn_sh_w1", "L0_ffn_sh_b1", "L0_ffn_sh_w2",
         "L0_ffn_sh_b2", "L0_ffn_re_w1", "L0_ffn_re_b1", "L0_ffn_re_w2", "L0_ffn_re_b2"]


def program(nc, t, out):
    def scratch(name, shape, dt=F32):
        t[name] = nc.dram_tensor(name, shape, dt).ap()

    scratch("qs1", (B * H, SP1, S))
    scratch("ks1", (B * H, SP1, S))
    scratch("vs1", (QUADS, S, 4 * D1))
    scratch("o1", (QUADS, 4, 32, S))
    scratch("qs2", (B * H, D2, S))
    scratch("ks2", (B * H, D2, S))
    scratch("vs2", (QUADS, S, 4 * D2))
    scratch("o2", (B * H // 2, 2 * D2, S))
    scratch("s2", (QUADS, 4, S))
    scratch("r2", (QUADS, 4, S))
    scratch("an", (TOK, D))
    scratch("ye", (P * NT, D))
    scratch("r1", (QUADS, 4, S))
    scratch("x1", (TILES, P, D))
    scratch("xn", (TILES, P, D))
    c = Alloc(nc, "keep")
    c.keep = c
    with c.stack:
        c.w1_loads = 2 * (1 + 2 * (B * H // 8 - 2)) + 1
        c.w1_in, c.w2_in, c.wqkv_in = c.sem("w1_in"), c.sem("w2_in"), c.sem("wqkv_in")
        c.small_in, c.o_scaled, c.r2_out, c.ow_in = (c.sem(n) for n in ("small_in", "o_scaled", "r2_out", "ow_in"))
        make_identities(nc, c)
        rope = Alloc(nc, "rope")
        with rope.stack:
            c.cos, c.sin, c.cos_q, c.sin_q = (rope.sb(n, [P, S]) for n in ("cos", "sin", "cos_q", "sin_q"))
            project1(nc, c, t)
            c.wqkv = rope.sb("wqkv", [P, 3, DC, W2])
            c.oT, c.rT = rope.sb("oT", [P, 2, DC, S]), rope.sb("rT", [P, 2, DC, S])
            c.x, c.wo = rope.sb("x", [P, 2, SB, D]), rope.sb("wo", [P, DC, D])
            c.bo, c.g1 = rope.sb("bo", [P, D]), rope.sb("g1", [P, D])
            c.bqk, c.bv = rope.sb("bqk", [P, 2, W2 // P]), rope.sb("bv", [1, W2])
            attention(nc, c, t, False)
            project2(nc, c, t)
        c.w1 = c.sb("w1", [P, E, DC * FF + FF // P])
        c.ow = c.sb("ow", [P, W2 // P, D])
        attention(nc, c, t, True)
        c.w2 = c.sb("w2", [P, E, FF // P, D])
        c.base = c.sb("base", [P, TILES, D])
        c.logits = c.sb("logits", [P, TILES, E])
        mix(nc, c, t)
        c.gates = c.sb("gates", [P, TILES, 8])
        c.slots = c.sb("slots", [P, TOPK, TILES], I32)
        c.ids = c.sb("ids", [P, NT], I32)
        c.experts = c.sb("experts", [1, P], I32)
        c.oh = c.sb("oh", [P, TOPK, TILES, E])
        route(nc, c, t)
        experts(nc, c, t)
        combine(nc, c, t, out)


def kernel(**inputs):
    import concourse.bacc as bacc
    from concourse.bass_utils import run_bass_kernel_spmd

    x = {n: np.asarray(inputs[n]) for n in NAMES}
    for n in ("L0_xattn_bq", "L0_xattn_bk"):
        x[n] = x[n].reshape(DC, P).T
    for n in ("L0_ffn_q_w", "L0_ffn_k_w", "L0_ffn_q_b", "L0_ffn_k_b"):
        w = x[n].reshape(-1, 4, 4, D2 // 2, 2)
        x[n] = np.moveaxis(w, 4, 2).reshape(x[n].shape)
    for n in ("L0_ffn_q_b", "L0_ffn_k_b"):
        x[n] = x[n].reshape(W2 // P, P).T
    x["L0_ffn_sh_b1"] = x["L0_ffn_sh_b1"].reshape(FF // P, P).T
    x["L0_ffn_re_b1"] = np.moveaxis(x["L0_ffn_re_b1"].reshape(E, FF // P, P), 2, 0)
    x["L0_ffn_theta"] = x["L0_ffn_theta"].reshape(-1, 1)
    x = {n: v.reshape(1, -1) if v.ndim == 1 else v for n, v in x.items()}
    nc = bacc.Bacc("TRN2", target_bir_lowering=False, num_devices=1)
    arrays, t = {}, {}
    for n in NAMES:
        arrays[f"in_{n}"] = v = np.ascontiguousarray(x[n])
        t[n] = nc.dram_tensor(f"in_{n}", v.shape, mybir.dt.from_np(v.dtype), kind="ExternalInput").ap()
    out = nc.dram_tensor("out", (B, S, D), F32, kind="ExternalOutput").ap()
    program(nc, t, out)
    r = run_bass_kernel_spmd(nc, [arrays], core_ids=[0])
    return r.results[0]["out"]
```
